# Optimizing a Trainium2 kernel written in Bass

```python
import numpy as np
import jax
import jax.numpy as jnp

def _softmax(x, axis=-1):
    return jax.nn.softmax(x, axis=axis)

def _gelu(x):
    return jax.nn.gelu(x, approximate=True)

def _silu(x):
    return jax.nn.silu(x)

def _sigmoid(x):
    return jax.nn.sigmoid(x)

def _layernorm(x, axis=-1, eps=1e-05):
    m = jnp.mean(x, axis=axis, keepdims=True)
    v = jnp.var(x, axis=axis, keepdims=True)
    return (x - m) / jnp.sqrt(v + eps)

def _scatter_add(tgt, idx, src, axis=0):
    return tgt.at[idx].add(src)

def _segment_sum(src, seg, n):
    return jax.ops.segment_sum(src, seg, n)
kernel_name = 'mk_xattn_ffn_d2_seqx_r8_d521d8'

def setup_inputs(seed: int=0):
    np.random.seed(seed)
    _w = jnp.asarray

    def _rec_inputs():
        import jax
        import jax.numpy as jnp
        _rk = jax.random.key(seed)
        x = 7.22e-05 + 1 * jax.random.normal(jax.random.fold_in(_rk, 1), (4, 256, 256), jnp.float32)
        _lenS = 256 - jax.random.randint(jax.random.fold_in(_rk, 7), (4,), 0, max(1, 256 // 4) + 1, jnp.int32)
        _lenS2 = 256 - jax.random.randint(jax.random.fold_in(_rk, 8), (4,), 0, max(1, 256 // 4) + 1, jnp.int32)
        _ctx_1024P = jax.random.normal(jax.random.fold_in(_rk, 11), (4, 16, 128), jnp.float32)
        _ctx_1024c = jax.random.dirichlet(jax.random.fold_in(_rk, 511), 0.3 * jnp.ones((16,), jnp.float32), (4, 256))
        _ctx_1024t = jnp.einsum('bsk,bkd->bsd', _ctx_1024c, _ctx_1024P)
        _ctx_1024t = _ctx_1024t * jax.lax.rsqrt(jnp.mean(jnp.square(_ctx_1024t)) + 1e-12) * 0.953939
        ctx_1024 = 2.81802e-05 + 1.00001 * (_ctx_1024t + 0.3 * jax.random.normal(jax.random.fold_in(_rk, 611), (4, 256, 128), jnp.float32))
        return (x, ctx_1024)
    x, ctx_1024 = _rec_inputs()

    def _L0_xattn_setup():
        import jax, jax.numpy as jnp
        import numpy as np
        key = jax.random.key(seed)
        ks = jax.random.split(key, 6)
        B, L, N, C, D = (8, 64, 256, 128, 128)
        return {'teacher_logits': jax.random.normal(ks[0], (B, L, N), dtype=jnp.float32), 'teacher_features': jax.random.normal(ks[1], (B, N, C), dtype=jnp.float32), 'Wq': jax.random.normal(ks[2], (D, C), dtype=jnp.float32) * (1.0 / np.sqrt(C)), 'bq': jnp.zeros((D,), dtype=jnp.float32), 'Wk': jax.random.normal(ks[3], (D, C), dtype=jnp.float32) * (1.0 / np.sqrt(C)), 'bk': jnp.zeros((D,), dtype=jnp.float32)}
    _L0_xattn_all = _L0_xattn_setup()
    _L0_xattn_in = {k: v for k, v in _L0_xattn_all.items() if k in ('Wq', 'bq', 'Wk', 'bk')}
    del _L0_xattn_all

    def _L0_ffn_setup():
        import jax, jax.numpy as jnp
        import numpy as np
        key = jax.random.key(seed)
        k1, k2, k3, k4, k5 = jax.random.split(key, 5)
        B, L, H, N = (2, 256, 256, 1024)
        x = jax.random.normal(k1, (B, L, H), dtype=jnp.float32)
        W0 = jax.random.normal(k2, (N, H), dtype=jnp.float32) * (1.0 / np.sqrt(H))
        bias0 = jax.random.normal(k3, (N,), dtype=jnp.float32) * 0.02
        W1 = jax.random.normal(k4, (H, N), dtype=jnp.float32) * (1.0 / np.sqrt(N))
        bias1 = jax.random.normal(k5, (H,), dtype=jnp.float32) * 0.02
        return {'x': x, 'W0': W0, 'bias0': bias0, 'W1': W1, 'bias1': bias1}
    _L0_ffn_all = _L0_ffn_setup()
    _L0_ffn_in = {k: v for k, v in _L0_ffn_all.items() if k in ('W0', 'bias0', 'W1', 'bias1')}
    del _L0_ffn_all

    def _L1_xattn_setup():
        import jax, jax.numpy as jnp
        import numpy as np
        B_, L_, D_MODEL = (4, 256, 128)
        D_STATE, D_CONV, EXPAND = (16, 4, 2)
        D_INNER = EXPAND * D_MODEL
        DT_RANK = (D_MODEL + 15) // 16

        def silu(x):
            return x * jax.nn.sigmoid(x)
        key = jax.random.key(seed)
        ks = jax.random.split(key, 10)
        f32 = jnp.float32
        hidden_states = jax.random.normal(ks[0], (B_, L_, D_MODEL), dtype=f32)
        z = jax.random.normal(ks[1], (B_, D_INNER, L_), dtype=f32)
        in_proj_w = jax.random.normal(ks[2], (D_INNER, D_MODEL), dtype=f32) * 0.02
        conv_w = jax.random.normal(ks[3], (D_INNER, 1, D_CONV), dtype=f32) * 0.1
        conv_b = jax.random.normal(ks[4], (D_INNER,), dtype=f32) * 0.02
        x_proj_w = jax.random.normal(ks[5], (DT_RANK + 2 * D_STATE, D_INNER), dtype=f32) * 0.02
        dt_proj_w = jax.random.uniform(ks[6], (D_INNER, DT_RANK), dtype=f32, minval=-DT_RANK ** (-0.5), maxval=DT_RANK ** (-0.5))
        dt = jnp.exp(jax.random.uniform(ks[7], (D_INNER,), dtype=f32, minval=np.log(0.001), maxval=np.log(0.1)))
        dt_proj_b = jnp.log(jnp.expm1(dt))
        A_log = jnp.log(jnp.broadcast_to(jnp.arange(1, D_STATE + 1, dtype=f32), (D_INNER, D_STATE)))
        D = jnp.ones((D_INNER,), f32)
        return {'hidden_states': hidden_states, 'z': z, 'in_proj_w': in_proj_w, 'conv_w': conv_w, 'conv_b': conv_b, 'x_proj_w': x_proj_w, 'dt_proj_w': dt_proj_w, 'dt_proj_b': dt_proj_b, 'A_log': A_log, 'D': D}
    _L1_xattn_all = _L1_xattn_setup()
    _L1_xattn_in = {k: v for k, v in _L1_xattn_all.items() if k in ('in_proj_w', 'conv_w', 'conv_b', 'x_proj_w', 'dt_proj_w', 'dt_proj_b', 'A_log', 'D')}
    del _L1_xattn_all

    def _L1_ffn_setup():
        import jax, jax.numpy as jnp
        import numpy as np
        H = 256
        E = 64
        I = 64
        SI = 64
        TOP_K = 8
        B, T = (2, 64)
        key = jax.random.key(seed)
        ks = jax.random.split(key, 8)
        s = 0.02
        return {'h': jax.random.normal(ks[0], (B, T, H), jnp.float32), 'gate_w': jax.random.normal(ks[1], (E, H), jnp.float32) * s, 'gu_w': jax.random.normal(ks[2], (E, 2 * I, H), jnp.float32) * s, 'dp_w': jax.random.normal(ks[3], (E, H, I), jnp.float32) * s, 'sh_gate_w': jax.random.normal(ks[4], (SI, H), jnp.float32) * s, 'sh_up_w': jax.random.normal(ks[5], (SI, H), jnp.float32) * s, 'sh_down_w': jax.random.normal(ks[6], (H, SI), jnp.float32) * s, 'sh_gate1_w': jax.random.normal(ks[7], (1, H), jnp.float32) * s}
    _L1_ffn_all = _L1_ffn_setup()
    _L1_ffn_in = {k: v for k, v in _L1_ffn_all.items() if k in ('gate_w', 'gu_w', 'dp_w', 'sh_gate_w', 'sh_up_w', 'sh_down_w', 'sh_gate1_w')}
    del _L1_ffn_all
    return {'x': x, 'ctx_1024': ctx_1024, 'L0_xattn_Wq': _L0_xattn_in['Wq'], 'L0_xattn_bq': _L0_xattn_in['bq'], 'L0_xattn_Wk': _L0_xattn_in['Wk'], 'L0_xattn_bk': _L0_xattn_in['bk'], 'L0_ffn_W0': _L0_ffn_in['W0'], 'L0_ffn_bias0': _L0_ffn_in['bias0'], 'L0_ffn_W1': _L0_ffn_in['W1'], 'L0_ffn_bias1': _L0_ffn_in['bias1'], 'L1_xattn_in_proj_w': _L1_xattn_in['in_proj_w'], 'L1_xattn_conv_w': _L1_xattn_in['conv_w'], 'L1_xattn_conv_b': _L1_xattn_in['conv_b'], 'L1_xattn_x_proj_w': _L1_xattn_in['x_proj_w'], 'L1_xattn_dt_proj_w': _L1_xattn_in['dt_proj_w'], 'L1_xattn_dt_proj_b': _L1_xattn_in['dt_proj_b'], 'L1_xattn_A_log': _L1_xattn_in['A_log'], 'L1_xattn_D': _L1_xattn_in['D'], 'L1_ffn_gate_w': _L1_ffn_in['gate_w'], 'L1_ffn_gu_w': _L1_ffn_in['gu_w'], 'L1_ffn_dp_w': _L1_ffn_in['dp_w'], 'L1_ffn_sh_gate_w': _L1_ffn_in['sh_gate_w'], 'L1_ffn_sh_up_w': _L1_ffn_in['sh_up_w'], 'L1_ffn_sh_down_w': _L1_ffn_in['sh_down_w'], 'L1_ffn_sh_gate1_w': _L1_ffn_in['sh_gate1_w']}

def reference(x, ctx_1024, L0_xattn_Wq, L0_xattn_bq, L0_xattn_Wk, L0_xattn_bk, L0_ffn_W0, L0_ffn_bias0, L0_ffn_W1, L0_ffn_bias1, L1_xattn_in_proj_w, L1_xattn_conv_w, L1_xattn_conv_b, L1_xattn_x_proj_w, L1_xattn_dt_proj_w, L1_xattn_dt_proj_b, L1_xattn_A_log, L1_xattn_D, L1_ffn_gate_w, L1_ffn_gu_w, L1_ffn_dp_w, L1_ffn_sh_gate_w, L1_ffn_sh_up_w, L1_ffn_sh_down_w, L1_ffn_sh_gate1_w):
    import jax
    import jax.numpy as jnp

    def _L0_xattn_ref(teacher_logits, teacher_features, Wq, bq, Wk, bk):
        import jax, jax.numpy as jnp
        import numpy as np
        query = jnp.einsum('bnc,dc->bnd', teacher_features, Wq) + bq
        key = jnp.einsum('bnc,dc->bnd', teacher_features, Wk) + bk
        energy = jnp.einsum('bnd,bmd->bnm', query, key)
        attention = jax.nn.softmax(energy, axis=-1)
        x_m = jnp.einsum('bln,bmn->blm', teacher_logits, attention)
        return x_m

    def _L0_ffn_ref(x, W0, bias0, W1, bias1):
        import jax, jax.numpy as jnp
        import numpy as np
        B, L, H = x.shape
        X = x.reshape(-1, H).astype(jnp.float16)
        D = jnp.dot(X.astype(jnp.float32), W0.T) + bias0
        D = jax.nn.gelu(D, approximate=False).astype(jnp.float16)
        E = jnp.dot(D.astype(jnp.float32), W1.T) + bias1
        return E.astype(jnp.float16).reshape(B, L, H)

    def _L1_xattn_ref(hidden_states, z, in_proj_w, conv_w, conv_b, x_proj_w, dt_proj_w, dt_proj_b, A_log, D):
        import jax, jax.numpy as jnp
        import numpy as np
        B_, L_, D_MODEL = (4, 256, 128)
        D_STATE, D_CONV, EXPAND = (16, 4, 2)
        D_INNER = EXPAND * D_MODEL
        DT_RANK = (D_MODEL + 15) // 16

        def silu(x):
            return x * jax.nn.sigmoid(x)
        Bsz, L, _ = hidden_states.shape
        d_inner, _, d_conv = conv_w.shape
        dt_rank = dt_proj_w.shape[1]
        d_state = A_log.shape[1]
        x = jnp.einsum('bld,ed->bel', hidden_states, in_proj_w)
        xc = jax.lax.conv_general_dilated(x, conv_w, window_strides=(1,), padding=[(d_conv - 1, 0)], feature_group_count=d_inner, dimension_numbers=('NCH', 'OIH', 'NCH'))
        x = silu(xc + conv_b[None, :, None])
        x_dbl = jnp.einsum('bdl,ed->bel', x, x_proj_w)
        dt_low, Bm, Cm = jnp.split(x_dbl, [dt_rank, dt_rank + d_state], axis=1)
        dt = jnp.einsum('brl,dr->bdl', dt_low, dt_proj_w)
        dt = jax.nn.softplus(dt + dt_proj_b[None, :, None])
        A = -jnp.exp(A_log)
        dt_t = jnp.moveaxis(dt, -1, 0)
        B_t = jnp.moveaxis(Bm, -1, 0)
        C_t = jnp.moveaxis(Cm, -1, 0)
        u_t = jnp.moveaxis(x, -1, 0)

        def step(state, inp):
            d, b, c, u = inp
            dA = jnp.exp(d[..., None] * A)
            state = state * dA + (d * u)[..., None] * b[:, None, :]
            y = jnp.einsum('bdn,bn->bd', state, c)
            return (state, y)
        state0 = jnp.zeros((Bsz, d_inner, d_state), x.dtype)
        _, ys = jax.lax.scan(step, state0, (dt_t, B_t, C_t, u_t))
        y = jnp.moveaxis(ys, 0, 2)
        y = y + D[None, :, None] * x
        y = y * silu(z)
        return jnp.swapaxes(y, 1, 2)

    def _L1_ffn_ref(h, gate_w, gu_w, dp_w, sh_gate_w, sh_up_w, sh_down_w, sh_gate1_w):
        import jax, jax.numpy as jnp
        import numpy as np
        H = 256
        E = 64
        I = 64
        SI = 64
        TOP_K = 8
        B, T = (2, 64)
        Bb, Tt, Hh = h.shape
        x = h.reshape(Bb * Tt, Hh)
        N = x.shape[0]
        logits = x @ gate_w.T
        topv, topi = jax.lax.top_k(logits, TOP_K)
        rw = jax.nn.softmax(topv.astype(jnp.float32), axis=-1).astype(x.dtype)
        W = jnp.zeros((N, E), x.dtype).at[jnp.arange(N)[:, None], topi].set(rw)
        gu = jnp.einsum('nh,eih->nei', x, gu_w)
        gate, up = (gu[..., :I], gu[..., I:])
        inter = jax.nn.silu(gate) * up
        inter_w = inter * W[:, :, None]
        out = jnp.einsum('nei,ehi->nh', inter_w, dp_w)
        sh_inter = jax.nn.silu(x @ sh_gate_w.T) * (x @ sh_up_w.T)
        sh_out = sh_inter @ sh_down_w.T
        sh_g = jax.nn.sigmoid(x @ sh_gate1_w.T)
        out = out + sh_g * sh_out
        return out.reshape(Bb, Tt, Hh)
    x = x + _L0_xattn_ref(_layernorm(x, axis=-1), ctx_1024, L0_xattn_Wq, L0_xattn_bq, L0_xattn_Wk, L0_xattn_bk)
    x = x + _L0_ffn_ref(_layernorm(x, axis=-1), L0_ffn_W0, L0_ffn_bias0, L0_ffn_W1, L0_ffn_bias1)
    x = x + _L1_xattn_ref(ctx_1024, _layernorm(x, axis=-1), L1_xattn_in_proj_w, L1_xattn_conv_w, L1_xattn_conv_b, L1_xattn_x_proj_w, L1_xattn_dt_proj_w, L1_xattn_dt_proj_b, L1_xattn_A_log, L1_xattn_D)
    x = x + _L1_ffn_ref(_layernorm(x, axis=-1), L1_ffn_gate_w, L1_ffn_gu_w, L1_ffn_dp_w, L1_ffn_sh_gate_w, L1_ffn_sh_up_w, L1_ffn_sh_down_w, L1_ffn_sh_gate1_w)
    return x

_drawn_inputs = setup_inputs


def setup_inputs(seed=0):
    import zlib

    import numpy as np

    out = dict(_drawn_inputs(seed))
    spreads = {'L0_xattn_bq': (0.0, 0.1), 'L0_xattn_bk': (0.0, 0.8), 'L1_xattn_D': (1.0, 0.6)}
    factors = {'L0_ffn_bias0': 6.264,
     'L0_ffn_bias1': 4.394,
     'L1_xattn_in_proj_w': 6.603,
     'L1_xattn_conv_w': 6.824,
     'L1_xattn_conv_b': 8.0,
     'L1_xattn_x_proj_w': 8.0,
     'L1_xattn_dt_proj_w': 8.0,
     'L1_xattn_dt_proj_b': 8.0,
     'L1_xattn_A_log': 8.0,
     'L1_ffn_gate_w': 8.0,
     'L1_ffn_gu_w': 8.0,
     'L1_ffn_dp_w': 8.0,
     'L1_ffn_sh_gate_w': 8.0,
     'L1_ffn_sh_up_w': 8.0,
     'L1_ffn_sh_down_w': 8.0,
     'L1_ffn_sh_gate1_w': 8.0}
    for name, (base, spread) in spreads.items():
        noise = np.random.default_rng([zlib.crc32(name.encode()), seed]).standard_normal(out[name].shape)
        drawn = base * np.exp(spread * noise) if base else spread * noise
        out[name] = jnp.asarray(drawn.astype(out[name].dtype))
    for name, factor in factors.items():
        out[name] = (out[name] * factor).astype(out[name].dtype)
    return out
```

```python
from contextlib import ExitStack

import concourse.bass as bass
from concourse import mybir

ALU = mybir.AluOpType
ACT = mybir.ActivationFunctionType
F32 = mybir.dt.float32
F32R = mybir.dt.float32r
F16 = mybir.dt.float16
AX_X = mybir.AxisListType.X

P = 128
B, L, D = 4, 256, 256
C = 128
T = B * L
NT = T // P
HALF = 512
F = 1024
FT = F // P
NS = 16
NG = 4
SPB = NS // NG
STEPS = B * SPB
R = 8
LO = 64
XROWS = LO + R + 2 * NS
NE, NI = 64, 64
NP = NE // 2
GW = NE + 1
EPS = 1e-5
LOWEST = -3.0e38

BQ, BK, B0, CW, CB, DB, AL, DD = 0, 1, 2, 10, 18, 20, 22, 54
NCOL = 56


def build(nc, x_in, ctx_in, wqk_in, cols_in, inproj_in, xproj_in, dtproj_in, w0_in, w1_in, b1_in,
          gate_in, experts_in, shared_in, shdown_in, wrow, out):
    with ExitStack() as stack:
        def sb(name, shape, dt, at=stack):
            return at.enter_context(nc.sbuf_tensor(name, shape, dt))

        def sem(name):
            return stack.enter_context(nc.semaphore(name))

        PS = stack.enter_context(nc.psum_tensor("PS", [P, 8, HALF], F32))

        X = sb("X", [P, NT, D], F32)
        XN = sb("XN", [P, NT, D], F32)
        cols = sb("cols", [P, NCOL + 1], F32)
        ident = sb("ident", [P, P], F32)
        ident16 = sb("ident16", [P, P], F16)
        stats = sb("stats", [P, NT, 6], F32)
        mv = sb("mv", [P, NT, 2], F32)
        std = sb("std", [P, NT], F32)
        rstd = sb("rstd", [P, NT], F32)
        silz = sb("silz", [P, NT, D], F32)
        ys = sb("ys", [P, NT, L], F32)
        XT = sb("XT", [P, 2, T], F32)
        gate = sb("gate", [P, 2, GW], F32)
        shraw = sb("shraw", [P, 2 * 2 * NI], F32)
        shdraw = sb("shdraw", [NI, D], F32)

        early = ExitStack()
        wqk = sb("wqk", [P, 2, P], F32, early)
        inproj = sb("inproj", [P, D], F32, early)
        xproj = sb("xproj", [P, 2, R + 2 * NS], F32, early)
        xproj2 = sb("xproj2", [P, 2, XROWS], F32, early)
        dtproj = sb("dtproj", [R, D], F32, early)
        sel1 = sb("sel1", [XROWS, 2 * NS], F32, early)
        sel = sb("sel", [XROWS, 2 * NS, P], F32R, early)
        xd = sb("xd", [XROWS, T], F32R, early)
        dtlow = sb("dtlow", [R, T], F32, early)
        negA = sb("negA", [P, 2, NS], F32, early)
        diagD = sb("diagD", [P, 2, P], F32, early)
        u = sb("u", [P, 2, T], F32, early)
        dt = sb("dt", [P, 2, T], F32, early)
        dtu = sb("dtu", [P, 2, T], F32, early)

        attn = ExitStack()
        ctxT = sb("ctxT", [P, T], F32, attn)
        qT = sb("qT", [P, T], F32, attn)
        kT = sb("kT", [P, T], F32, attn)
        xpad = sb("xpad", [P, 2, B, L + 3], F32, attn)
        att = sb("att", [P, B, 2, L], F32, attn)
        attT = sb("attT", [P, B, 2, L], F32, attn)
        w0hi = sb("w0hi", [P, 2, F], F32R, attn)
        w0lo = sb("w0lo", [P, 2, F], F32R, attn)
        w1hi = sb("w1hi", [P, FT, D], F32R, attn)
        w1lo = sb("w1lo", [P, FT, D], F32R, attn)
        b1 = sb("b1", [P, D], F32, attn)
        XN16 = sb("XN16", [P, NT, D], F16, attn)
        XTr = sb("XTr", [P, 2, T], F32R, attn)
        hid16 = sb("hid16", [P, 4, HALF], F16, attn)
        hid = sb("hid", [P, FT, HALF], F32R, attn)
        e16 = sb("e16", [P, NT, D], F16, attn)
        negmx = sb("negmx", [P, B, 2], F32, attn)
        esum = sb("esum", [P, B, 2], F32, attn)
        rsum = sb("rsum", [P, B, 2], F32, attn)
        attn.close()

        scan = ExitStack()
        dA = sb("dA", [P, 2, 2, NG, L], F32, scan)
        dBu = sb("dBu", [P, 2, 2, NG, L], F32, scan)
        h = sb("h", [P, 2, 2, NG, L], F32, scan)
        Ch = sb("Ch", [P, 2, 2, NG, L], F32, scan)
        Csb = sb("Csb", [P, 2, NG, L], F32, scan)
        scan.close()

        moe = ExitStack()
        XThi = sb("XThi", [P, 2, T], F32R, moe)
        XTlo = sb("XTlo", [P, 2, T], F32R, moe)
        logit = sb("logit", [P, NT, GW], F32, moe)
        top = sb("top", [P, NT, 8], F32, moe)
        rest = sb("rest", [P, NT, NE], F32, moe)
        chosen = sb("chosen", [P, NT, NE], F32, moe)
        pexp = sb("pexp", [P, NT, NE], F32, moe)
        nmax = sb("nmax", [P, NT], F32, moe)
        wsum = sb("wsum", [P, NT], F32, moe)
        wrec = sb("wrec", [P, NT], F32, moe)
        W2 = sb("W2", [P, NT, 2, NE], F32, moe)
        sg = sb("sg", [P, NT], F32, moe)
        sgb = sb("sgb", [P, NT, NI], F32, moe)
        Wst = sb("Wst", [P, T], F32R, moe)
        sgT = sb("sgT", [NI, T], F32, moe)
        sel4 = sb("sel4", [4, P], F32, moe)
        sel4r = sb("sel4r", [4, P], F32R, moe)
        raw = [sb(f"raw{i}", [P, 2 * 2 * P + D], F32, moe) for i in range(2)]
        wr4 = [sb(f"wr4_{i}", [4, T], F32R, moe) for i in range(2)]
        guhi = [sb(f"guhi{i}", [P, 2, 2, P], F32R, moe) for i in range(2)]
        gulo = [sb(f"gulo{i}", [P, 2, 2, P], F32R, moe) for i in range(2)]
        dphi = [sb(f"dphi{i}", [P, D], F32R, moe) for i in range(2)]
        dplo = [sb(f"dplo{i}", [P, D], F32R, moe) for i in range(2)]
        shhi = sb("shhi", [P, 2, 2, NI], F32R, moe)
        shlo = sb("shlo", [P, 2, 2, NI], F32R, moe)
        shdhi = sb("shdhi", [NI, D], F32R, moe)
        shdlo = sb("shdlo", [NI, D], F32R, moe)
        sil = [sb(f"sil{i}", [P, HALF], F32, moe) for i in range(2)]
        act1 = [sb(f"act1_{i}", [P, HALF], F32, moe) for i in range(2)]
        act2 = [sb(f"act2_{i}", [P, HALF], F32, moe) for i in range(2)]
        ahi = [sb(f"ahi{i}", [P, HALF], F32R, moe) for i in range(2)]
        alo = [sb(f"alo{i}", [P, HALF], F32R, moe) for i in range(2)]
        moT = sb("moT", [P, 2, T], F32, moe)
        moe.close()
        early.close()

        d_ctx, d_x, d_vec, d_prep, d_w0, d_w1, d_gate, d_sh = (
            sem(n) for n in ("d_ctx", "d_x", "d_vec", "d_prep", "d_w0", "d_w1", "d_gate", "d_sh"))
        d_raw = [sem(f"d_raw{i}") for i in range(2)]
        d_wr4 = [sem(f"d_wr4_{i}") for i in range(2)]
        d_wrow, d_out = sem("d_wrow"), sem("d_out")
        g_ident, g_pads, g_sel, g_sel4, g_self = (sem(n) for n in ("g_ident", "g_pads", "g_sel", "g_sel4", "g_self"))
        v_self, a_self = sem("v_self"), sem("a_self")
        v_var = [sem(f"v_var{i}") for i in range(4)]
        a_std = [sem(f"a_std{i}") for i in range(4)]
        v_ln = [sem(f"v_ln{i}") for i in range(4)]
        (t_qk, a_qk, t_xin, a_xin, v_conv, a_u, t_xt, v_xt, t_en, v_mx, a_ex, v_att, t_attT, a_attT,
         t_xm, v_x1, t_xdbl, v_xd, v_dtlow, t_dt, a_e, v_r, v_dt, a_A, v_negA, v_w0, v_w1, t_x16, v_x16, t_up,
         a_gelu, v_hid, t_dn, v_x2, a_silz) = (sem(n) for n in (
             "t_qk a_qk t_xin a_xin v_conv a_u t_xt v_xt t_en v_mx a_ex v_att t_attT a_attT t_xm v_x1 "
             "t_xdbl v_xd v_dtlow t_dt a_e v_r v_dt a_A v_negA v_w0 v_w1 t_x16 v_x16 t_up a_gelu "
             "v_hid t_dn v_x2 a_silz").split())
        (t_B, t_C, a_C, a_dA, v_dBu, v_scan, g_Ch, t_ys, a_ys, v_gated, t_yT, v_x3, g_dA0) = (sem(n) for n in
            "t_B t_C a_C a_dA v_dBu v_scan g_Ch t_ys a_ys v_gated t_yT v_x3 g_dA0".split())
        (v_eps, v_xp, v_prep2, t_hT, v_hT, a_hT, t_lg, v_lg, v_top, a_pexp, v_W, v_sg, t_WT, v_WT, t_sgT, a_sgT, g_shw, v_shw,
         g_gu, v_gu, g_dp, v_dp, t_gate, t_up2, t_wbc, t_down, a_sil, v_act1, v_act2, a_ahi, g_alo, a_mo, t_moT,
         v_x4) = (sem(n) for n in (
             "v_eps v_xp v_prep2 t_hT v_hT a_hT t_lg v_lg v_top a_pexp v_W v_sg t_WT v_WT t_sgT a_sgT g_shw v_shw g_gu v_gu g_dp v_dp "
             "t_gate t_up2 t_wbc t_down a_sil v_act1 v_act2 a_ahi g_alo a_mo t_moT v_x4").split())

        CREDIT = 4
        w0raw = att[:, :, :, :].rearrange("p b m l -> p (b m l)")
        w1raw = attT[:, :, :, :].rearrange("p b m l -> p (b m l)")
        f32r = lambda ap: ap.bitcast(F32)

        block = stack.enter_context(nc.Block())

        @block.sync
        def _(sp):
            sp.dma_start(ctxT[:, :], ctx_in).then_inc(d_ctx, 16)
            sp.dma_start(wqk[:, :, :], wqk_in).then_inc(d_ctx, 16)
            sp.dma_start(inproj[:, :], inproj_in).then_inc(d_ctx, 16)
            sp.dma_start(xproj[:, :, :], xproj_in).then_inc(d_prep, 16)
            sp.dma_start(dtproj[:, :], dtproj_in).then_inc(d_prep, 16)
            sp.dma_start(b1[:, :], b1_in.partition_broadcast(P)).then_inc(d_w1, 16)
            sp.dma_start(gate[:, :, :], gate_in).then_inc(d_gate, 16)
            sp.dma_start(shraw[:, :], shared_in).then_inc(d_sh, 16)
            sp.dma_start(shdraw[:, :], shdown_in).then_inc(d_sh, 16)
            sp.wait_ge(v_WT, 2)
            sp.dma_start(wrow[:, 0, :], f32r(Wst[0:NE, :])).then_inc(d_wrow, 16)
            sp.dma_start(wrow[:, 1, :], f32r(Wst[NE:P, :])).then_inc(d_wrow, 16)
            sp.wait_ge(d_wrow, 32)
            for i in range(2):
                sp.dma_start(raw[i][:, :], experts_in[i]).then_inc(d_raw[i], 16)
                sp.dma_start(f32r(wr4[i][:, :]), wrow[2 * i:2 * i + 2].rearrange("e s t -> (e s) t")).then_inc(d_wr4[i], 16)
            with sp.Fori(1, NP // 2) as q:
                for i in range(2):
                    sp.wait_ge(g_gu, 2 * q - 1 + i)
                    sp.wait_ge(g_dp, 2 * q - 1 + i)
                    sp.dma_start(raw[i][:, :], experts_in[bass.ds(2 * q + i, 1)].rearrange("o p n -> (o p) n")).then_inc(d_raw[i], 16)
                    sp.wait_ge(t_wbc, 2 * (2 * q - 1 + i))
                    sp.dma_start(f32r(wr4[i][:, :]), wrow[bass.ds(4 * q + 2 * i, 2)].rearrange("e s t -> (e s) t")).then_inc(d_wr4[i], 16)
            for b in range(B):
                sp.wait_ge(v_x4, b + 1)
                sp.dma_start(out[:, 2 * b:2 * b + 2, :], X[:, 2 * b:2 * b + 2, :]).then_inc(d_out, 16)
            sp.wait_ge(d_out, 16 * B)

        @block.gpsimd
        def _(pool):
            g = [0]

            def link(ins):
                g[0] += 1
                ins.then_inc(g_self, 1)
                pool.wait_ge(g_self, g[0])

            link(nc.gpsimd.memset(ident[:, :], 0.0))
            nc.gpsimd.affine_select(out=ident[:, :], in_=ident[:, :], compare_op=ALU.not_equal, fill=1.0,
                                    base=0, pattern=[[-1, P]], channel_multiplier=1).then_inc(g_ident, 1)
            nc.gpsimd.memset(xpad[:, :, :, :], 0.0).then_inc(g_pads, 1)
            nc.gpsimd.memset(xproj2[:, :, :], 0.0).then_inc(g_pads, 1)
            link(nc.gpsimd.memset(sel1[:, :], 0.0))
            link(nc.gpsimd.affine_select(out=sel1[:, :], in_=sel1[:, :], compare_op=ALU.not_equal, fill=1.0,
                                         base=-R, pattern=[[-1, 2 * NS]], channel_multiplier=1))
            link(nc.gpsimd.affine_select(out=sel1[:, :], in_=sel1[:, :], compare_op=ALU.not_equal, fill=1.0,
                                         base=-R - LO, pattern=[[-1, 2 * NS]], channel_multiplier=1))
            nc.gpsimd.tensor_copy(sel[:, :, :], sel1[:, :].unsqueeze(2).broadcast_to([XROWS, 2 * NS, P])).then_inc(g_sel, 1)

            pool.wait_ge(v_x2, B)
            nc.gpsimd.memset(dA[:, :, :, :, 0:1], 0.0).then_inc(g_dA0, 1)
            pool.sem_inc(g_Ch, CREDIT)
            with pool.Fori(0, B) as b:
                for j in range(SPB):
                    for c in range(2):
                        pool.wait_ge(a_C, SPB * b + (j + 1))
                        pool.wait_ge(v_scan, 2 * SPB * b + (2 * j + c + 1 + CREDIT))
                        pool.wait_ge(t_ys, 2 * SPB * b + (2 * j + c + 1))
                        nc.gpsimd.tensor_tensor(Ch[:, j % 2, c], h[:, j % 2, c], Csb[:, j % 2],
                                                ALU.mult).then_inc(g_Ch, 1)

            pool.wait_ge(v_gated, B)
            link(nc.gpsimd.memset(sel4[:, :], 0.0))
            for r in range(2):
                link(nc.gpsimd.affine_select(out=sel4[:, :].rearrange("r (e m) -> r e m", e=2),
                                             in_=sel4[:, :].rearrange("r (e m) -> r e m", e=2),
                                             compare_op=ALU.not_equal, fill=1.0, base=-r,
                                             pattern=[[-2, 2], [0, NI]], channel_multiplier=1))
            nc.gpsimd.tensor_copy(sel4r[:, :], sel4[:, :]).then_inc(g_sel4, 1)
            pool.wait_ge(v_shw, 2)
            nc.gpsimd.tensor_tensor(shlo[:, :, :, :].rearrange("p k g i -> p (k g i)"), shraw[:, :],
                                    f32r(shhi[:, :, :, :]).rearrange("p k g i -> p (k g i)"), ALU.subtract).then_inc(g_shw, 1)
            nc.gpsimd.tensor_tensor(shdlo[:, :], shdraw[:, :], f32r(shdhi[:, :]), ALU.subtract).then_inc(g_shw, 1)

            def split_gu(i, turn):
                pool.wait_ge(v_gu, turn + 1)
                nc.gpsimd.tensor_tensor(gulo[i][:, :, :, :].rearrange("p k g m -> p (k g m)"), raw[i][:, 0:4 * P],
                                        f32r(guhi[i][:, :, :, :]).rearrange("p k g m -> p (k g m)"), ALU.subtract).then_inc(g_gu, 1)

            def split_dp(i, turn):
                pool.wait_ge(v_dp, turn + 1)
                nc.gpsimd.tensor_tensor(dplo[i][:, :], raw[i][:, 4 * P:], f32r(dphi[i][:, :]), ALU.subtract).then_inc(g_dp, 1)

            def lo_of_act(m, k, first=False):
                pool.wait_ge(a_ahi, k + 1)
                if not first:
                    pool.wait_ge(t_down, k - 1)
                nc.gpsimd.tensor_tensor(alo[m][:, :], act2[m][:, :], f32r(ahi[m][:, :]), ALU.subtract).then_inc(g_alo, 1)

            for m in range(2):
                pool.wait_ge(a_ahi, m + 1)
                nc.gpsimd.tensor_tensor(alo[m][0:NI, :], act2[m][0:NI, :], f32r(ahi[m][0:NI, :]), ALU.subtract).then_inc(g_alo, 1)
                if m == 0:
                    split_gu(0, 0)
                    split_dp(0, 0)
            with pool.Fori(0, NP // 2 - 1) as q:
                for i in range(2):
                    split_gu(1 - i, 2 * q + (i + 1))
                    lo_of_act(0, 4 * q + (2 * i + 2))
                    split_dp(1 - i, 2 * q + (i + 1))
                    lo_of_act(1, 4 * q + (2 * i + 3))
            split_gu(1, NP - 1)
            lo_of_act(0, 2 * NP - 2)
            split_dp(1, NP - 1)
            for k in range(2 * NP - 1, 2 * NP + 2):
                lo_of_act(k % 2, k)

        @block.scalar
        def _(act):
            a = [0]

            def link(ins):
                a[0] += 1
                ins.then_inc(a_self, 1)
                act.wait_ge(a_self, a[0])

            act.dma_start(cols[:, 0:NCOL], cols_in).then_inc(d_vec, 16)
            act.dma_start(X[:, :, :], x_in).then_inc(d_x, 16)
            act.dma_start(w0raw, w0_in).then_inc(d_w0, 16)
            act.dma_start(w1raw, w1_in).then_inc(d_w1, 16)

            def root(i):
                act.wait_ge(v_var[i], 1)
                nc.scalar.activation(std[:, :], mv[:, :, 1], ACT.Sqrt, bias=cols[:, NCOL:NCOL + 1]).then_inc(a_std[i], 1)

            act.wait_ge(d_vec, 16)
            for i in range(4):
                act.wait_ge(t_qk, i + 1)
                dst = (qT, kT)[i // 2][:, (i % 2) * HALF:(i % 2 + 1) * HALF]
                nc.scalar.activation(dst, PS[:, i], ACT.Identity, bias=cols[:, BQ + i // 2:BQ + i // 2 + 1]).then_inc(a_qk, 1)
            act.wait_ge(g_pads, 1)
            for i in range(4):
                act.wait_ge(t_xin, i + 1)
                nc.scalar.activation(xpad[:, i // 2, 2 * (i % 2):2 * (i % 2) + 2, 3:],
                                     PS[:, 4 + i].rearrange("p (b l) -> p b l", b=2), ACT.Copy).then_inc(a_xin, 1)
            act.wait_ge(v_eps, 1)
            root(0)
            for c in range(2):
                act.wait_ge(v_conv, c + 1)
                nc.scalar.activation(u[:, c], dt[:, c], ACT.Silu, bias=cols[:, CB + c:CB + c + 1]).then_inc(a_u, 1)
            for b in range(B):
                act.wait_ge(v_mx, b + 1)
                for m in range(2):
                    nc.scalar.activation(att[:, b, m], PS[:, 4 + b, m * L:(m + 1) * L], ACT.Exp,
                                         bias=negmx[:, b, m:m + 1], accum_out=esum[:, b, m:m + 1]).then_inc(a_ex, 1)
            nc.scalar.activation(negA[:, :, :], cols[:, AL:AL + 2 * NS].rearrange("p (c n) -> p c n", c=2),
                                 ACT.Exp).then_inc(a_A, 1)
            for b in range(B):
                act.wait_ge(t_attT, b + 1)
                nc.scalar.activation(attT[:, b].rearrange("p m l -> p (m l)"), PS[:, 2 + b % 2], ACT.Copy).then_inc(a_attT, 1)
            for c in range(2):
                act.wait_ge(v_r, c + 1)
                link(nc.scalar.activation(dtu[:, c], dt[:, c], ACT.Abs))
                nc.scalar.activation(dtu[:, c], dtu[:, c], ACT.Exp, scale=-1.0).then_inc(a_e, 1)
            act.wait_ge(a_e, 2)
            act.wait_ge(t_xm, B)
            for c in range(2):
                nc.scalar.activation(XT[:, c], dtu[:, c], ACT.Ln, bias=1.0).then_inc(a_e, 1)
            root(1)
            for k in range(2 * FT):
                act.wait_ge(t_up, k + 1)
                if k >= 4:
                    act.wait_ge(v_hid, k - 3)
                nc.scalar.activation(hid16[:, k % 4], PS[:, k % 4], ACT.Gelu,
                                     bias=cols[:, B0 + k % FT:B0 + k % FT + 1]).then_inc(a_gelu, 1)
            root(2)
            act.wait_ge(v_ln[2], NT)
            nc.scalar.activation(silz[:, :, :], XN[:, :, :], ACT.Silu).then_inc(a_silz, 1)

            act.wait_ge(g_dA0, 1)
            act.wait_ge(v_negA, 1)
            act.wait_ge(v_dt, 2)

            def step(b, j, y_of=None):
                act.wait_ge(t_C, SPB * b + (j + 1))
                act.wait_ge(g_Ch, 2 * SPB * b + (2 * j + 2))
                act.wait_ge(v_scan, 2 * SPB * b + (2 * j + 2))
                if y_of is not None:
                    act.wait_ge(t_ys, 2 * SPB * b + CREDIT)
                nc.scalar.activation(Csb[:, j % 2].rearrange("p n l -> p (n l)"),
                                     PS[:, 4:6].rearrange("p h t -> p (h t)"), ACT.Copy).then_inc(a_C, 1)
                if y_of is not None:
                    nc.scalar.activation(ys[:, bass.ds(2 * y_of, 2), :], PS[:, 6:8, 0:L], ACT.Copy).then_inc(a_ys, 1)
                for c in range(2):
                    for n in range(NG):
                        s = j * NG + n
                        ins = nc.scalar.activation(dA[:, j % 2, c, n, 1:], dt[:, c, bass.ds(b * L + 1, L - 1)], ACT.Exp,
                                                   scale=negA[:, c, s:s + 1])
                    ins.then_inc(a_dA, 1)

            act.sem_inc(a_ys, 1)
            for j in range(SPB):
                step(0, j)
            with act.Fori(1, B) as b:
                for j in range(SPB):
                    step(b, j, y_of=b - 1 if j == 1 else None)
            act.wait_ge(t_ys, 2 * STEPS + CREDIT)
            nc.scalar.activation(ys[:, 2 * B - 2:2 * B, :], PS[:, 6:8, 0:L], ACT.Copy).then_inc(a_ys, 1)

            root(3)
            for b in range(B):
                act.wait_ge(t_hT, b + 1)
                nc.scalar.activation(XT[:, :, b * L:(b + 1) * L], PS[:, 4 + b].rearrange("p (k l) -> p k l", k=2), ACT.Copy).then_inc(a_hT, 1)
            act.wait_ge(v_top, 1)
            for t in range(NT):
                nc.scalar.activation(pexp[:, t], logit[:, t, 0:NE], ACT.Exp, bias=nmax[:, t:t + 1]).then_inc(a_pexp, 1)
            nc.scalar.activation(sg[:, :], logit[:, :, NE], ACT.Exp, scale=-1.0).then_inc(a_pexp, 1)
            for m in range(2):
                act.wait_ge(t_sgT, m + 1)
                nc.scalar.activation(sgT[:, m * HALF:(m + 1) * HALF], PS[0:NI, 6 + m], ACT.Copy).then_inc(a_sgT, 1)

            def silu_and_hi(m, k, rows, first=False):
                act.wait_ge(t_gate, k + 1)
                if not first:
                    act.wait_ge(v_act1, k - 1)
                nc.scalar.activation(sil[m][0:rows, :], PS[0:rows, 4], ACT.Silu).then_inc(a_sil, 1)
                act.wait_ge(v_act2, k + 1)
                if not first:
                    act.wait_ge(t_down, k - 1)
                nc.scalar.activation(ahi[m][0:rows, :], act2[m][0:rows, :], ACT.Copy).then_inc(a_ahi, 1)

            for m in range(2):
                silu_and_hi(m, m, NI, first=True)
            with act.Fori(0, NP) as p:
                for m in range(2):
                    silu_and_hi(m, 2 * p + (2 + m), P)
            for i in range(4):
                act.wait_ge(t_down, 2 * NP + 2)
                nc.scalar.activation(moT[:, i // 2, (i % 2) * HALF:(i % 2 + 1) * HALF], PS[:, i], ACT.Copy).then_inc(a_mo, 1)

        @block.vector
        def _(dve):
            v = [0]

            def link(ins):
                v[0] += 1
                ins.then_inc(v_self, 1)
                dve.wait_ge(v_self, v[0])

            def moments(i):
                for t in range(NT):
                    last = nc.vector.bn_stats(stats[:, t], X[:, t])
                link(last)
                for t in range(NT):
                    last = nc.vector.bn_aggr(mv[:, t], stats[:, t])
                last.then_inc(v_var[i], 1)

            def normalise(i, dst):
                dve.wait_ge(a_std[i], 1)
                link(nc.vector.reciprocal(rstd[:, :], std[:, :]))
                for t in range(NT):
                    nc.vector.tensor_scalar(dst[:, t], X[:, t], mv[:, t, 0:1], rstd[:, t:t + 1],
                                            ALU.subtract, ALU.mult).then_inc(v_ln[i], 1)

            nc.vector.memset(cols[:, NCOL:NCOL + 1], EPS).then_inc(v_eps, 1)
            dve.wait_ge(d_x, 16)
            moments(0)
            dve.wait_ge(d_vec, 16)
            for c in range(2):
                dve.wait_ge(a_xin, 2 * c + 2)
                acc = dt[:, c].rearrange("p (b l) -> p b l", b=B)
                link(nc.vector.tensor_scalar(acc, xpad[:, c, :, 0:L], cols[:, CW + 4 * c:CW + 4 * c + 1], None, ALU.mult))
                for k in range(1, 4):
                    ins = nc.vector.scalar_tensor_tensor(acc, xpad[:, c, :, k:k + L], cols[:, CW + 4 * c + k:CW + 4 * c + k + 1],
                                                         acc, ALU.mult, ALU.add)
                    if k < 3:
                        link(ins)
                ins.then_inc(v_conv, 1)
                if c == 0:
                    normalise(0, XN)
            for b in range(B):
                dve.wait_ge(t_xt, b + 1)
                nc.vector.tensor_copy(XT[:, :, b * L:(b + 1) * L], PS[:, b].rearrange("p (k l) -> p k l", k=2)).then_inc(v_xt, 1)
            dve.wait_ge(d_prep, 32)
            dve.wait_ge(g_pads, 2)
            nc.vector.tensor_copy(xproj2[:, :, 0:R + 2 * NS], xproj[:, :, :])
            nc.vector.tensor_copy(xproj2[:, :, LO:XROWS], xproj[:, :, :]).then_inc(v_xp, 1)
            dve.wait_ge(g_ident, 1)
            for c in range(2):
                nc.vector.tensor_scalar(diagD[:, c], ident[:, :], cols[:, DD + c:DD + c + 1], None, ALU.mult)
            nc.vector.tensor_copy(ident16[:, :], ident[:, :]).then_inc(v_xp, 1)
            dve.wait_ge(d_w0, 16)
            link(nc.vector.tensor_copy(w0hi[:, :, :].rearrange("p k f -> p (k f)"), w0raw))
            nc.vector.tensor_tensor(w0lo[:, :, :].rearrange("p k f -> p (k f)"), w0raw,
                                    f32r(w0hi[:, :, :]).rearrange("p k f -> p (k f)"), ALU.subtract).then_inc(v_w0, 1)
            dve.wait_ge(d_w1, 32)
            link(nc.vector.tensor_copy(w1hi[:, :, :].rearrange("p k f -> p (k f)"), w1raw))
            nc.vector.tensor_tensor(w1lo[:, :, :].rearrange("p k f -> p (k f)"), w1raw,
                                    f32r(w1hi[:, :, :]).rearrange("p k f -> p (k f)"), ALU.subtract).then_inc(v_w1, 1)
            dve.wait_ge(v_w0, 1)
            for b in range(B):
                dve.wait_ge(t_en, b + 1)
                link(nc.vector.reduce_max(negmx[:, b], PS[:, 4 + b].rearrange("p (m l) -> p m l", m=2), AX_X))
                nc.vector.tensor_scalar(negmx[:, b], negmx[:, b], -1.0, None, ALU.mult).then_inc(v_mx, 1)
            for b in range(B):
                dve.wait_ge(a_ex, 2 * b + 2)
                link(nc.vector.reciprocal(rsum[:, b], esum[:, b]))
                for m in range(2):
                    nc.vector.tensor_scalar(att[:, b, m], att[:, b, m], rsum[:, b, m:m + 1], None, ALU.mult).then_inc(v_att, 1)
            for m in range(2):
                dve.wait_ge(t_xdbl, m + 1)
                tok = slice(m * HALF, (m + 1) * HALF)
                nc.vector.tensor_copy(dtlow[:, tok], PS[0:R, m]).then_inc(v_dtlow, 1)
                link(nc.vector.tensor_copy(xd[:, tok], PS[0:XROWS, m]))
                nc.vector.tensor_tensor(xd[LO:XROWS, tok], PS[LO:XROWS, m], f32r(xd[LO:XROWS, tok]), ALU.subtract).then_inc(v_xd, 1)
            dve.wait_ge(a_A, 1)
            nc.vector.tensor_scalar(negA[:, :, :], negA[:, :, :], -1.0, None, ALU.mult).then_inc(v_negA, 1)
            for b in range(B):
                dve.wait_ge(t_xm, b + 1)
                ins = nc.vector.tensor_tensor(X[:, 2 * b:2 * b + 2], PS[:, 4 + b % 2].rearrange("p (m l) -> p m l", m=2),
                                              X[:, 2 * b:2 * b + 2], ALU.add)
                ins.then_inc(v_x1, 1)
            dve.wait_ge(v_x1, B)
            moments(1)
            for c in range(2):
                dve.wait_ge(t_dt, c + 1)
                nc.vector.tensor_scalar(dt[:, c], PS[:, 6 * c:6 * c + 2].rearrange("p h t -> p (h t)"),
                                        cols[:, DB + c:DB + c + 1], None, ALU.add).then_inc(v_r, 1)
            normalise(1, XN16)
            for b in range(B):
                dve.wait_ge(t_x16, b + 1)
                nc.vector.tensor_copy(XTr[:, :, b * L:(b + 1) * L],
                                      PS[:, 4 + b, 0:L].bitcast(F16).rearrange("p (k l) -> p k l", k=2)).then_inc(v_x16, 1)
            for c in range(2):
                dve.wait_ge(a_e, 3 + c)
                e, ln = dtu[:, c], XT[:, c]
                link(nc.vector.scalar_tensor_tensor(dt[:, c], dt[:, c], 0.0, ln, ALU.max, ALU.add))
                link(nc.vector.tensor_scalar(ln, e, 1.0, -1.0, ALU.add, ALU.add))
                link(nc.vector.tensor_tensor(ln, e, ln, ALU.subtract))
                link(nc.vector.tensor_tensor(dt[:, c], dt[:, c], ln, ALU.add))
                nc.vector.tensor_tensor(dtu[:, c], dt[:, c], u[:, c], ALU.mult).then_inc(v_dt, 1)
            for hf in range(2):
                for f in range(FT):
                    k = hf * FT + f
                    dve.wait_ge(a_gelu, k + 1)
                    if hf:
                        dve.wait_ge(t_dn, 2)
                    nc.vector.tensor_copy(hid[:, f], hid16[:, k % 4]).then_inc(v_hid, 1)
                for i in range(2):
                    dve.wait_ge(t_dn, 2 * hf + i + 1)
                    t0 = 4 * hf + 2 * i
                    link(nc.vector.tensor_tensor(e16[:, t0:t0 + 2], PS[:, 4 + 2 * hf + i].rearrange("p (m l) -> p m l", m=2),
                                                 b1[:, :].unsqueeze(1).broadcast_to([P, 2, D]), ALU.add))
                    nc.vector.tensor_tensor(X[:, t0:t0 + 2], e16[:, t0:t0 + 2], X[:, t0:t0 + 2], ALU.add).then_inc(v_x2, 1)
            dve.wait_ge(v_x2, B)
            moments(2)
            normalise(2, XN)

            dve.sem_inc(v_scan, CREDIT)
            dve.sem_inc(v_dBu, CREDIT)
            dve.wait_ge(v_dt, 2)
            with dve.Fori(0, B) as b:
                for j in range(SPB):
                    dve.wait_ge(t_B, SPB * b + (j + 1))
                    for c in range(2):
                        nc.vector.tensor_tensor(dBu[:, j % 2, c], PS[:, 2 * (j % 2):2 * (j % 2) + 2].rearrange("p h (n l) -> p (h n) l", n=2),
                                                dtu[:, c, bass.ds(b * L, L)].unsqueeze(1).broadcast_to([P, NG, L]),
                                                ALU.mult).then_inc(v_dBu, 1)
                    for c in range(2):
                        dve.wait_ge(v_dBu, 2 * SPB * b + (2 * j + c + 1 + CREDIT))
                        dve.wait_ge(a_dA, 2 * SPB * b + (2 * j + c + 1))
                        dve.wait_ge(g_Ch, 2 * SPB * b + (2 * j + c + 1))
                        nc.vector.tensor_tensor_scan(h[:, j % 2, c].rearrange("p n l -> p (n l)"),
                                                     dA[:, j % 2, c].rearrange("p n l -> p (n l)"),
                                                     dBu[:, j % 2, c].rearrange("p n l -> p (n l)"),
                                                     0.0, ALU.mult, ALU.add).then_inc(v_scan, 1)
            dve.wait_ge(a_silz, 1)
            for b in range(B):
                dve.wait_ge(a_ys, b + 2)
                nc.vector.tensor_tensor(ys[:, 2 * b:2 * b + 2], ys[:, 2 * b:2 * b + 2], silz[:, 2 * b:2 * b + 2],
                                        ALU.mult).then_inc(v_gated, 1)
            for b in range(B):
                dve.wait_ge(t_yT, b + 1)
                nc.vector.tensor_tensor(X[:, 2 * b:2 * b + 2], PS[:, b].rearrange("p (m l) -> p m l", m=2),
                                        X[:, 2 * b:2 * b + 2], ALU.add).then_inc(v_x3, 1)
            dve.wait_ge(v_x3, B)
            moments(3)
            dve.wait_ge(d_sh, 32)
            nc.vector.tensor_copy(shhi[:, :, :, :].rearrange("p k g i -> p (k g i)"), shraw[:, :]).then_inc(v_shw, 1)
            nc.vector.tensor_copy(shdhi[:, :], shdraw[:, :]).then_inc(v_shw, 1)
            normalise(3, XN)
            for b in range(B):
                dve.wait_ge(a_hT, b + 1)
                tok = slice(b * L, (b + 1) * L)
                link(nc.vector.tensor_copy(XThi[:, :, tok], XT[:, :, tok]))
                nc.vector.tensor_tensor(XTlo[:, :, tok], XT[:, :, tok], f32r(XThi[:, :, tok]), ALU.subtract).then_inc(v_hT, 1)
            for m in range(2):
                dve.wait_ge(t_lg, m + 1)
                nc.vector.tensor_copy(logit[:, 4 * m:4 * m + 4],
                                      PS[:, m].rearrange("p (t n) -> p t n", t=4)[:, :, 0:GW]).then_inc(v_lg, 1)
            dve.wait_ge(v_lg, 2)
            for t in range(NT):
                ins = nc.vector.max(top[:, t], logit[:, t, 0:NE])
            link(ins)
            nc.vector.tensor_scalar(nmax[:, :], top[:, :, 0], -1.0, None, ALU.mult).then_inc(v_top, 1)
            for t in range(NT):
                ins = nc.vector.match_replace(rest[:, t], top[:, t], logit[:, t, 0:NE], LOWEST)
            link(ins)
            link(nc.vector.tensor_tensor(chosen[:, :, :], rest[:, :, :], logit[:, :, 0:NE], ALU.not_equal))
            dve.wait_ge(a_pexp, NT + 1)
            link(nc.vector.tensor_tensor(chosen[:, :, :], pexp[:, :, :], chosen[:, :, :], ALU.mult))
            link(nc.vector.reduce_sum(wsum[:, :], chosen[:, :, :], AX_X))
            link(nc.vector.reciprocal(wrec[:, :], wsum[:, :]))
            for s in range(2):
                nc.vector.tensor_tensor(W2[:, :, s], chosen[:, :, :], wrec[:, :].unsqueeze(2).broadcast_to([P, NT, NE]),
                                        ALU.mult).then_inc(v_W, 1)
            link(nc.vector.tensor_scalar(sg[:, :], sg[:, :], 1.0, None, ALU.add))
            link(nc.vector.reciprocal(sg[:, :], sg[:, :]))
            nc.vector.tensor_copy(sgb[:, :, :], sg[:, :].unsqueeze(2).broadcast_to([P, NT, NI])).then_inc(v_sg, 1)
            for m in range(2):
                dve.wait_ge(t_WT, m + 1)
                tok = slice(m * HALF, (m + 1) * HALF)
                link(nc.vector.tensor_copy(Wst[:, tok], PS[:, 2 + m]))
                nc.vector.tensor_tensor(Wst[NE:P, tok], PS[NE:P, 2 + m], f32r(Wst[NE:P, tok]), ALU.subtract).then_inc(v_WT, 1)

            def gu_hi(i, turn, rounds):
                dve.wait_ge(d_raw[i], 16 * rounds)
                if turn is not 0:
                    dve.wait_ge(t_up2, 2 * turn)
                nc.vector.tensor_copy(guhi[i][:, :, :, :].rearrange("p k g m -> p (k g m)"), raw[i][:, 0:4 * P]).then_inc(v_gu, 1)

            def dp_hi(i, turn):
                if turn is not 0:
                    dve.wait_ge(t_down, 2 * turn)
                nc.vector.tensor_copy(dphi[i][:, :], raw[i][:, 4 * P:]).then_inc(v_dp, 1)

            def activations(m, k, rows, first=False):
                dve.wait_ge(a_sil, k + 1)
                dve.wait_ge(t_up2, k + 1)
                nc.vector.tensor_tensor(act1[m][0:rows, :], PS[0:rows, 5], sil[m][0:rows, :], ALU.mult).then_inc(v_act1, 1)
                dve.wait_ge(v_act1, k + 1)
                if first:
                    dve.wait_ge(a_sgT, m + 1)
                    weight = sgT[:, m * HALF:(m + 1) * HALF]
                else:
                    dve.wait_ge(t_wbc, k - 1)
                    dve.wait_ge(g_alo, k - 1)
                    weight = PS[:, 6]
                nc.vector.tensor_tensor(act2[m][0:rows, :], act1[m][0:rows, :], weight, ALU.mult).then_inc(v_act2, 1)

            gu_hi(0, 0, 1)
            dp_hi(0, 0)
            for m in range(2):
                activations(m, m, NI, first=True)
            with dve.Fori(0, NP // 2 - 1) as q:
                for i in range(2):
                    gu_hi(1 - i, 2 * q + (i + 1), q + (i + 1))
                    activations(0, 4 * q + (2 * i + 2), P)
                    dp_hi(1 - i, 2 * q + (i + 1))
                    activations(1, 4 * q + (2 * i + 3), P)
            gu_hi(1, NP - 1, NP // 2)
            activations(0, 2 * NP - 2, P)
            dp_hi(1, NP - 1)
            for k in range(2 * NP - 1, 2 * NP + 2):
                activations(k % 2, k, P)
            for b in range(B):
                dve.wait_ge(t_moT, b + 1)
                nc.vector.tensor_tensor(X[:, 2 * b:2 * b + 2], PS[:, 4 + b].rearrange("p (m l) -> p m l", m=2),
                                        X[:, 2 * b:2 * b + 2], ALU.add).then_inc(v_x4, 1)

        @block.tensor
        def _(pe):
            mm = nc.tensor.matmul

            def tok(m):
                return slice(m * HALF, (m + 1) * HALF)

            pe.wait_ge(d_ctx, 48)
            for i in range(4):
                mm(PS[:, i], wqk[:, i // 2], ctxT[:, tok(i % 2)], start=True, stop=True).then_inc(t_qk, 1)
            for i in range(4):
                mm(PS[:, 4 + i], inproj[:, (i // 2) * P:(i // 2 + 1) * P], ctxT[:, tok(i % 2)],
                   start=True, stop=True).then_inc(t_xin, 1)
            pe.wait_ge(g_ident, 1)
            for b in range(B):
                pe.wait_ge(v_ln[0], 2 * b + 2)
                pe.wait_ge(a_qk, b + 1)
                for k in range(2):
                    for m in range(2):
                        ins = nc.tensor.transpose(PS[:, b, k * L + m * P:k * L + (m + 1) * P],
                                                  XN[:, 2 * b + m, k * P:(k + 1) * P], ident[:, :])
                ins.then_inc(t_xt, 1)
            for b in range(B):
                pe.wait_ge(a_qk, 4)
                pe.wait_ge(a_xin, b + 1)
                for m in range(2):
                    ins = mm(PS[:, 4 + b, m * L:(m + 1) * L], qT[:, b * L + m * P:b * L + (m + 1) * P],
                             kT[:, b * L:(b + 1) * L], start=True, stop=True)
                ins.then_inc(t_en, 1)
            pe.wait_ge(v_xp, 1)
            for m in range(2):
                pe.wait_ge(a_u, 2)
                pe.wait_ge(v_xt, m + 1)
                for k in range(2):
                    ins = mm(PS[0:XROWS, m], xproj2[:, k], u[:, k, tok(m)], start=k == 0, stop=k == 1)
                ins.then_inc(t_xdbl, 1)
            for b in range(B):
                pe.wait_ge(v_att, 2 * b + 2)
                if b < 2:
                    pe.wait_ge(v_xt, b + 3)
                else:
                    pe.wait_ge(a_attT, b - 1)
                for n in range(2):
                    for m in range(2):
                        ins = nc.tensor.transpose(PS[:, 2 + b % 2, n * L + m * P:n * L + (m + 1) * P],
                                                  att[:, b, m, n * P:(n + 1) * P], ident[:, :])
                ins.then_inc(t_attT, 1)
            for c in range(2):
                if c:
                    pe.wait_ge(a_ex, 2 * B)
                for m in range(2):
                    pe.wait_ge(v_xd, 2 if c == 0 else m + 1)
                    ins = mm(PS[:, 6 * c + m], dtproj[:, c * P:(c + 1) * P], dtlow[:, tok(m)], start=True, stop=True)
                ins.then_inc(t_dt, 1)
            for b in range(B):
                pe.wait_ge(a_attT, b + 1)
                if b < 2:
                    pe.wait_ge(a_ex, 2 * b + 2)
                else:
                    pe.wait_ge(v_x1, b - 1)
                for m in range(2):
                    for n in range(2):
                        ins = mm(PS[:, 4 + b % 2, m * L:(m + 1) * L], XT[:, n, b * L + m * P:b * L + (m + 1) * P],
                                 attT[:, b, n], start=n == 0, stop=n == 1)
                ins.then_inc(t_xm, 1)
            pe.wait_ge(v_xp, 2)
            pe.wait_ge(v_r, 2)
            pe.wait_ge(v_x1, B)
            for b in range(B):
                pe.wait_ge(v_ln[1], 2 * b + 2)
                for k in range(2):
                    for m in range(2):
                        lo = k * L + m * P
                        ins = nc.tensor.transpose(PS[:, 4 + b, 0:L].bitcast(F16)[:, lo:lo + P],
                                                  XN16[:, 2 * b + m, k * P:(k + 1) * P], ident16[:, :])
                ins.then_inc(t_x16, 1)
            pe.wait_ge(v_x16, B)
            pe.wait_ge(v_w0, 1)
            pe.wait_ge(v_w1, 1)
            pe.wait_ge(a_attT, B)

            def ffn_up(k):
                hf, f = k // FT, k % FT
                if k >= 4:
                    pe.wait_ge(a_gelu, k - 3)
                for i, w in enumerate((w0hi, w0lo)):
                    for c in range(2):
                        ins = mm(PS[:, k % 4], w[:, c, f * P:(f + 1) * P], XTr[:, c, tok(hf)],
                                 start=i + c == 0, stop=i + c == 2)
                ins.then_inc(t_up, 1)

            def ffn_down(hf):
                pe.wait_ge(v_hid, FT * (hf + 1))
                for i in range(2):
                    for m in range(2):
                        for f in range(FT):
                            for s, w in enumerate((w1hi, w1lo)):
                                ins = mm(PS[:, 4 + 2 * hf + i, m * L:(m + 1) * L], hid[:, f, (2 * i + m) * P:(2 * i + m + 1) * P],
                                         w[:, f], start=f + s == 0, stop=f + s == FT)
                    ins.then_inc(t_dn, 1)

            for k in range(FT + 4):
                ffn_up(k)
            ffn_down(0)
            for k in range(FT + 4, 2 * FT):
                ffn_up(k)
            ffn_down(1)

            def spread(j, s, tok0, after_first):
                pe.wait_ge(v_dBu, 2 * s + 2)
                if after_first:
                    pe.wait_ge(a_C, s)
                for n in range(NG):
                    ins = mm(PS[:, 2 * (j % 2) + n // 2, (n % 2) * L:(n % 2 + 1) * L], sel[:, NG * j + n],
                             xd[:, bass.ds(tok0, L)], start=True, stop=True)
                ins.then_inc(t_B, 1)
                for n in range(NG):
                    ins = mm(PS[:, 4 + n // 2, (n % 2) * L:(n % 2 + 1) * L], sel[:, NS + NG * j + n],
                             xd[:, bass.ds(tok0, L)], start=True, stop=True)
                ins.then_inc(t_C, 1)

            def sum_states(b, j):
                for c in range(2):
                    if j == 0:
                        pe.wait_ge(a_ys, b + 1)
                        mm(PS[:, 6 + c, 0:L], diagD[:, c], u[:, c, bass.ds(b * L, L)], start=True, stop=False)
                    pe.wait_ge(g_Ch, 2 * SPB * b + (2 * j + c + 1 + CREDIT))
                    for n in range(NG):
                        ins = mm(PS[:, 6 + c, 0:L], ident[:, :], Ch[:, j % 2, c, n], start=False,
                                 stop=j == SPB - 1 and n == NG - 1)
                    ins.then_inc(t_ys, 1)

            pe.sem_inc(t_ys, CREDIT)
            pe.wait_ge(g_sel, 1)
            pe.wait_ge(a_gelu, 2 * FT)
            pe.wait_ge(v_x2, B)
            spread(0, 0, 0, False)
            with pe.Fori(0, B - 1) as b:
                for j in range(SPB):
                    spread((j + 1) % SPB, SPB * b + (j + 1), b * L + L * ((j + 1) // SPB), True)
                    sum_states(b, j)
            for j in range(SPB):
                if j < SPB - 1:
                    spread(j + 1, SPB * (B - 1) + j + 1, (B - 1) * L, True)
                sum_states(B - 1, j)
            for b in range(B):
                pe.wait_ge(v_gated, b + 1)
                pe.wait_ge(v_dBu, 2 * STEPS + CREDIT)
                for m in range(2):
                    for c in range(2):
                        ins = nc.tensor.transpose(PS[:, b, m * L + c * P:m * L + (c + 1) * P],
                                                  ys[:, 2 * b + c, m * P:(m + 1) * P], ident[:, :])
                ins.then_inc(t_yT, 1)
            for b in range(B):
                pe.wait_ge(v_ln[3], 2 * b + 2)
                for k in range(2):
                    for m in range(2):
                        ins = nc.tensor.transpose(PS[:, 4 + b, k * L + m * P:k * L + (m + 1) * P],
                                                  XN[:, 2 * b + m, k * P:(k + 1) * P], ident[:, :])
                ins.then_inc(t_hT, 1)
            pe.wait_ge(d_gate, 16)
            for m in range(2):
                for t in range(4 * m, 4 * m + 4):
                    pe.wait_ge(a_hT, t // 2 + 1)
                    for k in range(2):
                        ins = mm(PS[:, m, (t % 4) * P:(t % 4) * P + GW], XT[:, k, t * P:(t + 1) * P], gate[:, k],
                                 start=k == 0, stop=k == 1)
                ins.then_inc(t_lg, 1)
            pe.wait_ge(v_W, 2)
            for t in range(NT):
                ins = nc.tensor.transpose(PS[:, 2 + t // 4, (t % 4) * P:(t % 4 + 1) * P],
                                          W2[:, t].rearrange("p s e -> p (s e)"), ident[:, :])
                if t % 4 == 3:
                    ins.then_inc(t_WT, 1)
            pe.wait_ge(v_sg, 1)
            pe.wait_ge(v_hT, B)
            for t in range(NT):
                ins = nc.tensor.transpose(PS[0:NI, 6 + t // 4, (t % 4) * P:(t % 4 + 1) * P], sgb[:, t], ident[:, :])
                if t % 4 == 3:
                    ins.then_inc(t_sgT, 1)

            def three(out_ap, whi, wlo, xhi, xlo, first, last):
                n = len(xhi)
                for i in range(n):
                    mm(out_ap, whi[i], xhi[i], start=first and i == 0, stop=False)
                    mm(out_ap, whi[i], xlo[i], start=False, stop=False)
                    ins = mm(out_ap, wlo[i], xhi[i], start=False, stop=last and i == n - 1)
                return ins

            def gate_up(hi, lo, m, k, rows):
                xhi = [XThi[:, c, tok(m)] for c in range(2)]
                xlo = [XTlo[:, c, tok(m)] for c in range(2)]
                for g, (bank, signal) in enumerate(((4, t_gate), (5, t_up2))):
                    if k is not 0:
                        pe.wait_ge((a_sil, v_act1)[g], k)
                    three(PS[0:rows, bank], [hi[:, c, g] for c in range(2)], [lo[:, c, g] for c in range(2)],
                          xhi, xlo, True, True).then_inc(signal, 1)

            def pair_gate_up(i, m, k, turn, rounds):
                pe.wait_ge(g_gu, turn + 1)
                gate_up(guhi[i], gulo[i], m, k, P)
                pe.wait_ge(d_wr4[i], 16 * rounds)
                pe.wait_ge(v_act2, k)
                mm(PS[:, 6], sel4r[:, :], wr4[i][:, tok(m)], start=True, stop=True).then_inc(t_wbc, 1)

            def down(hi, lo, m, k, rows, first=False, last=False):
                pe.wait_ge(g_alo, k + 1)
                for t in range(2):
                    ins = three(PS[:, 2 * t + m], [hi[:, t * P:(t + 1) * P]], [lo[:, t * P:(t + 1) * P]],
                                [ahi[m][0:rows, :]], [alo[m][0:rows, :]], first, last)
                ins.then_inc(t_down, 1)

            def pair_down(i, m, k, turn, last=False):
                pe.wait_ge(g_dp, turn + 1)
                down(dphi[i], dplo[i], m, k, P, last=last)

            pe.wait_ge(g_shw, 2)
            pe.wait_ge(v_hT, B)
            pe.wait_ge(a_hT, B)
            gate_up(shhi, shlo, 0, 0, NI)
            gate_up(shhi, shlo, 1, 1, NI)
            pe.wait_ge(v_lg, 2)
            pe.wait_ge(v_WT, 2)
            pe.wait_ge(g_sel4, 1)
            pe.wait_ge(a_sgT, 2)
            down(shdhi, shdlo, 0, 0, NI, first=True)
            pair_gate_up(0, 0, 2, 0, 1)
            down(shdhi, shdlo, 1, 1, NI, first=True)

            def two_pairs(q, last=False):
                for i in range(2):
                    turn, k = 2 * q + i, 4 * q + (2 * i + 2)
                    pair_gate_up(i, 1, 4 * q + (2 * i + 3), turn, q + 1)
                    end = last and i == 1
                    pair_down(i, 0, k, turn, last=end)
                    if not end:
                        pair_gate_up(1 - i, 0, 4 * q + (2 * i + 4), 2 * q + (i + 1), q + (i + 1))
                    pair_down(i, 1, 4 * q + (2 * i + 3), turn, last=end)

            with pe.Fori(0, NP // 2 - 1) as q:
                two_pairs(q)
            two_pairs(NP // 2 - 1, last=True)
            pe.wait_ge(v_act2, 2 * NP + 2)
            for b in range(B):
                pe.wait_ge(a_mo, 4)
                for m in range(2):
                    for t in range(2):
                        ins = nc.tensor.transpose(PS[:, 4 + b, m * L + t * P:m * L + (t + 1) * P],
                                                  moT[:, t, (2 * b + m) * P:(2 * b + m + 1) * P], ident[:, :])
                ins.then_inc(t_moT, 1)


def kernel(x, ctx_1024, L0_xattn_Wq, L0_xattn_bq, L0_xattn_Wk, L0_xattn_bk, L0_ffn_W0, L0_ffn_bias0, L0_ffn_W1,
           L0_ffn_bias1, L1_xattn_in_proj_w, L1_xattn_conv_w, L1_xattn_conv_b, L1_xattn_x_proj_w, L1_xattn_dt_proj_w,
           L1_xattn_dt_proj_b, L1_xattn_A_log, L1_xattn_D, L1_ffn_gate_w, L1_ffn_gu_w, L1_ffn_dp_w,
           L1_ffn_sh_gate_w, L1_ffn_sh_up_w, L1_ffn_sh_down_w, L1_ffn_sh_gate1_w):
    import numpy as np
    import concourse.bacc as bacc
    from concourse.bass_utils import run_bass_kernel_spmd

    def ktiles(w):
        return w.T.reshape(-1, P, w.shape[0]).transpose(1, 0, 2)

    def per_partition(v):
        return v.reshape(-1, P, *v.shape[1:]).swapaxes(0, 1).reshape(P, -1)

    a = {}
    a["x"] = x.reshape(NT, P, D).transpose(1, 0, 2)
    a["ctxT"] = ctx_1024.reshape(T, C).T
    a["wqk"] = np.stack([L0_xattn_Wq.T, L0_xattn_Wk.T], 1)
    a["cols"] = np.concatenate([per_partition(v) for v in (
        L0_xattn_bq, L0_xattn_bk, L0_ffn_bias0, L1_xattn_conv_w.reshape(D, 4), L1_xattn_conv_b, L1_xattn_dt_proj_b,
        L1_xattn_A_log, L1_xattn_D)], 1)
    a["inproj"] = L1_xattn_in_proj_w.T
    a["xproj"] = ktiles(L1_xattn_x_proj_w)
    a["dtproj"] = L1_xattn_dt_proj_w.T
    a["w0"] = ktiles(L0_ffn_W0).reshape(P, -1)
    a["w1"] = ktiles(L0_ffn_W1).reshape(P, -1)
    a["b1"] = L0_ffn_bias1
    a["gate"] = ktiles(np.concatenate([L1_ffn_gate_w, L1_ffn_sh_gate1_w], 0))
    gu = L1_ffn_gu_w.reshape(NP, 2, 2, NI, 2, P).transpose(0, 5, 4, 2, 1, 3).reshape(NP, P, 4 * P)
    dp = L1_ffn_dp_w.transpose(0, 2, 1).reshape(NP, P, D)
    a["experts"] = np.concatenate([gu, dp], 2)
    a["shared"] = ktiles(np.concatenate([L1_ffn_sh_gate_w, L1_ffn_sh_up_w], 0)).reshape(P, -1)
    a["shdown"] = L1_ffn_sh_down_w.T

    nc = bacc.Bacc("TRN2", target_bir_lowering=False, num_devices=1)
    arrays, args = {}, []
    for name, v in a.items():
        v = np.ascontiguousarray(v)
        arrays["in_" + name] = v
        args.append(nc.dram_tensor("in_" + name, v.shape, mybir.dt.from_np(v.dtype), kind="ExternalInput").ap())
    wrow = nc.dram_tensor("wrow", (NE, 2, T), F32, kind="Internal").ap()
    out = nc.dram_tensor("out_0", (T, D), F32, kind="ExternalOutput").ap()
    build(nc, *args, wrow, out.rearrange("(t p) d -> p t d", p=P))
    r = run_bass_kernel_spmd(nc, [arrays], core_ids=[0])
    return r.results[0]["out_0"].reshape(B, L, D)
```

```python
from contextlib import ExitStack

import concourse.bass as bass
from concourse import mybir

ALU = mybir.AluOpType
ACT = mybir.ActivationFunctionType
F32 = mybir.dt.float32
F32R = mybir.dt.float32r
F16 = mybir.dt.float16
AX_X = mybir.AxisListType.X

P = 128
B, L, D = 4, 256, 256
C = 128
T = B * L
NT = T // P
HALF = 512
F = 1024
FT = F // P
NS = 16
NG = 2
UPB = NS // NG
UNITS = B * UPB
PAIRED = 16
HRING = 4
R = 8
LO = 64
XROWS = LO + R + 2 * NS
NE, NI = 64, 64
NP = NE // 2
TURNS = NP + 1
AHEAD = 6
STEPS = 2 * TURNS
LOADS = TURNS + AHEAD
GW = NE + 1
EPS = 1e-5
LOWEST = -3.0e38

BQ, BK, B0, CB, DB, AL, DD = 0, 1, 2, 10, 12, 14, 46
NCOL = 48

SCAN_B, SCAN_C, SCAN_Y = 4, 5, 7
L0_BANKS = (0, 1, 2, 3, 6)
ACC, GATE, UP, WBC = (0, 1, 2, 3), 4, 5, 6

L0_USES = ([("qk", i) for i in range(4)] + [("xin", 0), ("xin", 1), ("en", 0), ("en", 1)]
           + [("xd", 0), ("dt", 0), ("dt", 1), ("en", 2), ("en", 3)]
           + [("xt", b) for b in range(B)] + [("xin", 2), ("xin", 3)] + [("attT", b) for b in range(B)]
           + [("xm", b) for b in range(B)] + [("xd", 1), ("dt", 2), ("dt", 3)] + [("x16", b) for b in range(B)]
           + [("up", k) for k in range(FT)] + [("up", FT), ("up", FT + 1), ("dn", 0), ("dn", 1)]
           + [("up", k) for k in range(FT + 2, 2 * FT)] + [("dn", 2), ("dn", 3)]
           + [("yT", 0), ("yT", 1), ("hT", 0), ("hT", 1), ("lg", 0), ("WT", 0), ("sT", 0)]
           + [("yT", 2)])
BANK = {use: L0_BANKS[i % len(L0_BANKS)] for i, use in enumerate(L0_USES)}
BEFORE = {use: L0_USES[i - len(L0_BANKS)] for i, use in enumerate(L0_USES) if i >= len(L0_BANKS)}
BANK.update({("yT", 3): 3, ("hT", 2): 1, ("hT", 3): 7, ("lg", 1): 3, ("WT", 1): 1, ("sT", 1): 7})
BEFORE.update({("yT", 3): ("lg", 0), ("hT", 2): ("yT", 2), ("lg", 1): ("yT", 3), ("WT", 1): ("hT", 2),
               ("sT", 1): ("hT", 3)})
OUT_BANKS = (7, 0, 2, GATE)


def half_of(k):
    return 0 if k < AHEAD else 1 if k >= STEPS - AHEAD else k % 2


def load_of(k):
    return k if k < AHEAD else k - (STEPS - AHEAD) + TURNS if k >= STEPS - AHEAD else (k + AHEAD) // 2


def steps_through(load):
    return load + 1 if load < AHEAD else 2 * load + 2 - AHEAD if load < TURNS else load + 1 + STEPS - AHEAD - TURNS


def build(nc, x_in, ctx_in, wqk_in, cols_in, inproj_in, conv_in, xproj_in, dtproj_in, w0_in, w1_in, b1_in,
          gate_in, experts_in, wrow, out):
    with ExitStack() as stack:
        def sb(name, shape, dt, at=stack):
            return at.enter_context(nc.sbuf_tensor(name, shape, dt))

        def sem(name):
            return stack.enter_context(nc.semaphore(name))

        PS = stack.enter_context(nc.psum_tensor("PS", [P, 8, HALF], F32))

        X = sb("X", [P, NT, D], F32)
        XN = sb("XN", [P, NT, D], F32)
        cols = sb("cols", [P, NCOL + 1], F32)
        ident = sb("ident", [P, P], F32)
        ident16 = sb("ident16", [P, P], F16)
        stats = sb("stats", [P, 4, NT, 6], F32)
        mv = sb("mv", [P, 4, NT, 2], F32)
        std = sb("std", [P, 4, NT], F32)
        rstd = sb("rstd", [P, 4, NT], F32)
        silz = sb("silz", [P, NT, D], F32)
        ys = sb("ys", [P, NT, L], F32)
        XT = sb("XT", [P, 2, T], F32)
        gate = sb("gate", [P, 2, GW], F32)

        sel = sb("sel", [XROWS, 2 * NS, P], F32R)
        xd = sb("xd", [XROWS, T], F32R)
        negA = sb("negA", [P, 2, NS], F32)
        diagD = sb("diagD", [P, 2, P], F32)
        u = sb("u", [P, 2, T], F32)
        dt = sb("dt", [P, 2, T], F32)
        dtu = sb("dtu", [P, 2, T], F32)
        dA = sb("dA", [P, 2, 2, NG, L], F32)
        H = sb("H", [P, HRING, 2, NG, L], F32)
        Csb = sb("Csb", [P, 2, NG, L], F32)
        zero = sb("zero", [P, P], F32R)

        l0 = ExitStack()
        w0hi = sb("w0hi", [P, 2, F], F32R, l0)
        w0lo = sb("w0lo", [P, 2, F], F32R, l0)
        w1hi = sb("w1hi", [P, FT, D], F32R, l0)
        w1lo = sb("w1lo", [P, FT, D], F32R, l0)
        b1 = sb("b1", [P, D], F32, l0)
        sel1 = sb("sel1", [XROWS, 2 * NS], F32, l0)
        negmx = sb("negmx", [P, B, 2], F32, l0)
        esum = sb("esum", [P, B, 2], F32, l0)
        rsum = sb("rsum", [P, B, 2], F32, l0)
        one = ExitStack()
        att = sb("att", [P, B, 2, L], F32, one)
        one.close()
        XTr = sb("XTr", [P, 2, T], F32R, l0)
        two = ExitStack()
        attT = sb("attT", [P, B, 2, L], F32, two)
        two.close()
        XN16 = sb("XN16", [P, NT, D], F16, l0)
        e16 = sb("e16", [P, NT, D], F16, l0)
        three_ = ExitStack()
        ctxT = sb("ctxT", [P, B, L + 3], F32, three_)
        taps = sb("taps", [P, 4, D], F32, three_)
        winc = sb("winc", [P, 4, D], F32, three_)
        corr = sb("corr", [P, 4, HALF], F32, three_)
        wqk = sb("wqk", [P, 2, P], F32, three_)
        inproj = sb("inproj", [P, D], F32, three_)
        xproj = sb("xproj", [P, 2, R + 2 * NS], F32, three_)
        xproj2 = sb("xproj2", [P, 2, XROWS], F32, three_)
        dtproj = sb("dtproj", [R, D], F32, three_)
        qT = sb("qT", [P, T], F32, three_)
        kT = sb("kT", [P, T], F32, three_)
        dtlow = sb("dtlow", [R, T], F32, three_)
        three_.close()
        hid16 = sb("hid16", [P, 4, HALF], F16, l0)
        hid = sb("hid", [P, FT, HALF], F32R, l0)
        l0.close()
        w0raw = silz[:, :, :].rearrange("p t d -> p (t d)")
        w1raw = attT[:, :, :, :].rearrange("p b m l -> p (b m l)")

        moe = ExitStack()
        XThi = sb("XThi", [P, 2, 2, HALF], F32R, moe)
        XTlo = sb("XTlo", [P, 2, 2, HALF], F32R, moe)
        logit = sb("logit", [P, 2, 4, GW], F32, moe)
        top = sb("top", [P, 2, 4, 8], F32, moe)
        nmax = sb("nmax", [P, 2, 4], F32, moe)
        rest = sb("rest", [P, 4, NE], F32, moe)
        chosen = sb("chosen", [P, 4, NE], F32, moe)
        pexp = sb("pexp", [P, 2, 4, NE], F32, moe)
        wsum = sb("wsum", [P, 2, 4], F32, moe)
        wrec = sb("wrec", [P, 2, 4], F32, moe)
        W2 = sb("W2", [P, 4, 2, NE], F32, moe)
        sg = sb("sg", [P, 2, 4], F32, moe)
        sgr = sb("sgr", [P, 2, 4], F32R, moe)
        sg4 = sb("sg4", [P, 2, 4, 4], F32, moe)
        Wst = sb("Wst", [P, 2, HALF], F32R, moe)
        sgT = sb("sgT", [4, 2, HALF], F32, moe)
        sel4 = sb("sel4", [4, P], F32, moe)
        sel4r = sb("sel4r", [4, P], F32R, moe)
        raw = [sb(f"raw{i}", [P, 4 * P + D], F32, moe) for i in range(2)]
        wr4 = [sb(f"wr4_{i}", [4, T], F32R, moe) for i in range(2)]
        guhi = [sb(f"guhi{i}", [P, 2, 2, P], F32R, moe) for i in range(2)]
        gulo = [sb(f"gulo{i}", [P, 2, 2, P], F32R, moe) for i in range(2)]
        dphi = [sb(f"dphi{i}", [P, D], F32R, moe) for i in range(2)]
        dplo = [sb(f"dplo{i}", [P, D], F32R, moe) for i in range(2)]
        sil = [sb(f"sil{i}", [P, HALF], F32, moe) for i in range(2)]
        act2 = [sb(f"act2_{i}", [P, HALF], F32, moe) for i in range(2)]
        ahi = [sb(f"ahi{i}", [P, HALF], F32R, moe) for i in range(2)]
        alo = [sb(f"alo{i}", [P, HALF], F32R, moe) for i in range(2)]
        moe.close()
        moT = [XN[:, 4 * hf:4 * hf + 4].rearrange("p (h a) d -> p h (a d)", h=2) for hf in range(2)]

        names = """d_ctx d_x d_vec d_prep d_w0 d_w1 d_b1 d_gate d_raw0 d_raw1 d_wr0 d_wr1 d_in d_wrow d_out
            g_ident g_pads g_xp g_id16 g_sel1 g_diag g_sel4 g_self g_w0 g_w1 v_hid g_zero g_Ch g_gu g_dp g_alo
            v_self v_var0 v_var1 v_var2 v_var3 v_ln0 v_ln1 v_ln2 v_ln3 v_eps v_winc v_w0 v_w1 v_mo v_pair v_mx v_att v_xd v_dtlow
            v_x1 v_r v_x16 v_dt v_ffn v_x2 v_negA v_dBu v_scan v_gated v_x3 v_hT v_lg v_top v_W v_sg v_WT v_sgT
            v_gu v_dp v_act1 v_act2 v_x4
            a_self a_std0 a_std1 a_std2 a_std3 a_qk a_xt a_sel a_u a_ex a_A a_attT a_e a_ln a_gelu a_silz a_C a_dA a_ys
            a_hT a_pexp a_sg a_sil a_ahi a_mo
            t_qk t_xin t_xt t_en t_xd t_attT t_dt t_xm t_x16 t_up t_dn t_B t_C t_ys t_yT t_hT t_lg t_WT t_sT
            t_gate t_up2 t_wbc t_down t_moT""".split()
        S = {n: sem(n) for n in names}
        (d_ctx, d_x, d_vec, d_prep, d_w0, d_w1, d_b1, d_gate, d_raw0, d_raw1, d_wr0, d_wr1, d_in, d_wrow, d_out,
         g_ident, g_pads, g_xp, g_id16, g_sel1, g_diag, g_sel4, g_self, g_w0, g_w1, v_hid, g_zero, g_Ch, g_gu, g_dp, g_alo,
         v_self, v_var0, v_var1, v_var2, v_var3, v_ln0, v_ln1, v_ln2, v_ln3, v_eps, v_winc, v_w0, v_w1, v_mo, v_pair, v_mx, v_att, v_xd, v_dtlow,
         v_x1, v_r, v_x16, v_dt, v_ffn, v_x2, v_negA, v_dBu, v_scan, v_gated, v_x3, v_hT, v_lg, v_top, v_W, v_sg, v_WT, v_sgT,
         v_gu, v_dp, v_act1, v_act2, v_x4,
         a_self, a_std0, a_std1, a_std2, a_std3, a_qk, a_xt, a_sel, a_u, a_ex, a_A, a_attT, a_e, a_ln, a_gelu, a_silz, a_C, a_dA, a_ys,
         a_hT, a_pexp, a_sg, a_sil, a_ahi, a_mo,
         t_qk, t_xin, t_xt, t_en, t_xd, t_attT, t_dt, t_xm, t_x16, t_up, t_dn, t_B, t_C, t_ys, t_yT, t_hT, t_lg, t_WT, t_sT,
         t_gate, t_up2, t_wbc, t_down, t_moT) = (S[n] for n in names)
        d_raw, d_wr = (d_raw0, d_raw1), (d_wr0, d_wr1)
        v_var, v_ln, a_std = (v_var0, v_var1, v_var2, v_var3), (v_ln0, v_ln1, v_ln2, v_ln3), (a_std0, a_std1, a_std2, a_std3)

        READ = {"xin": (a_u, 1), "qk": (a_qk, 1), "xd": (v_xd, 1), "dt": (v_r, 1), "xt": (a_xt, 1), "en": (a_ex, 2),
                "attT": (a_attT, 1), "xm": (v_x1, 1), "x16": (v_x16, 1), "up": (a_gelu, 1), "dn": (v_ffn, 1),
                "yT": (v_x3, 1), "hT": (a_hT, 1), "lg": (v_lg, 1), "WT": (v_WT, 1), "sT": (v_sgT, 1)}
        CREDIT, YCREDIT = 4, HRING

        def plain(ap):
            return ap.bitcast(F32)

        def flat(ap):
            return ap.rearrange("p k g m -> p (k g m)")

        def tok(m):
            return slice(m * HALF, (m + 1) * HALF)

        def bank(name, i):
            return PS[:, BANK[name, i]]

        def lnbuf(i):
            return ys[:, :, :].rearrange("p (c t) l -> p c (t l)", c=2)[:, i % 2, tok(i // 2)]

        def two_tiles(ap):
            return ap.rearrange("p (m l) -> p m l", m=2)

        block = stack.enter_context(nc.Block())

        @block.sync
        def _(sp):
            sp.dma_start(ctxT[:, :, 3:], ctx_in).then_inc(d_ctx, 16)
            sp.dma_start(wqk[:, :, :], wqk_in).then_inc(d_ctx, 16)
            sp.dma_start(inproj[:, :], inproj_in).then_inc(d_in, 16)
            sp.dma_start(xproj[:, :, :], xproj_in).then_inc(d_prep, 16)
            sp.dma_start(dtproj[:, :], dtproj_in).then_inc(d_prep, 16)
            sp.dma_start(w0raw, w0_in).then_inc(d_w0, 16)
            sp.dma_start(w1raw, w1_in).then_inc(d_w1, 16)
            sp.dma_start(b1[:, :], b1_in.partition_broadcast(P)).then_inc(d_b1, 16)
            sp.dma_start(gate[:, :, :], gate_in).then_inc(d_gate, 16)

            def load_experts(i, at):
                sp.dma_start(raw[i][:, :], experts_in[bass.ds(at, 1)].rearrange("o p n -> (o p) n")).then_inc(d_raw[i], 16)

            def load_rows(i, at, rows):
                src = wrow[bass.ds(2 * at, 2)].rearrange("e s t -> (e s) t")[:, rows]
                sp.dma_start(plain(wr4[i][:, rows]), src).then_inc(d_wr[i], 16)

            def load(l, weights_of, rows):
                i = l % 2
                sp.wait_ge(g_gu, l - 1)
                sp.wait_ge(g_dp, l - 1)
                load_experts(i, weights_of)
                sp.wait_ge(t_wbc, steps_through(l - 2))
                load_rows(i, weights_of, rows)

            def write_rows(hf):
                sp.wait_ge(v_WT, hf + 1)
                sp.wait_ge(v_sgT, hf + 1)
                sp.dma_start(wrow[0:2].rearrange("e s t -> (e s) t")[:, tok(hf)], sgT[:, hf]).then_inc(d_wrow, 16)
                sp.dma_start(wrow[2:NE + 2, 0, tok(hf)], plain(Wst[0:NE, hf])).then_inc(d_wrow, 16)
                sp.dma_start(wrow[2:NE + 2, 1, tok(hf)], plain(Wst[NE:P, hf])).then_inc(d_wrow, 16)
                sp.wait_ge(d_wrow, 48 * (hf + 1))

            sp.wait_ge(v_ffn, 4)
            for i in range(2):
                load_experts(i, i)
            write_rows(0)
            for i in range(2):
                load_rows(i, i, tok(0))
            for l in range(2, AHEAD):
                load(l, l, tok(0))
            both = slice(0, T)
            sp.wait_ge(g_gu, AHEAD - 1)
            sp.wait_ge(g_dp, AHEAD - 1)
            load_experts(0, AHEAD)
            write_rows(1)
            sp.wait_ge(t_wbc, AHEAD - 1)
            load_rows(0, AHEAD, both)
            with sp.Fori(0, (NP - AHEAD) // 2) as q:
                for r in range(1, 3):
                    i, l = (AHEAD + r) % 2, 2 * q + (AHEAD + r)
                    sp.wait_ge(g_gu, l - 1)
                    sp.wait_ge(g_dp, l - 1)
                    load_experts(i, l)
                    sp.wait_ge(t_wbc, 4 * q + (AHEAD + 2 * r - 2))
                    load_rows(i, l, both)
            for l in range(TURNS, LOADS):
                load(l, l - TURNS, tok(1))
            for b in range(B):
                sp.wait_ge(v_x4, b + 1)
                sp.dma_start(out[:, 2 * b:2 * b + 2, :], X[:, 2 * b:2 * b + 2, :]).then_inc(d_out, 16)
            sp.wait_ge(d_out, 16 * B)

        @block.gpsimd
        def _(pool):
            g = [0]

            def link(ins):
                g[0] += 1
                ins.then_inc(g_self, 1)
                pool.wait_ge(g_self, g[0])

            nc.gpsimd.memset(ctxT[:, :, 0:3], 0.0).then_inc(g_pads, 1)
            link(nc.gpsimd.memset(xproj2[:, :, :], 0.0))
            link(nc.gpsimd.memset(ident[:, :], 0.0))
            nc.gpsimd.affine_select(out=ident[:, :], in_=ident[:, :], compare_op=ALU.not_equal, fill=1.0,
                                    base=0, pattern=[[-1, P]], channel_multiplier=1).then_inc(g_ident, 1)
            link(nc.gpsimd.memset(sel1[:, :], 0.0))
            link(nc.gpsimd.affine_select(out=sel1[:, :], in_=sel1[:, :], compare_op=ALU.not_equal, fill=1.0,
                                         base=-R, pattern=[[-1, 2 * NS]], channel_multiplier=1))
            nc.gpsimd.affine_select(out=sel1[:, :], in_=sel1[:, :], compare_op=ALU.not_equal, fill=1.0,
                                    base=-R - LO, pattern=[[-1, 2 * NS]], channel_multiplier=1).then_inc(g_sel1, 1)
            pool.wait_ge(d_prep, 32)
            for at in (0, LO):
                nc.gpsimd.tensor_copy(xproj2[:, :, at:at + R + 2 * NS], xproj[:, :, :]).then_inc(g_xp, 1)
            nc.gpsimd.memset(dA[:, :, :, :, 0:1], 0.0).then_inc(g_zero, 1)
            nc.gpsimd.memset(plain(zero[:, :]), 0.0).then_inc(g_zero, 1)
            pool.wait_ge(g_ident, 1)
            pool.wait_ge(d_vec, 16)
            for c in range(2):
                nc.gpsimd.tensor_scalar(diagD[:, c], ident[:, :], cols[:, DD + c:DD + c + 1], None, ALU.mult).then_inc(g_diag, 1)
            nc.gpsimd.tensor_copy(ident16[:, :], ident[:, :]).then_inc(g_id16, 1)

            for ready, rawt, hi, lo, done in ((v_w0, w0raw, w0hi, w0lo, g_w0), (v_w1, w1raw, w1hi, w1lo, g_w1)):
                pool.wait_ge(ready, 1)
                nc.gpsimd.tensor_tensor(lo[:, :, :].rearrange("p k f -> p (k f)"), rawt,
                                        plain(hi[:, :, :]).rearrange("p k f -> p (k f)"), ALU.subtract).then_inc(done, 1)

            pool.sem_inc(g_Ch, CREDIT)

            def times_C(b, j):
                for c in range(2):
                    pool.wait_ge(a_C, UPB * b + (j + 1))
                    pool.wait_ge(v_scan, 2 * UPB * b + (2 * j + c + 1 + CREDIT))
                    nc.gpsimd.tensor_tensor(H[:, j % HRING, c], H[:, j % HRING, c], Csb[:, j % 2],
                                            ALU.mult).then_inc(g_Ch, 1)

            def gu_lo(i, l):
                pool.wait_ge(v_gu, l + 1)
                nc.gpsimd.tensor_tensor(flat(gulo[i][:, :, :, :]), raw[i][:, 0:4 * P], plain(flat(guhi[i][:, :, :, :])),
                                        ALU.subtract).then_inc(g_gu, 1)

            def dp_lo(i, l):
                pool.wait_ge(v_dp, l + 1)
                nc.gpsimd.tensor_tensor(dplo[i][:, :], raw[i][:, 4 * P:], plain(dphi[i][:, :]), ALU.subtract).then_inc(g_dp, 1)

            def act_lo(s, k, reuse=True):
                pool.wait_ge(a_ahi, k + 1)
                if reuse:
                    pool.wait_ge(t_down, k - 1)
                nc.gpsimd.tensor_tensor(alo[s][:, :], act2[s][:, :], plain(ahi[s][:, :]), ALU.subtract).then_inc(g_alo, 1)

            def single(k):
                l = load_of(k)
                if l + 1 < LOADS:
                    gu_lo((l + 1) % 2, l + 1)
                act_lo(k % 2, k, reuse=k > 1)
                if l + 1 < LOADS:
                    dp_lo((l + 1) % 2, l + 1)

            def double(par, l, k):
                gu_lo(1 - par, l + 1)
                act_lo(0, k)
                dp_lo(1 - par, l + 1)
                act_lo(1, k + 1)

            for n in range(UNITS):
                times_C(n // UPB, n % UPB)
                if n == 20:
                    pool.wait_ge(v_ffn, 4)
                    link(nc.gpsimd.memset(sel4[:, :], 0.0))
                    view = sel4[:, :].rearrange("r (e m) -> r e m", e=2)
                    for r in range(2):
                        link(nc.gpsimd.affine_select(out=view, in_=view, compare_op=ALU.not_equal, fill=1.0, base=-r,
                                                     pattern=[[-2, 2], [0, NI]], channel_multiplier=1))
                    nc.gpsimd.tensor_copy(sel4r[:, :], sel4[:, :]).then_inc(g_sel4, 1)
                if n == 22:
                    gu_lo(0, 0)
                    dp_lo(0, 0)
            for k in range(AHEAD):
                single(k)
            with pool.Fori(0, (TURNS - AHEAD) // 2) as q:
                double(0, 2 * q + AHEAD, 4 * q + AHEAD)
                double(1, 2 * q + (AHEAD + 1), 4 * q + (AHEAD + 2))
            double(0, TURNS - 1, STEPS - AHEAD - 2)
            for k in range(STEPS - AHEAD, STEPS):
                single(k)

        @block.scalar
        def _(act):
            a = [0]

            def link(ins):
                a[0] += 1
                ins.then_inc(a_self, 1)
                act.wait_ge(a_self, a[0])

            act.dma_start(taps[:, :, :], conv_in.partition_broadcast(P)).then_inc(d_in, 16)
            act.dma_start(cols[:, 0:NCOL], cols_in).then_inc(d_vec, 16)
            act.dma_start(X[:, :, :], x_in).then_inc(d_x, 16)

            def root(i, hf, tiles):
                act.wait_ge(v_var[i], hf + 1)
                nc.scalar.activation(std[:, i, tiles], mv[:, i, tiles, 1], ACT.Sqrt,
                                     bias=cols[:, NCOL:NCOL + 1]).then_inc(a_std[i], 1)

            def silu_u(i):
                hf, c = i // 2, i % 2
                act.wait_ge(t_xin, i + 1)
                nc.scalar.activation(u[:, c, tok(hf)], bank("xin", i), ACT.Silu,
                                     bias=cols[:, CB + c:CB + c + 1]).then_inc(a_u, 1)

            def softplus(hf):
                for c in range(2):
                    i = 2 * hf + c
                    act.wait_ge(v_r, i + 1)
                    link(nc.scalar.activation(dtu[:, c, tok(hf)], dt[:, c, tok(hf)], ACT.Abs))
                    nc.scalar.activation(dtu[:, c, tok(hf)], dtu[:, c, tok(hf)], ACT.Exp, scale=-1.0).then_inc(a_e, 1)
                if hf == 0:
                    exp_energy(2)
                    exp_energy(3)
                for c in range(2):
                    i = 2 * hf + c
                    act.wait_ge(a_e, i + 1)
                    nc.scalar.activation(lnbuf(i), dtu[:, c, tok(hf)], ACT.Ln, bias=1.0).then_inc(a_ln, 1)

            def unit(b, j):
                act.wait_ge(t_C, UPB * b + (j + 1))
                act.wait_ge(g_Ch, 2 * UPB * b + (2 * j + 2))
                act.wait_ge(v_scan, 2 * UPB * b + (2 * j + 2))
                nc.scalar.activation(Csb[:, j % 2].rearrange("p n l -> p (n l)"), PS[:, SCAN_C], ACT.Copy).then_inc(a_C, 1)
                for c in range(2):
                    for n in range(NG):
                        s = j * NG + n
                        ins = nc.scalar.activation(dA[:, j % 2, c, n, 1:], dt[:, c, bass.ds(b * L + 1, L - 1)], ACT.Exp,
                                                   scale=negA[:, c, s:s + 1])
                    ins.then_inc(a_dA, 1)

            def take_y(b):
                nc.scalar.activation(ys[:, bass.ds(2 * b, 2), :], two_tiles(PS[:, SCAN_Y]), ACT.Copy).then_inc(a_ys, 1)

            def exp_energy(b):
                act.wait_ge(v_mx, b + 1)
                for m in range(2):
                    nc.scalar.activation(att[:, b, m], bank("en", b)[:, m * L:(m + 1) * L], ACT.Exp,
                                         bias=negmx[:, b, m:m + 1], accum_out=esum[:, b, m:m + 1]).then_inc(a_ex, 1)

            act.wait_ge(g_sel1, 1)
            nc.scalar.activation(sel[:, :, :], sel1[:, :].unsqueeze(2).broadcast_to([XROWS, 2 * NS, P]), ACT.Copy).then_inc(a_sel, 1)
            act.wait_ge(d_vec, 16)
            nc.scalar.activation(negA[:, :, :], cols[:, AL:AL + 2 * NS].rearrange("p (c n) -> p c n", c=2),
                                 ACT.Exp).then_inc(a_A, 1)
            for i in range(4):
                act.wait_ge(t_qk, i + 1)
                nc.scalar.activation((qT, kT)[i // 2][:, tok(i % 2)], bank("qk", i), ACT.Identity,
                                     bias=cols[:, BQ + i // 2:BQ + i // 2 + 1]).then_inc(a_qk, 1)
            act.wait_ge(v_eps, 1)
            root(0, 0, slice(0, NT))
            silu_u(0)
            silu_u(1)
            exp_energy(0)
            exp_energy(1)
            softplus(0)
            for b in range(B):
                act.wait_ge(t_xt, b + 1)
                nc.scalar.activation(XT[:, :, b * L:(b + 1) * L], two_tiles(bank("xt", b)), ACT.Copy).then_inc(a_xt, 1)
            silu_u(2)
            silu_u(3)
            act.sem_inc(a_ys, 1)
            act.wait_ge(g_zero, 1)
            act.wait_ge(v_negA, 1)
            act.wait_ge(v_dt, 2)
            unit(0, 0)
            unit(0, 1)
            act.wait_ge(g_w1, 1)
            for b in range(B):
                act.wait_ge(t_attT, b + 1)
                nc.scalar.activation(attT[:, b].rearrange("p m l -> p (m l)"), bank("attT", b), ACT.Copy).then_inc(a_attT, 1)

            def gelu(ks):
                for k in ks:
                    act.wait_ge(t_up, k + 1)
                    if k >= 4:
                        act.wait_ge(v_hid, k - 3)
                    nc.scalar.activation(hid16[:, k % 4], bank("up", k), ACT.Gelu,
                                         bias=cols[:, B0 + k % FT:B0 + k % FT + 1]).then_inc(a_gelu, 1)

            def silu_z(hf):
                act.wait_ge(v_ln[2], 4 * hf + 4)
                nc.scalar.activation(silz[:, 4 * hf:4 * hf + 4], XN[:, 4 * hf:4 * hf + 4], ACT.Silu).then_inc(a_silz, 1)


            def transposed(b):
                act.wait_ge(t_hT, b + 1)
                nc.scalar.activation(XT[:, :, b * L:(b + 1) * L], two_tiles(bank("hT", b)), ACT.Copy).then_inc(a_hT, 1)

            def exp_logits(hf):
                act.wait_ge(v_top, hf + 1)
                for t in range(4):
                    nc.scalar.activation(pexp[:, hf, t], logit[:, hf, t, 0:NE], ACT.Exp, bias=nmax[:, hf, t:t + 1]).then_inc(a_pexp, 1)
                nc.scalar.activation(sg[:, hf], logit[:, hf, :, NE], ACT.Exp, scale=-1.0).then_inc(a_sg, 1)

            for n in range(2, UNITS):
                unit(n // UPB, n % UPB)
                if n == 3:
                    root(1, 0, slice(0, NT))
                if n == 4:
                    softplus(1)
                if n == 5:
                    act.wait_ge(v_dt, 4)
                gelu({5: range(0, 4), 6: range(4, 8), 7: range(8, 10), 10: range(10, 13), 11: range(13, 16)}.get(n, ()))
                if n in (9, 17, 25):
                    act.wait_ge(t_ys, n - 1 + YCREDIT)
                    take_y(n // UPB - 1)
                if n == 11:
                    root(2, 0, slice(0, 4))
                if n == 12:
                    act.wait_ge(g_w0, 1)
                    silu_z(0)
                if n == 17:
                    root(2, 1, slice(4, 8))
                if n == 18:
                    silu_z(1)
                if n == 21:
                    root(3, 0, slice(0, 4))
                if n == 24:
                    transposed(0)
                    transposed(1)
                if n == 27:
                    exp_logits(0)

            def act_step(s, k, reuse=True):
                act.wait_ge(t_gate, k + 1)
                if reuse:
                    act.wait_ge(v_act2, k - 1)
                nc.scalar.activation(sil[s][:, :], PS[:, GATE], ACT.Silu).then_inc(a_sil, 1)
                act.wait_ge(v_act2, k + 1)
                if reuse:
                    act.wait_ge(t_down, k - 1)
                nc.scalar.activation(ahi[s][:, :], act2[s][:, :], ACT.Copy).then_inc(a_ahi, 1)

            def take_experts(hf):
                act.wait_ge(t_down, (STEPS - AHEAD - 1, STEPS)[hf])
                nc.scalar.activation(moT[hf][:, 0], PS[:, ACC[hf]], ACT.Copy).then_inc(a_mo, 1)

            act.wait_ge(t_ys, UNITS + YCREDIT)
            take_y(3)
            for k in range(AHEAD):
                act_step(k % 2, k, reuse=k > 1)
                if k == 1:
                    root(3, 1, slice(4, 8))
                if k == 2:
                    transposed(2)
                    transposed(3)
                if k == 3:
                    exp_logits(1)
            with act.Fori(AHEAD, TURNS) as l:
                for m in range(2):
                    act_step(m, 2 * l + (m - AHEAD))
            take_experts(0)
            for k in range(STEPS - AHEAD, STEPS):
                act_step(k % 2, k)
            take_experts(1)

        @block.vector
        def _(dve):
            v = [0]

            def link(ins):
                v[0] += 1
                ins.then_inc(v_self, 1)
                dve.wait_ge(v_self, v[0])

            def moments(i, tiles):
                for t in tiles:
                    ins = nc.vector.bn_stats(stats[:, i, t], X[:, t])
                link(ins)
                for t in tiles:
                    ins = nc.vector.bn_aggr(mv[:, i, t], stats[:, i, t])
                ins.then_inc(v_var[i], 1)

            def normalise(i, hf, tiles, dst):
                dve.wait_ge(a_std[i], hf + 1)
                t0, t1 = tiles[0], tiles[-1] + 1
                link(nc.vector.reciprocal(rstd[:, i, t0:t1], std[:, i, t0:t1]))
                for t in tiles:
                    nc.vector.tensor_scalar(dst[:, t], X[:, t], mv[:, i, t, 0:1], rstd[:, i, t:t + 1],
                                            ALU.subtract, ALU.mult).then_inc(v_ln[i], 1)

            def take_xd(m):
                dve.wait_ge(t_xd, m + 1)
                nc.vector.tensor_copy(dtlow[:, tok(m)], bank("xd", m)[0:R]).then_inc(v_dtlow, 1)
                link(nc.vector.tensor_copy(xd[:, tok(m)], bank("xd", m)[0:XROWS]))
                nc.vector.tensor_tensor(xd[LO:XROWS, tok(m)], bank("xd", m)[LO:XROWS], plain(xd[LO:XROWS, tok(m)]),
                                        ALU.subtract).then_inc(v_xd, 1)

            def dt_bias(i):
                hf, c = i // 2, i % 2
                dve.wait_ge(t_dt, i + 1)
                nc.vector.tensor_scalar(dt[:, c, tok(hf)], bank("dt", i), cols[:, DB + c:DB + c + 1], None, ALU.add).then_inc(v_r, 1)

            def softplus_rest(i):
                dve.wait_ge(a_e, i + 1)
                e = dtu[:, i % 2, tok(i // 2)]
                link(nc.vector.tensor_scalar(corr[:, i], e, 1.0, -1.0, ALU.add, ALU.add))
                link(nc.vector.tensor_tensor(corr[:, i], e, corr[:, i], ALU.subtract))

            def dt_finish(i):
                hf, c = i // 2, i % 2
                dve.wait_ge(a_ln, i + 1)
                r, e, ln = dt[:, c, tok(hf)], dtu[:, c, tok(hf)], lnbuf(i)
                link(nc.vector.scalar_tensor_tensor(r, r, 0.0, ln, ALU.max, ALU.add))
                link(nc.vector.tensor_tensor(r, r, corr[:, i], ALU.add))
                nc.vector.tensor_tensor(e, r, u[:, c, tok(hf)], ALU.mult).then_inc(v_dt, 1)

            def unit_dBu(b, j):
                dve.wait_ge(t_B, UPB * b + (j + 1))
                dve.wait_ge(t_ys, UPB * b + (j + 1))
                nc.vector.tensor_tensor(H[:, j % HRING], two_tiles(PS[:, SCAN_B]).unsqueeze(1).broadcast_to([P, 2, NG, L]),
                                        dtu[:, :, b * L:(b + 1) * L].unsqueeze(2).broadcast_to([P, 2, NG, L]),
                                        ALU.mult).then_inc(v_dBu, 1)

            def unit_scan(b, j):
                dve.wait_ge(v_dBu, UPB * b + (j + 1))
                for c in range(2):
                    dve.wait_ge(a_dA, 2 * UPB * b + (2 * j + c + 1))
                    states = H[:, j % HRING, c].rearrange("p n l -> p (n l)")
                    nc.vector.tensor_tensor_scan(states, dA[:, j % 2, c].rearrange("p n l -> p (n l)"), states,
                                                 0.0, ALU.mult, ALU.add).then_inc(v_scan, 1)

            def add_pair(n):
                dve.wait_ge(g_Ch, 2 * (n + 1) + CREDIT)
                H0, H1 = (H[:, n % HRING, :, s] for s in range(2))
                nc.vector.tensor_tensor(H0, H0, H1, ALU.add).then_inc(v_pair, 1)

            def add_to_x(name, b, arrived, done):
                dve.wait_ge(arrived, b + 1)
                nc.vector.tensor_tensor(X[:, 2 * b:2 * b + 2], two_tiles(bank(name, b)), X[:, 2 * b:2 * b + 2],
                                        ALU.add).then_inc(done, 1)

            def ffn_out(i):
                dve.wait_ge(t_dn, i + 1)
                nc.vector.tensor_tensor(e16[:, 2 * i:2 * i + 2], two_tiles(bank("dn", i)),
                                        b1[:, :].unsqueeze(1).broadcast_to([P, 2, D]), ALU.add).then_inc(v_ffn, 1)
                dve.wait_ge(v_ffn, i + 1)
                nc.vector.tensor_tensor(X[:, 2 * i:2 * i + 2], e16[:, 2 * i:2 * i + 2], X[:, 2 * i:2 * i + 2],
                                        ALU.add).then_inc(v_x2, 1)

            def hidden(ks):
                for k in ks:
                    dve.wait_ge(a_gelu, k + 1)
                    if k >= FT:
                        dve.wait_ge(t_dn, 2)
                    nc.vector.tensor_copy(hid[:, k % FT], hid16[:, k % 4]).then_inc(v_hid, 1)

            def gate_y(b):
                dve.wait_ge(a_ys, b + 2)
                dve.wait_ge(a_silz, b // 2 + 1)
                nc.vector.tensor_tensor(ys[:, 2 * b:2 * b + 2], ys[:, 2 * b:2 * b + 2], silz[:, 2 * b:2 * b + 2],
                                        ALU.mult).then_inc(v_gated, 1)

            def row_maxima(b):
                dve.wait_ge(t_en, b + 1)
                link(nc.vector.reduce_max(negmx[:, b], two_tiles(bank("en", b)), AX_X))
                nc.vector.tensor_scalar(negmx[:, b], negmx[:, b], -1.0, None, ALU.mult).then_inc(v_mx, 1)

            nc.vector.memset(cols[:, NCOL:NCOL + 1], EPS).then_inc(v_eps, 1)
            dve.wait_ge(d_in, 32)
            nc.vector.tensor_tensor(winc[:, :, :], taps[:, :, :], inproj[:, :].unsqueeze(1).broadcast_to([P, 4, D]),
                                    ALU.mult).then_inc(v_winc, 1)
            dve.wait_ge(a_A, 1)
            nc.vector.tensor_scalar(negA[:, :, :], negA[:, :, :], -1.0, None, ALU.mult).then_inc(v_negA, 1)
            dve.wait_ge(d_x, 16)
            moments(0, range(NT))
            normalise(0, 0, range(NT), XN)

            def weights_hi(landed, rawt, hi, done):
                dve.wait_ge(landed, 16)
                nc.vector.tensor_copy(hi[:, :, :].rearrange("p k f -> p (k f)"), rawt).then_inc(done, 1)

            weights_hi(d_w0, w0raw, w0hi, v_w0)
            row_maxima(0)
            row_maxima(1)
            weights_hi(d_w1, w1raw, w1hi, v_w1)
            take_xd(0)
            for i in range(2):
                dt_bias(i)
            row_maxima(2)
            row_maxima(3)
            for i in range(2):
                softplus_rest(i)
            for i in range(2):
                dt_finish(i)
            dve.sem_inc(v_scan, CREDIT)
            dve.wait_ge(v_dt, 2)
            unit_dBu(0, 0)
            for b in range(B):
                dve.wait_ge(a_ex, 2 * b + 2)
                link(nc.vector.reciprocal(rsum[:, b], esum[:, b]))
                for m in range(2):
                    nc.vector.tensor_scalar(att[:, b, m], att[:, b, m], rsum[:, b, m:m + 1], None, ALU.mult).then_inc(v_att, 1)
            unit_scan(0, 0)
            unit_dBu(0, 1)
            unit_scan(0, 1)
            add_pair(0)

            def x3_moments(hf):
                dve.wait_ge(v_x3, 2 * hf + 2)
                moments(3, range(4 * hf, 4 * hf + 4))

            def layernorm_parts(hf):
                for b in range(2 * hf, 2 * hf + 2):
                    dve.wait_ge(a_hT, b + 1)
                    part = slice((b % 2) * L, (b % 2 + 1) * L)
                    src = XT[:, :, b * L:(b + 1) * L]
                    link(nc.vector.tensor_copy(XThi[:, hf, :, part], src))
                    nc.vector.tensor_tensor(XTlo[:, hf, :, part], src, plain(XThi[:, hf, :, part]), ALU.subtract).then_inc(v_hT, 1)

            def choose(hf):
                dve.wait_ge(t_lg, hf + 1)
                nc.vector.tensor_copy(logit[:, hf], bank("lg", hf).rearrange("p (t n) -> p t n", t=4)[:, :, 0:GW]).then_inc(v_lg, 1)
                dve.wait_ge(v_lg, hf + 1)
                for t in range(4):
                    ins = nc.vector.max(top[:, hf, t], logit[:, hf, t, 0:NE])
                link(ins)
                nc.vector.tensor_scalar(nmax[:, hf], top[:, hf, :, 0], -1.0, None, ALU.mult).then_inc(v_top, 1)
                for t in range(4):
                    ins = nc.vector.match_replace(rest[:, t], top[:, hf, t], logit[:, hf, t, 0:NE], LOWEST)
                link(ins)
                link(nc.vector.tensor_tensor(chosen[:, :, :], rest[:, :, :], logit[:, hf, :, 0:NE], ALU.not_equal))

            def weigh(hf):
                dve.wait_ge(a_pexp, 4 * hf + 4)
                link(nc.vector.tensor_tensor(chosen[:, :, :], pexp[:, hf], chosen[:, :, :], ALU.mult))
                link(nc.vector.reduce_sum(wsum[:, hf], chosen[:, :, :], AX_X))
                link(nc.vector.reciprocal(wrec[:, hf], wsum[:, hf]))
                if hf:
                    dve.wait_ge(t_WT, 1)
                for s in range(2):
                    nc.vector.tensor_tensor(W2[:, :, s], chosen[:, :, :], wrec[:, hf].unsqueeze(2).broadcast_to([P, 4, NE]),
                                            ALU.mult).then_inc(v_W, 1)
                dve.wait_ge(a_sg, hf + 1)
                link(nc.vector.tensor_scalar(sg[:, hf], sg[:, hf], 1.0, None, ALU.add))
                link(nc.vector.reciprocal(sg[:, hf], sg[:, hf]))
                link(nc.vector.tensor_copy(sgr[:, hf], sg[:, hf]))
                nc.vector.tensor_copy(sg4[:, hf, :, 0], plain(sgr[:, hf])).then_inc(v_sg, 1)
                nc.vector.tensor_tensor(sg4[:, hf, :, 1], sg[:, hf], plain(sgr[:, hf]), ALU.subtract).then_inc(v_sg, 1)

            def weights_by_expert(hf):
                dve.wait_ge(t_WT, hf + 1)
                link(nc.vector.tensor_copy(Wst[:, hf], bank("WT", hf)))
                nc.vector.tensor_tensor(Wst[NE:P, hf], bank("WT", hf)[NE:P], plain(Wst[NE:P, hf]), ALU.subtract).then_inc(v_WT, 1)
                dve.wait_ge(t_sT, hf + 1)
                nc.vector.tensor_copy(sgT[:, hf], bank("sT", hf)[0:4]).then_inc(v_sgT, 1)

            def gu_hi(i, l, rounds, freed):
                dve.wait_ge(d_raw[i], 16 * rounds)
                if freed is not 0:
                    dve.wait_ge(t_up2, freed)
                nc.vector.tensor_copy(flat(guhi[i][:, :, :, :]), raw[i][:, 0:4 * P]).then_inc(v_gu, 1)

            def dp_hi(i, l, freed):
                if freed is not 0:
                    dve.wait_ge(t_down, freed)
                nc.vector.tensor_copy(dphi[i][:, :], raw[i][:, 4 * P:]).then_inc(v_dp, 1)

            def activations(s, k, reuse=True):
                dve.wait_ge(a_sil, k + 1)
                dve.wait_ge(t_up2, k + 1)
                nc.vector.tensor_tensor(sil[s][:, :], PS[:, UP], sil[s][:, :], ALU.mult).then_inc(v_act1, 1)
                dve.wait_ge(v_act1, k + 1)
                dve.wait_ge(t_wbc, k + 1)
                if reuse:
                    dve.wait_ge(g_alo, k - 1)
                nc.vector.tensor_tensor(act2[s][:, :], sil[s][:, :], PS[:, WBC], ALU.mult).then_inc(v_act2, 1)

            def single(k):
                l = load_of(k)
                i, rounds = (l + 1) % 2, (l + 1) // 2 + 1
                freed = steps_through(l - 1) if l else 0
                if l + 1 < LOADS:
                    gu_hi(i, l + 1, rounds, freed)
                activations(k % 2, k, reuse=k > 1)
                if l + 1 < LOADS:
                    dp_hi(i, l + 1, freed)

            def double(par, l, k, rounds):
                gu_hi(1 - par, l + 1, rounds, k)
                activations(0, k)
                dp_hi(1 - par, l + 1, k)
                activations(1, k + 1)

            for n in range(2, UNITS):
                unit_dBu(n // UPB, n % UPB)
                unit_scan(n // UPB, n % UPB)
                if n <= PAIRED:
                    add_pair(n - 1)
                if n == 2:
                    for b in range(B):
                        add_to_x("xm", b, t_xm, v_x1)
                    dve.wait_ge(v_x1, B)
                    moments(1, range(NT))
                    take_xd(1)
                if n == 3:
                    normalise(1, 0, range(NT), XN16)
                    for i in range(2, 4):
                        dt_bias(i)
                if n == 5:
                    for i in range(2, 4):
                        softplus_rest(i)
                    for i in range(2, 4):
                        dt_finish(i)
                    dve.wait_ge(v_dt, 4)
                if n == 4:
                    for b in range(B):
                        dve.wait_ge(t_x16, b + 1)
                        nc.vector.tensor_copy(XTr[:, :, b * L:(b + 1) * L], two_tiles(bank("x16", b)[:, 0:L].bitcast(F16))).then_inc(v_x16, 1)
                hidden({5: range(0, 2), 6: range(2, 6), 7: range(6, 8), 9: range(8, 10), 10: range(10, 11),
                        11: range(11, 14), 12: range(14, 16)}.get(n, ()))
                if n == 8:
                    dve.wait_ge(d_b1, 16)
                    ffn_out(0)
                if n == 9:
                    ffn_out(1)
                    dve.wait_ge(v_x2, 2)
                    moments(2, range(0, 4))
                if n == 11:
                    normalise(2, 0, range(0, 4), XN)
                if n == 14:
                    ffn_out(2)
                if n == 15:
                    ffn_out(3)
                    gate_y(0)
                    dve.wait_ge(v_x2, 4)
                    moments(2, range(4, 8))
                    link(nc.vector.memset(sg4[:, :, :, :], 0.0))
                if n == 17:
                    normalise(2, 1, range(4, 8), XN)
                if n == 18:
                    add_to_x("yT", 0, t_yT, v_x3)
                    gate_y(1)
                if n == 20:
                    add_to_x("yT", 1, t_yT, v_x3)
                    x3_moments(0)
                if n == 22:
                    normalise(3, 0, range(0, 4), XN)
                if n == 24:
                    layernorm_parts(0)
                if n == 25:
                    choose(0)
                if n == 27:
                    gate_y(2)
                    weigh(0)
                if n == 29:
                    weights_by_expert(0)
                if n == 31:
                    add_to_x("yT", 2, t_yT, v_x3)
                if n == 19:
                    gu_hi(0, 0, 1, 0)
                    dp_hi(0, 0, 0)
            for k in range(AHEAD):
                single(k)
                if k == 0:
                    gate_y(3)
                if k == 1:
                    add_to_x("yT", 3, t_yT, v_x3)
                    x3_moments(1)
                    normalise(3, 1, range(4, 8), XN)
                if k == 2:
                    layernorm_parts(1)
                if k == 3:
                    choose(1)
                    weigh(1)
                if k == 4:
                    weights_by_expert(1)
            with dve.Fori(0, (TURNS - AHEAD) // 2) as q:
                double(0, 2 * q + AHEAD, 4 * q + AHEAD, q + (AHEAD // 2 + 1))
                double(1, 2 * q + (AHEAD + 1), 4 * q + (AHEAD + 2), q + (AHEAD // 2 + 2))
            double(0, TURNS - 1, STEPS - AHEAD - 2, TURNS // 2 + 1)

            def take_experts(hf):
                dve.wait_ge(t_down, (STEPS - AHEAD - 1, STEPS)[hf])
                nc.vector.tensor_copy(moT[hf][:, 1], PS[:, ACC[2 + hf]]).then_inc(v_mo, 1)

            def x4(b):
                dve.wait_ge(t_moT, b + 1)
                nc.vector.tensor_tensor(X[:, 2 * b:2 * b + 2], two_tiles(PS[:, OUT_BANKS[b]]), X[:, 2 * b:2 * b + 2],
                                        ALU.add).then_inc(v_x4, 1)

            take_experts(0)
            for k in range(STEPS - AHEAD, STEPS):
                single(k)
                if k == STEPS - AHEAD + 2:
                    x4(0)
                    x4(1)
            take_experts(1)
            x4(2)
            x4(3)

        @block.tensor
        def _(pe):
            mm = nc.tensor.matmul

            def into(name, i):
                if (name, i) in BEFORE:
                    was, n = BEFORE[name, i]
                    signal, per = READ[was]
                    pe.wait_ge(signal, per * (n + 1))
                return bank(name, i)

            def transposes(name, i, src, signal):
                dst = into(name, i)
                for k in range(2):
                    for m in range(2):
                        ins = nc.tensor.transpose(dst[:, k * L + m * P:k * L + (m + 1) * P], src(m, k), ident[:, :])
                ins.then_inc(signal, 1)

            def xin(i):
                hf, c = i // 2, i % 2
                dst = two_tiles(into("xin", i))
                for k in range(4):
                    ins = mm(dst, winc[:, k, c * P:(c + 1) * P], ctxT[:, 2 * hf:2 * hf + 2, k:k + L], start=k == 0, stop=k == 3)
                ins.then_inc(t_xin, 1)

            def x_dbl(m):
                pe.wait_ge(a_u, 2 * m + 2)
                dst = into("xd", m)
                for k in range(2):
                    ins = mm(dst[0:XROWS], xproj2[:, k], u[:, k, tok(m)], start=k == 0, stop=k == 1)
                ins.then_inc(t_xd, 1)

            def dt_proj(i):
                hf, c = i // 2, i % 2
                pe.wait_ge(v_dtlow, hf + 1)
                mm(into("dt", i), dtproj[:, c * P:(c + 1) * P], dtlow[:, tok(hf)], start=True, stop=True).then_inc(t_dt, 1)

            def energy(b):
                dst = into("en", b)
                for m in range(2):
                    ins = mm(dst[:, m * L:(m + 1) * L], qT[:, b * L + m * P:b * L + (m + 1) * P],
                             kT[:, b * L:(b + 1) * L], start=True, stop=True)
                ins.then_inc(t_en, 1)

            def att_transposed(b):
                pe.wait_ge(v_att, 2 * b + 2)
                transposes("attT", b, lambda m, n: att[:, b, m, n * P:(n + 1) * P], t_attT)

            def att_out(b):
                pe.wait_ge(a_attT, b + 1)
                dst = into("xm", b)
                for m in range(2):
                    for n in range(2):
                        ins = mm(dst[:, m * L:(m + 1) * L], XT[:, n, b * L + m * P:b * L + (m + 1) * P],
                                 attT[:, b, n], start=n == 0, stop=n == 1)
                ins.then_inc(t_xm, 1)

            def x16(b):
                pe.wait_ge(v_ln[1], 2 * b + 2)
                dst = into("x16", b)[:, 0:L].bitcast(F16)
                for k in range(2):
                    for m in range(2):
                        lo = k * L + m * P
                        ins = nc.tensor.transpose(dst[:, lo:lo + P], XN16[:, 2 * b + m, k * P:(k + 1) * P], ident16[:, :])
                ins.then_inc(t_x16, 1)

            def ffn_up(ks):
                for k in ks:
                    hf, f = k // FT, k % FT
                    dst = into("up", k)
                    for i, w in enumerate((w0hi, w0lo)):
                        for c in range(2):
                            ins = mm(dst, w[:, c, f * P:(f + 1) * P], XTr[:, c, tok(hf)],
                                     start=i + c == 0, stop=i + c == 2)
                    ins.then_inc(t_up, 1)

            def ffn_down(i):
                pe.wait_ge(v_hid, FT * (i // 2 + 1))
                dst = into("dn", i)
                for m in range(2):
                    at = (2 * (i % 2) + m) * P
                    for f in range(FT):
                        for s, w in enumerate((w1hi, w1lo)):
                            ins = mm(dst[:, m * L:(m + 1) * L], hid[:, f, at:at + P], w[:, f],
                                     start=f + s == 0, stop=f + s == FT)
                ins.then_inc(t_dn, 1)

            def spread(b, j, first=False):
                if not first:
                    pe.wait_ge(v_dBu, UPB * b + j)
                for n in range(NG):
                    ins = mm(PS[:, SCAN_B, n * L:(n + 1) * L], sel[:, NG * j + n], xd[:, b * L:(b + 1) * L],
                             start=True, stop=True)
                ins.then_inc(t_B, 1)
                if not first:
                    pe.wait_ge(a_C, UPB * b + j)
                for n in range(NG):
                    ins = mm(PS[:, SCAN_C, n * L:(n + 1) * L], sel[:, NS + NG * j + n], xd[:, b * L:(b + 1) * L],
                             start=True, stop=True)
                ins.then_inc(t_C, 1)

            def sum_states(b, j):
                n = UPB * b + j
                if j == 0:
                    pe.wait_ge(a_ys, b + 1)
                    for c in range(2):
                        mm(PS[:, SCAN_Y, c * L:(c + 1) * L], diagD[:, c], u[:, c, b * L:(b + 1) * L], start=c == 0,
                           stop=False, skip_group_check=True)
                if n < PAIRED:
                    pe.wait_ge(v_pair, n + 1)
                else:
                    pe.wait_ge(g_Ch, 2 * (n + 1) + CREDIT)
                states = 1 if n < PAIRED else NG
                for i in range(states):
                    ins = mm(two_tiles(PS[:, SCAN_Y]), ident[:, :], H[:, j % HRING, :, i], start=False,
                             stop=j == UPB - 1 and i == states - 1, skip_group_check=True)
                ins.then_inc(t_ys, 1)

            def y_transposed(b):
                pe.wait_ge(v_gated, b + 1)
                transposes("yT", b, lambda c, m: ys[:, 2 * b + c, m * P:(m + 1) * P], t_yT)

            def transposed_layernorm(hf):
                for b in range(2 * hf, 2 * hf + 2):
                    pe.wait_ge(v_ln[3], 2 * b + 2)
                    transposes("hT", b, lambda m, k: XN[:, 2 * b + m, k * P:(k + 1) * P], t_hT)

            def logits(hf):
                pe.wait_ge(d_gate, 16)
                dst = into("lg", hf)
                for t in range(4):
                    pe.wait_ge(a_hT, 2 * hf + t // 2 + 1)
                    at = (4 * hf + t) * P
                    for k in range(2):
                        ins = mm(dst[:, t * P:t * P + GW], XT[:, k, at:at + P], gate[:, k], start=k == 0, stop=k == 1)
                ins.then_inc(t_lg, 1)

            def to_expert_rows(hf):
                dst = into("WT", hf)
                pe.wait_ge(v_W, 2 * hf + 2)
                for t in range(4):
                    ins = nc.tensor.transpose(dst[:, t * P:(t + 1) * P], W2[:, t].rearrange("p s e -> p (s e)"), ident[:, :])
                ins.then_inc(t_WT, 1)
                dst = into("sT", hf)
                pe.wait_ge(v_sg, 2 * hf + 2)
                for t in range(4):
                    ins = nc.tensor.transpose(dst[0:4, t * P:(t + 1) * P], sg4[:, hf, t], ident[:, :])
                ins.then_inc(t_sT, 1)

            pe.sem_inc(t_ys, YCREDIT)
            pe.wait_ge(d_ctx, 32)
            for i in range(4):
                m = i % 2
                mm(two_tiles(into("qk", i)), wqk[:, i // 2], ctxT[:, 2 * m:2 * m + 2, 3:], start=True, stop=True).then_inc(t_qk, 1)
            pe.wait_ge(g_pads, 1)
            pe.wait_ge(v_winc, 1)
            xin(0)
            xin(1)
            pe.wait_ge(a_qk, 4)
            energy(0)
            energy(1)
            pe.wait_ge(g_xp, 2)
            x_dbl(0)
            dt_proj(0)
            dt_proj(1)
            energy(2)
            energy(3)
            pe.wait_ge(a_sel, 1)
            pe.wait_ge(v_xd, 1)
            spread(0, 0, first=True)
            pe.wait_ge(g_ident, 1)
            for b in range(B):
                pe.wait_ge(v_ln[0], 2 * b + 2)
                transposes("xt", b, lambda m, k: XN[:, 2 * b + m, k * P:(k + 1) * P], t_xt)
            xin(2)
            xin(3)
            spread(0, 1)
            for b in range(B):
                att_transposed(b)
            pe.wait_ge(a_xt, B)
            pe.wait_ge(g_diag, 2)
            for n in range(1, UNITS):
                if n + 1 < UNITS:
                    spread((n + 1) // UPB, (n + 1) % UPB)
                if n > 1:
                    sum_states((n - 2) // UPB, (n - 2) % UPB)
                if n == 1:
                    for b in range(B):
                        att_out(b)
                if n == 2:
                    x_dbl(1)
                    dt_proj(2)
                    dt_proj(3)
                if n == 3:
                    pe.wait_ge(g_id16, 1)
                    for b in range(B):
                        x16(b)
                if n == 4:
                    pe.wait_ge(v_x16, B)
                    pe.wait_ge(g_w0, 1)
                    ffn_up(range(0, 4))
                if n == 5:
                    ffn_up(range(4, 8))
                if n == 6:
                    ffn_up(range(8, 10))
                if n == 7:
                    pe.wait_ge(g_w1, 1)
                    ffn_down(0)
                if n == 8:
                    ffn_down(1)
                if n == 9:
                    ffn_up(range(10, 13))
                if n == 10:
                    ffn_up(range(13, 16))
                if n == 13:
                    ffn_down(2)
                if n == 14:
                    ffn_down(3)
                if n == 16:
                    y_transposed(0)
                if n == 19:
                    y_transposed(1)
                if n == 23:
                    transposed_layernorm(0)
                if n == 24:
                    logits(0)
                if n == 28:
                    to_expert_rows(0)
                if n == 30:
                    y_transposed(2)

            def three(out_ap, whi, wlo, xhi, xlo, first, last):
                n = len(xhi)
                for i in range(n):
                    mm(out_ap, whi[i], xhi[i], start=first and i == 0, stop=False)
                    mm(out_ap, whi[i], xlo[i], start=False, stop=False)
                    ins = mm(out_ap, wlo[i], xhi[i], start=False, stop=last and i == n - 1)
                return ins

            def gate_up(i, m, k, l, rounds, first=False):
                pe.wait_ge(g_gu, l + 1)
                xhi = [XThi[:, m, c] for c in range(2)]
                xlo = [XTlo[:, m, c] for c in range(2)]
                for g, (to, read, signal) in enumerate(((GATE, a_sil, t_gate), (UP, v_act1, t_up2))):
                    if not first:
                        pe.wait_ge(read, k)
                    three(PS[:, to], [guhi[i][:, c, g] for c in range(2)], [gulo[i][:, c, g] for c in range(2)],
                          xhi, xlo, True, True).then_inc(signal, 1)
                pe.wait_ge(d_wr[i], 16 * rounds)
                if not first:
                    pe.wait_ge(v_act2, k)
                mm(PS[:, WBC], sel4r[:, :], wr4[i][:, tok(m)], start=True, stop=True).then_inc(t_wbc, 1)

            def down(i, m, s, k, l, last=False):
                pe.wait_ge(g_alo, k + 1)
                pe.wait_ge(g_dp, l + 1)
                for o in range(2):
                    ins = three(PS[:, ACC[2 * o + m]], [dphi[i][:, o * P:(o + 1) * P]], [dplo[i][:, o * P:(o + 1) * P]],
                                [ahi[s][:, :]], [alo[s][:, :]], False, last)
                ins.then_inc(t_down, 1)

            def gate_up_of(k):
                l = load_of(k)
                gate_up(l % 2, half_of(k), k, l, l // 2 + 1, first=k == 0)

            def down_of(k):
                l = load_of(k)
                down(l % 2, half_of(k), k % 2, k, l, last=k in (STEPS - AHEAD - 2, STEPS - 1))

            def clear(m):
                for o in range(2):
                    mm(PS[:, ACC[2 * o + m]], zero[:, :], XThi[:, 0, 0], start=True, stop=False)

            def to_tokens(b):
                hf = b // 2
                pe.wait_ge(a_mo, hf + 1)
                pe.wait_ge(v_mo, hf + 1)
                for m in range(2):
                    for o in range(2):
                        at = (2 * (b % 2) + m) * P
                        ins = nc.tensor.transpose(PS[:, OUT_BANKS[b], m * L + o * P:m * L + (o + 1) * P],
                                                  moT[hf][:, o, at:at + P], ident[:, :])
                ins.then_inc(t_moT, 1)

            sum_states(B - 1, UPB - 2)
            pe.wait_ge(v_hT, 2)
            pe.wait_ge(v_dBu, UNITS)
            pe.wait_ge(a_C, UNITS)
            pe.wait_ge(g_sel4, 1)
            pe.wait_ge(v_WT, 1)
            pe.wait_ge(v_sgT, 1)
            pe.wait_ge(g_zero, 2)
            gate_up_of(0)
            sum_states(B - 1, UPB - 1)
            clear(0)
            for k in range(AHEAD):
                if k == AHEAD - 2:
                    to_expert_rows(1)
                gate_up_of(k + 1)
                down_of(k)
                if k == 0:
                    y_transposed(3)
                if k == 1:
                    pe.wait_ge(a_ys, B + 1)
                    transposed_layernorm(1)
                if k == 2:
                    logits(1)
            pe.wait_ge(v_hT, 4)
            pe.wait_ge(v_lg, 2)
            pe.wait_ge(v_WT, 2)
            clear(1)

            def double(par, l, k, rounds, next_rounds):
                gate_up(par, 1, k + 1, l, rounds)
                down(par, 0, 0, k, l)
                gate_up(1 - par, 0, k + 2, l + 1, next_rounds)
                down(par, 1, 1, k + 1, l)

            with pe.Fori(0, (TURNS - AHEAD) // 2) as q:
                double(0, 2 * q + AHEAD, 4 * q + AHEAD, q + (AHEAD // 2 + 1), q + (AHEAD // 2 + 1))
                double(1, 2 * q + (AHEAD + 1), 4 * q + (AHEAD + 2), q + (AHEAD // 2 + 1), q + (AHEAD // 2 + 2))
            for k in range(STEPS - AHEAD - 2, STEPS):
                if k + 1 < STEPS:
                    gate_up_of(k + 1)
                down_of(k)
                if k == STEPS - AHEAD:
                    pe.wait_ge(v_sgT, 2)
                    to_tokens(0)
                    to_tokens(1)
            pe.wait_ge(a_sil, STEPS)
            to_tokens(2)
            to_tokens(3)


def kernel(x, ctx_1024, L0_xattn_Wq, L0_xattn_bq, L0_xattn_Wk, L0_xattn_bk, L0_ffn_W0, L0_ffn_bias0, L0_ffn_W1,
           L0_ffn_bias1, L1_xattn_in_proj_w, L1_xattn_conv_w, L1_xattn_conv_b, L1_xattn_x_proj_w, L1_xattn_dt_proj_w,
           L1_xattn_dt_proj_b, L1_xattn_A_log, L1_xattn_D, L1_ffn_gate_w, L1_ffn_gu_w, L1_ffn_dp_w,
           L1_ffn_sh_gate_w, L1_ffn_sh_up_w, L1_ffn_sh_down_w, L1_ffn_sh_gate1_w):
    import numpy as np
    import concourse.bacc as bacc
    from concourse.bass_utils import run_bass_kernel_spmd

    def ktiles(w):
        return w.T.reshape(-1, P, w.shape[0]).transpose(1, 0, 2)

    def per_partition(v):
        return v.reshape(-1, P, *v.shape[1:]).swapaxes(0, 1).reshape(P, -1)

    a = {}
    a["x"] = x.reshape(NT, P, D).transpose(1, 0, 2)
    a["ctxT"] = ctx_1024.transpose(2, 0, 1)
    a["wqk"] = np.stack([L0_xattn_Wq.T, L0_xattn_Wk.T], 1)
    a["cols"] = np.concatenate([per_partition(v) for v in (
        L0_xattn_bq, L0_xattn_bk, L0_ffn_bias0, L1_xattn_conv_b, L1_xattn_dt_proj_b,
        L1_xattn_A_log, L1_xattn_D)], 1)
    a["inproj"] = L1_xattn_in_proj_w.T
    a["conv"] = L1_xattn_conv_w.reshape(D, 4).T
    a["xproj"] = ktiles(L1_xattn_x_proj_w)
    a["dtproj"] = L1_xattn_dt_proj_w.T
    a["w0"] = ktiles(L0_ffn_W0).reshape(P, -1)
    a["w1"] = ktiles(L0_ffn_W1).reshape(P, -1)
    a["b1"] = L0_ffn_bias1
    a["gate"] = ktiles(np.concatenate([L1_ffn_gate_w, L1_ffn_sh_gate1_w], 0))
    gu = L1_ffn_gu_w.reshape(NP, 2, 2, NI, 2, P).transpose(0, 5, 4, 2, 1, 3).reshape(NP, P, 4 * P)
    dp = L1_ffn_dp_w.transpose(0, 2, 1).reshape(NP, P, D)
    sh = np.zeros((1, P, 4 * P + D), np.float32)
    sh[0, :, :4 * P].reshape(P, 2, 2, 2, NI)[:, :, :, 0] = np.stack(
        [ktiles(L1_ffn_sh_gate_w), ktiles(L1_ffn_sh_up_w)], 2)
    sh[0, :NI, 4 * P:] = L1_ffn_sh_down_w.T
    a["experts"] = np.concatenate([sh, np.concatenate([gu, dp], 2)], 0)

    nc = bacc.Bacc("TRN2", target_bir_lowering=False, num_devices=1)
    arrays, args = {}, []
    for name, v in a.items():
        v = np.ascontiguousarray(v)
        arrays["in_" + name] = v
        args.append(nc.dram_tensor("in_" + name, v.shape, mybir.dt.from_np(v.dtype), kind="ExternalInput").ap())
    wrow = nc.dram_tensor("wrow", (NE + 2, 2, T), F32, kind="Internal").ap()
    out = nc.dram_tensor("out_0", (T, D), F32, kind="ExternalOutput").ap()
    build(nc, *args, wrow, out.rearrange("(t p) d -> p t d", p=P))
    r = run_bass_kernel_spmd(nc, [arrays], core_ids=[0])
    return r.results[0]["out_0"].reshape(B, L, D)
```

```python
from contextlib import ExitStack

import concourse.bass as bass
from concourse import mybir

ALU = mybir.AluOpType
ACT = mybir.ActivationFunctionType
F32 = mybir.dt.float32
F32R = mybir.dt.float32r
F16 = mybir.dt.float16
AX_X = mybir.AxisListType.X

P = 128
B, L, D = 4, 256, 256
C = 128
T = B * L
NT = T // P
HALF = 512
F = 1024
FT = F // P
NS = 16
NG = 2
UPB = NS // NG
UNITS = B * UPB
PAIRED = 12
HRING = 4
ARING = 4
R = 8
LO = 64
XROWS = LO + R + 2 * NS
NE, NI = 64, 64
NP = NE // 2
TURNS = NP + 1
AHEAD = 6
STEPS = 2 * TURNS
LOADS = TURNS + AHEAD
GW = NE + 1
EPS = 1e-5
LOWEST = -3.0e38

BQ, BK, B0, CB, DB, AL, DD = 0, 1, 2, 10, 12, 14, 46
NCOL = 48

SCAN_B, SCAN_C, SCAN_Y = 4, 5, 7
L0_BANKS = (0, 1, 2, 3, 6)
ACC, GATE, UP = (0, 1, 2, 3), 4, 5

L0_USES = ([("qk", i) for i in range(4)] + [("xin", 0), ("xin", 1), ("en", 0), ("en", 1)]
           + [("xd", 0), ("dt", 0), ("dt", 1), ("en", 2), ("en", 3)]
           + [("xt", b) for b in range(B)] + [("xin", 2), ("xin", 3)] + [("attT", b) for b in range(B)]
           + [("xm", b) for b in range(B)] + [("xd", 1), ("dt", 2), ("dt", 3)] + [("x16", b) for b in range(B)]
           + [("up", k) for k in range(FT + 1)] + [("dn", 0), ("up", FT + 1), ("up", FT + 2), ("dn", 1)]
           + [("up", k) for k in range(FT + 3, 2 * FT)] + [("dn", 2), ("dn", 3)]
           + [("yT", 0), ("yT", 1), ("hT", 0), ("hT", 1), ("lg", 0), ("WT", 0)])
BANK = {use: L0_BANKS[i % len(L0_BANKS)] for i, use in enumerate(L0_USES)}
BEFORE = {use: L0_USES[i - len(L0_BANKS)] for i, use in enumerate(L0_USES) if i >= len(L0_BANKS)}
BANK.update({("yT", 2): 1, ("yT", 3): 3, ("hT", 2): 6, ("hT", 3): SCAN_Y, ("lg", 1): 1, ("WT", 1): 3})
BEFORE.update({("yT", 2): ("hT", 0), ("yT", 3): ("lg", 0), ("hT", 2): ("WT", 0), ("lg", 1): ("yT", 2),
               ("WT", 1): ("yT", 3)})
OUT_BANKS = (7, 0, 2, 6)


def half_of(k):
    return 0 if k < AHEAD else 1 if k >= STEPS - AHEAD else k % 2


def load_of(k):
    return k if k < AHEAD else k - (STEPS - AHEAD) + TURNS if k >= STEPS - AHEAD else (k + AHEAD) // 2


def steps_through(load):
    return load + 1 if load < AHEAD else 2 * load + 2 - AHEAD if load < TURNS else load + 1 + STEPS - AHEAD - TURNS


def build(nc, x_in, ctx_in, wqk_in, cols_in, inproj_in, conv_in, xproj_in, dtproj_in, w0_in, w1_in, b1_in,
          gate_in, experts_in, wrow, out):
    with ExitStack() as stack:
        def sb(name, shape, dt, at=stack):
            return at.enter_context(nc.sbuf_tensor(name, shape, dt))

        def sem(name):
            return stack.enter_context(nc.semaphore(name))

        PS = stack.enter_context(nc.psum_tensor("PS", [P, 8, HALF], F32))

        X = sb("X", [P, NT, D], F32)
        XN = sb("XN", [P, NT, D], F32)
        cols = sb("cols", [P, NCOL + 1], F32)
        ident = sb("ident", [P, P], F32)
        ident16 = sb("ident16", [P, P], F16)
        stats = sb("stats", [P, 4, NT, 6], F32)
        mv = sb("mv", [P, 4, NT, 2], F32)
        std = sb("std", [P, 4, NT], F32)
        rstd = sb("rstd", [P, 4, NT], F32)
        silz = sb("silz", [P, NT, D], F32)
        ys = sb("ys", [P, NT, L], F32)
        XT = sb("XT", [P, 2, T], F32)
        gate = sb("gate", [P, 2, GW], F32)

        sel = sb("sel", [XROWS, 2 * NS, P], F32R)
        xd = sb("xd", [XROWS, T], F32R)
        negA = sb("negA", [P, 2, NS], F32)
        diagD = sb("diagD", [P, 2, P], F32)
        u = sb("u", [P, 2, T], F32)
        dt = sb("dt", [P, 2, T], F32)
        dtu = sb("dtu", [P, 2, T], F32)
        dA = sb("dA", [P, ARING, 2, NG, L], F32)
        H = sb("H", [P, HRING, 2, NG, L], F32)
        Csb = sb("Csb", [P, 2, NG, L], F32)
        zero = sb("zero", [P, P], F32R)

        l0 = ExitStack()
        w0hi = sb("w0hi", [P, 2, F], F32R, l0)
        w0lo = sb("w0lo", [P, 2, F], F32R, l0)
        w1hi = sb("w1hi", [P, FT, D], F32R, l0)
        w1lo = sb("w1lo", [P, FT, D], F32R, l0)
        b1 = sb("b1", [P, D], F32, l0)
        sel1 = sb("sel1", [XROWS, 2 * NS], F32, l0)
        negmx = sb("negmx", [P, B, 2], F32, l0)
        esum = sb("esum", [P, B, 2], F32, l0)
        rsum = sb("rsum", [P, B, 2], F32, l0)
        one = ExitStack()
        att = sb("att", [P, B, 2, L], F32, one)
        one.close()
        XTr = sb("XTr", [P, 2, T], F32R, l0)
        two = ExitStack()
        attT = sb("attT", [P, B, 2, L], F32, two)
        two.close()
        XN16 = sb("XN16", [P, NT, D], F16, l0)
        e16 = sb("e16", [P, NT, D], F16, l0)
        three_ = ExitStack()
        ctxT = sb("ctxT", [P, B, L + 3], F32, three_)
        winc = sb("winc", [P, 4, D], F32, three_)
        wqk = sb("wqk", [P, 2, P], F32, three_)
        inproj = sb("inproj", [P, D], F32, three_)
        xproj = sb("xproj", [P, 2, R + 2 * NS], F32, three_)
        xproj2 = sb("xproj2", [P, 2, XROWS], F32, three_)
        dtproj = sb("dtproj", [R, D], F32, three_)
        qT = sb("qT", [P, T], F32, three_)
        kT = sb("kT", [P, T], F32, three_)
        dtlow = sb("dtlow", [R, T], F32, three_)
        corr = sb("corr", [P, 2, HALF], F32, three_)
        three_.close()
        hid16 = sb("hid16", [P, 4, HALF], F16, l0)
        hid = sb("hid", [P, FT, HALF], F32R, l0)
        l0.close()
        w0raw = silz[:, :, :].rearrange("p t d -> p (t d)")
        w1raw = attT[:, :, :, :].rearrange("p b m l -> p (b m l)")

        moe = ExitStack()
        XThi = sb("XThi", [P, 2, 2, HALF], F32R, moe)
        XTlo = sb("XTlo", [P, 2, 2, HALF], F32R, moe)
        logit = sb("logit", [P, 2, 4, GW], F32, moe)
        top = sb("top", [P, 2, 4, 8], F32, moe)
        nmax = sb("nmax", [P, 2, 4], F32, moe)
        rest = sb("rest", [P, 4, NE], F32, moe)
        chosen = sb("chosen", [P, 4, NE], F32, moe)
        pexp = sb("pexp", [P, 2, 4, NE], F32, moe)
        wsum = sb("wsum", [P, 2, 4], F32, moe)
        wrec = sb("wrec", [P, 2, 4], F32, moe)
        W = sb("W", [P, 4, 2 + NE], F32, moe)
        sg = sb("sg", [P, 2, 4], F32, moe)
        WT = sb("WT", [2 + NE, 2, HALF], F32, moe)
        raw = [sb(f"raw{i}", [P, 4 * P + D], F32, moe) for i in range(2)]
        wb = [sb(f"wb{i}", [P, T], F32, moe) for i in range(2)]
        guhi = [sb(f"guhi{i}", [P, 2, 2, P], F32R, moe) for i in range(2)]
        gulo = [sb(f"gulo{i}", [P, 2, 2, P], F32R, moe) for i in range(2)]
        dphi = [sb(f"dphi{i}", [P, D], F32R, moe) for i in range(2)]
        dplo = [sb(f"dplo{i}", [P, D], F32R, moe) for i in range(2)]
        sil = [sb(f"sil{i}", [P, HALF], F32, moe) for i in range(2)]
        act2 = [sb(f"act2_{i}", [P, HALF], F32, moe) for i in range(2)]
        ahi = [sb(f"ahi{i}", [P, HALF], F32R, moe) for i in range(2)]
        alo = [sb(f"alo{i}", [P, HALF], F32R, moe) for i in range(2)]
        moe.close()
        moT = [XN[:, 4 * hf:4 * hf + 4].rearrange("p (h a) d -> p h (a d)", h=2) for hf in range(2)]

        names = """d_ctx d_x d_vec d_prep d_w0 d_w1 d_b1 d_gate d_raw0 d_raw1 d_wr0 d_wr1 d_in d_wrow d_out
            g_ident g_pads g_xp g_id16 g_sel1 g_diag g_self g_w0 g_w1 v_hid g_zero g_gated g_Ch g_gu g_dp g_alo
            v_self v_var0 v_var1 v_var2 v_var3 v_ln0 v_ln1 v_ln2 v_ln3 v_eps v_winc v_w0 v_w1 v_mo v_pair v_mx v_att v_xd
            v_x1 v_dt v_ffn v_x2 v_negA v_dBu v_scan v_gated v_x3 v_hT v_lg v_top v_W v_WT
            v_gu v_dp v_act1 v_act2 v_x4
            a_self a_std0 a_std1 a_std2 a_std3 a_qk a_dtlow a_r a_x16 a_xt a_sel a_u a_ex a_A a_attT a_e a_ln a_gelu a_silz a_C a_dA a_ys
            a_hT a_pexp a_sg a_sil a_ahi a_mo
            t_qk t_xin t_xt t_en t_xd t_attT t_dt t_xm t_x16 t_up t_dn t_B t_C t_ys t_yT t_hT t_lg t_WT
            t_gate t_up2 t_down t_moT""".split()
        S = {n: sem(n) for n in names}
        (d_ctx, d_x, d_vec, d_prep, d_w0, d_w1, d_b1, d_gate, d_raw0, d_raw1, d_wr0, d_wr1, d_in, d_wrow, d_out,
         g_ident, g_pads, g_xp, g_id16, g_sel1, g_diag, g_self, g_w0, g_w1, v_hid, g_zero, g_gated, g_Ch, g_gu, g_dp, g_alo,
         v_self, v_var0, v_var1, v_var2, v_var3, v_ln0, v_ln1, v_ln2, v_ln3, v_eps, v_winc, v_w0, v_w1, v_mo, v_pair, v_mx, v_att, v_xd,
         v_x1, v_dt, v_ffn, v_x2, v_negA, v_dBu, v_scan, v_gated, v_x3, v_hT, v_lg, v_top, v_W, v_WT,
         v_gu, v_dp, v_act1, v_act2, v_x4,
         a_self, a_std0, a_std1, a_std2, a_std3, a_qk, a_dtlow, a_r, a_x16,  a_xt, a_sel, a_u, a_ex, a_A, a_attT, a_e, a_ln, a_gelu, a_silz, a_C, a_dA, a_ys,
         a_hT, a_pexp, a_sg, a_sil, a_ahi, a_mo,
         t_qk, t_xin, t_xt, t_en, t_xd, t_attT, t_dt, t_xm, t_x16, t_up, t_dn, t_B, t_C, t_ys, t_yT, t_hT, t_lg, t_WT,
         t_gate, t_up2, t_down, t_moT) = (S[n] for n in names)
        d_raw, d_wr = (d_raw0, d_raw1), (d_wr0, d_wr1)
        v_var, v_ln, a_std = (v_var0, v_var1, v_var2, v_var3), (v_ln0, v_ln1, v_ln2, v_ln3), (a_std0, a_std1, a_std2, a_std3)

        READ = {"xin": (a_u, 1), "qk": (a_qk, 1), "xd": (v_xd, 1), "dt": (a_r, 1), "xt": (a_xt, 1), "en": (a_ex, 2),
                "attT": (a_attT, 1), "xm": (v_x1, 1), "x16": (a_x16, 1), "up": (a_gelu, 1), "dn": (v_ffn, 1),
                "yT": (v_x3, 1), "hT": (a_hT, 1), "lg": (v_lg, 1), "WT": (v_WT, 1)}
        CREDIT, YCREDIT = 4, HRING

        def plain(ap):
            return ap.bitcast(F32)

        def flat(ap):
            return ap.rearrange("p k g m -> p (k g m)")

        def tok(m):
            return slice(m * HALF, (m + 1) * HALF)

        def bank(name, i):
            return PS[:, BANK[name, i]]

        def lnbuf(i):
            return ys[:, :, :].rearrange("p (c t) l -> p c (t l)", c=2)[:, i % 2, tok(i // 2)]

        def two_tiles(ap):
            return ap.rearrange("p (m l) -> p m l", m=2)

        block = stack.enter_context(nc.Block())

        @block.sync
        def _(sp):
            sp.dma_start(ctxT[:, :, 3:], ctx_in).then_inc(d_ctx, 16)
            sp.dma_start(wqk[:, :, :], wqk_in).then_inc(d_ctx, 16)
            sp.dma_start(inproj[:, :], inproj_in).then_inc(d_in, 16)
            sp.dma_start(xproj[:, :, :], xproj_in).then_inc(d_prep, 16)
            sp.dma_start(dtproj[:, :], dtproj_in).then_inc(d_prep, 16)
            sp.dma_start(w0raw, w0_in).then_inc(d_w0, 16)
            sp.dma_start(w1raw, w1_in).then_inc(d_w1, 16)
            sp.dma_start(b1[:, :], b1_in.partition_broadcast(P)).then_inc(d_b1, 16)
            sp.dma_start(gate[:, :, :], gate_in).then_inc(d_gate, 16)

            def load_experts(i, at):
                sp.dma_start(raw[i][:, :], experts_in[bass.ds(at, 1)].rearrange("o p n -> (o p) n")).then_inc(d_raw[i], 16)

            def load_rows(i, at, rows):
                for e in range(2):
                    src = wrow[bass.ds(2 * at + e, 1), rows].broadcast_to([NI, rows.stop - rows.start])
                    sp.dma_start(wb[i][e * NI:(e + 1) * NI, rows], src).then_inc(d_wr[i], 16)

            def load(l, weights_of, rows):
                i = l % 2
                sp.wait_ge(g_gu, l - 1)
                sp.wait_ge(g_dp, l - 1)
                load_experts(i, weights_of)
                sp.wait_ge(v_act2, steps_through(l - 2))
                load_rows(i, weights_of, rows)

            def write_rows(hf):
                sp.wait_ge(v_WT, hf + 1)
                sp.dma_start(wrow[:, tok(hf)], WT[:, hf]).then_inc(d_wrow, 16)
                sp.wait_ge(d_wrow, 16 * (hf + 1))

            sp.wait_ge(v_ffn, 4)
            for i in range(2):
                load_experts(i, i)
            write_rows(0)
            for i in range(2):
                load_rows(i, i, tok(0))
            for l in range(2, AHEAD):
                load(l, l, tok(0))
            both = slice(0, T)
            sp.wait_ge(g_gu, AHEAD - 1)
            sp.wait_ge(g_dp, AHEAD - 1)
            load_experts(0, AHEAD)
            write_rows(1)
            sp.wait_ge(v_act2, AHEAD - 1)
            load_rows(0, AHEAD, both)
            with sp.Fori(0, (NP - AHEAD) // 2) as q:
                for r in range(1, 3):
                    i, l = (AHEAD + r) % 2, 2 * q + (AHEAD + r)
                    sp.wait_ge(g_gu, l - 1)
                    sp.wait_ge(g_dp, l - 1)
                    load_experts(i, l)
                    sp.wait_ge(v_act2, 4 * q + (AHEAD + 2 * r - 2))
                    load_rows(i, l, both)
            for l in range(TURNS, LOADS):
                load(l, l - TURNS, tok(1))
            for b in range(B):
                sp.wait_ge(v_x4, b + 1)
                sp.dma_start(out[:, 2 * b:2 * b + 2, :], X[:, 2 * b:2 * b + 2, :]).then_inc(d_out, 16)
            sp.wait_ge(d_out, 16 * B)

        @block.gpsimd
        def _(pool):
            g = [0]

            def link(ins):
                g[0] += 1
                ins.then_inc(g_self, 1)
                pool.wait_ge(g_self, g[0])

            nc.gpsimd.memset(ctxT[:, :, 0:3], 0.0).then_inc(g_pads, 1)
            link(nc.gpsimd.memset(xproj2[:, :, :], 0.0))
            link(nc.gpsimd.memset(ident[:, :], 0.0))
            nc.gpsimd.affine_select(out=ident[:, :], in_=ident[:, :], compare_op=ALU.not_equal, fill=1.0,
                                    base=0, pattern=[[-1, P]], channel_multiplier=1).then_inc(g_ident, 1)
            link(nc.gpsimd.memset(sel1[:, :], 0.0))
            link(nc.gpsimd.affine_select(out=sel1[:, :], in_=sel1[:, :], compare_op=ALU.not_equal, fill=1.0,
                                         base=-R, pattern=[[-1, 2 * NS]], channel_multiplier=1))
            nc.gpsimd.affine_select(out=sel1[:, :], in_=sel1[:, :], compare_op=ALU.not_equal, fill=1.0,
                                    base=-R - LO, pattern=[[-1, 2 * NS]], channel_multiplier=1).then_inc(g_sel1, 1)
            pool.wait_ge(d_prep, 32)
            for at in (0, LO):
                nc.gpsimd.tensor_copy(xproj2[:, :, at:at + R + 2 * NS], xproj[:, :, :]).then_inc(g_xp, 1)
            nc.gpsimd.memset(dA[:, :, :, :, 0:1], 0.0).then_inc(g_zero, 1)
            nc.gpsimd.memset(plain(zero[:, :]), 0.0).then_inc(g_zero, 1)
            pool.wait_ge(g_ident, 1)
            pool.wait_ge(d_vec, 16)
            for c in range(2):
                nc.gpsimd.tensor_scalar(diagD[:, c], ident[:, :], cols[:, DD + c:DD + c + 1], None, ALU.mult).then_inc(g_diag, 1)
            nc.gpsimd.tensor_copy(ident16[:, :], ident[:, :]).then_inc(g_id16, 1)

            for ready, rawt, hi, lo, done in ((v_w0, w0raw, w0hi, w0lo, g_w0), (v_w1, w1raw, w1hi, w1lo, g_w1)):
                pool.wait_ge(ready, 1)
                nc.gpsimd.tensor_tensor(lo[:, :, :].rearrange("p k f -> p (k f)"), rawt,
                                        plain(hi[:, :, :]).rearrange("p k f -> p (k f)"), ALU.subtract).then_inc(done, 1)

            pool.sem_inc(g_Ch, CREDIT)

            def times_C(b, j):
                for c in range(2):
                    pool.wait_ge(a_C, UPB * b + (j + 1))
                    pool.wait_ge(v_scan, 2 * UPB * b + (2 * j + c + 1 + CREDIT))
                    nc.gpsimd.tensor_tensor(H[:, j % HRING, c], H[:, j % HRING, c], Csb[:, j % 2],
                                            ALU.mult).then_inc(g_Ch, 1)

            def gate_y(b):
                pool.wait_ge(a_ys, b + 2)
                pool.wait_ge(a_silz, b // 2 + 1)
                nc.gpsimd.tensor_tensor(ys[:, 2 * b:2 * b + 2], ys[:, 2 * b:2 * b + 2], silz[:, 2 * b:2 * b + 2],
                                        ALU.mult).then_inc(g_gated, 1)

            def gu_lo(i, l):
                pool.wait_ge(v_gu, l + 1)
                nc.gpsimd.tensor_tensor(flat(gulo[i][:, :, :, :]), raw[i][:, 0:4 * P], plain(flat(guhi[i][:, :, :, :])),
                                        ALU.subtract).then_inc(g_gu, 1)

            def dp_lo(i, l):
                pool.wait_ge(v_dp, l + 1)
                nc.gpsimd.tensor_tensor(dplo[i][:, :], raw[i][:, 4 * P:], plain(dphi[i][:, :]), ALU.subtract).then_inc(g_dp, 1)

            def act_lo(s, k, reuse=True):
                pool.wait_ge(a_ahi, k + 1)
                if reuse:
                    pool.wait_ge(t_down, k - 1)
                nc.gpsimd.tensor_tensor(alo[s][:, :], act2[s][:, :], plain(ahi[s][:, :]), ALU.subtract).then_inc(g_alo, 1)

            def single(k):
                l = load_of(k)
                if l + 1 < LOADS:
                    gu_lo((l + 1) % 2, l + 1)
                act_lo(k % 2, k, reuse=k > 1)
                if l + 1 < LOADS:
                    dp_lo((l + 1) % 2, l + 1)

            def double(par, l, k):
                gu_lo(1 - par, l + 1)
                act_lo(0, k)
                dp_lo(1 - par, l + 1)
                act_lo(1, k + 1)

            for n in range(UNITS):
                times_C(n // UPB, n % UPB)
                if n == 18:
                    gate_y(0)
                    gate_y(1)
                if n == 26:
                    gate_y(2)
                if n == 28:
                    gu_lo(0, 0)
                    dp_lo(0, 0)
            for k in range(AHEAD):
                single(k)
            with pool.Fori(0, (TURNS - AHEAD) // 2) as q:
                double(0, 2 * q + AHEAD, 4 * q + AHEAD)
                double(1, 2 * q + (AHEAD + 1), 4 * q + (AHEAD + 2))
            double(0, TURNS - 1, STEPS - AHEAD - 2)
            for k in range(STEPS - AHEAD, STEPS):
                single(k)

        @block.scalar
        def _(act):
            a = [0]

            def link(ins):
                a[0] += 1
                ins.then_inc(a_self, 1)
                act.wait_ge(a_self, a[0])

            act.dma_start(winc[:, :, :], conv_in.partition_broadcast(P)).then_inc(d_in, 16)
            act.dma_start(cols[:, 0:NCOL], cols_in).then_inc(d_vec, 16)
            act.dma_start(X[:, :, :], x_in).then_inc(d_x, 16)

            def root(i, hf, tiles):
                act.wait_ge(v_var[i], hf + 1)
                nc.scalar.activation(std[:, i, tiles], mv[:, i, tiles, 1], ACT.Sqrt,
                                     bias=cols[:, NCOL:NCOL + 1]).then_inc(a_std[i], 1)

            def silu_u(i):
                hf, c = i // 2, i % 2
                act.wait_ge(t_xin, i + 1)
                nc.scalar.activation(u[:, c, tok(hf)], bank("xin", i), ACT.Silu,
                                     bias=cols[:, CB + c:CB + c + 1]).then_inc(a_u, 1)

            def take_dtlow(m):
                act.wait_ge(t_xd, m + 1)
                nc.scalar.activation(dtlow[:, tok(m)], bank("xd", m)[0:R], ACT.Copy).then_inc(a_dtlow, 1)

            def softplus(hf):
                for c in range(2):
                    i = 2 * hf + c
                    act.wait_ge(t_dt, i + 1)
                    bias = cols[:, DB + c:DB + c + 1]
                    link(nc.scalar.activation(dtu[:, c, tok(hf)], bank("dt", i), ACT.Abs, bias=bias))
                    nc.scalar.activation(dt[:, c, tok(hf)], bank("dt", i), ACT.Relu, bias=bias).then_inc(a_r, 1)
                    nc.scalar.activation(dtu[:, c, tok(hf)], dtu[:, c, tok(hf)], ACT.Exp, scale=-1.0).then_inc(a_e, 1)
                if hf == 0:
                    exp_energy(2)
                    exp_energy(3)
                for c in range(2):
                    i = 2 * hf + c
                    act.wait_ge(a_e, i + 1)
                    nc.scalar.activation(lnbuf(i), dtu[:, c, tok(hf)], ACT.Ln, bias=1.0).then_inc(a_ln, 1)

            def copy_C(n):
                act.wait_ge(t_C, n + 1)
                act.wait_ge(g_Ch, 2 * n + 2)
                nc.scalar.activation(Csb[:, n % 2].rearrange("p n l -> p (n l)"), PS[:, SCAN_C], ACT.Copy).then_inc(a_C, 1)

            def decay(n):
                b, j = n // UPB, n % UPB
                if n >= ARING:
                    act.wait_ge(v_scan, 2 * (n - ARING + 1) + CREDIT)
                for c in range(2):
                    for s in range(NG):
                        ins = nc.scalar.activation(dA[:, n % ARING, c, s, 1:], dt[:, c, b * L + 1:(b + 1) * L], ACT.Exp,
                                                   scale=negA[:, c, j * NG + s:j * NG + s + 1])
                    ins.then_inc(a_dA, 1)

            def unit(n):
                if n % 2 == 0:
                    decay(n)
                copy_C(n)
                if n % 2 == 0:
                    decay(n + 1)

            def take_y(b):
                nc.scalar.activation(ys[:, bass.ds(2 * b, 2), :], two_tiles(PS[:, SCAN_Y]), ACT.Copy).then_inc(a_ys, 1)

            def exp_energy(b):
                act.wait_ge(v_mx, b + 1)
                for m in range(2):
                    nc.scalar.activation(att[:, b, m], bank("en", b)[:, m * L:(m + 1) * L], ACT.Exp,
                                         bias=negmx[:, b, m:m + 1], accum_out=esum[:, b, m:m + 1]).then_inc(a_ex, 1)

            act.wait_ge(g_sel1, 1)
            nc.scalar.activation(sel[:, :, :], sel1[:, :].unsqueeze(2).broadcast_to([XROWS, 2 * NS, P]), ACT.Copy).then_inc(a_sel, 1)
            act.wait_ge(d_vec, 16)
            nc.scalar.activation(negA[:, :, :], cols[:, AL:AL + 2 * NS].rearrange("p (c n) -> p c n", c=2),
                                 ACT.Exp).then_inc(a_A, 1)
            for i in range(4):
                act.wait_ge(t_qk, i + 1)
                nc.scalar.activation((qT, kT)[i // 2][:, tok(i % 2)], bank("qk", i), ACT.Identity,
                                     bias=cols[:, BQ + i // 2:BQ + i // 2 + 1]).then_inc(a_qk, 1)
            act.wait_ge(v_eps, 1)
            root(0, 0, slice(0, NT))
            silu_u(0)
            silu_u(1)
            exp_energy(0)
            exp_energy(1)
            take_dtlow(0)
            softplus(0)
            for b in range(B):
                act.wait_ge(t_xt, b + 1)
                nc.scalar.activation(XT[:, :, b * L:(b + 1) * L], two_tiles(bank("xt", b)), ACT.Copy).then_inc(a_xt, 1)
            silu_u(2)
            silu_u(3)
            act.sem_inc(a_ys, 1)
            act.wait_ge(g_zero, 1)
            act.wait_ge(v_negA, 1)
            act.wait_ge(v_dt, 2)
            unit(0)
            unit(1)
            act.wait_ge(g_w1, 1)
            for b in range(B):
                act.wait_ge(t_attT, b + 1)
                nc.scalar.activation(attT[:, b].rearrange("p m l -> p (m l)"), bank("attT", b), ACT.Copy).then_inc(a_attT, 1)

            def gelu(ks):
                for k in ks:
                    act.wait_ge(t_up, k + 1)
                    if k >= 4:
                        act.wait_ge(v_hid, k - 3)
                    nc.scalar.activation(hid16[:, k % 4], bank("up", k), ACT.Gelu,
                                         bias=cols[:, B0 + k % FT:B0 + k % FT + 1]).then_inc(a_gelu, 1)

            def silu_z(hf):
                act.wait_ge(v_ln[2], 4 * hf + 4)
                nc.scalar.activation(silz[:, 4 * hf:4 * hf + 4], XN[:, 4 * hf:4 * hf + 4], ACT.Silu).then_inc(a_silz, 1)

            def transposed(b):
                act.wait_ge(t_hT, b + 1)
                part = slice((b % 2) * L, (b % 2 + 1) * L)
                nc.scalar.activation(XThi[:, b // 2, :, part], two_tiles(bank("hT", b)), ACT.Copy)
                nc.scalar.activation(XT[:, :, b * L:(b + 1) * L], two_tiles(bank("hT", b)), ACT.Copy).then_inc(a_hT, 1)

            def exp_logits(hf):
                act.wait_ge(v_top, hf + 1)
                for t in range(4):
                    nc.scalar.activation(pexp[:, hf, t], logit[:, hf, t, 0:NE], ACT.Exp, bias=nmax[:, hf, t:t + 1]).then_inc(a_pexp, 1)
                nc.scalar.activation(sg[:, hf], logit[:, hf, :, NE], ACT.Exp, scale=-1.0).then_inc(a_sg, 1)

            for n in range(2, UNITS):
                unit(n)
                if n == 2:
                    take_dtlow(1)
                if n == 3:
                    root(1, 0, slice(0, NT))
                if n == 4:
                    softplus(1)
                    for b in range(B):
                        act.wait_ge(t_x16, b + 1)
                        nc.scalar.activation(XTr[:, :, b * L:(b + 1) * L], two_tiles(bank("x16", b)[:, 0:L].bitcast(F16)),
                                             ACT.Copy).then_inc(a_x16, 1)
                gelu({5: range(0, 2), 6: range(2, 4), 7: range(4, 6), 8: range(6, 8), 11: range(8, 10),
                      13: range(10, 12), 14: range(12, 14), 15: range(14, 16)}.get(n, ()))
                if n in (9, 18, 26):
                    act.wait_ge(t_ys, n // UPB * UPB + YCREDIT)
                    take_y(n // UPB - 1)
                if n == 15:
                    root(2, 0, slice(0, 4))
                if n == 17:
                    act.wait_ge(g_w0, 1)
                    silu_z(0)
                if n == 23:
                    root(2, 1, slice(4, 8))
                    root(3, 0, slice(0, 4))
                if n == 25:
                    silu_z(1)
                if n == 26:
                    transposed(0)
                    transposed(1)
                if n == 29:
                    exp_logits(0)

            def act_silu(s, k, reuse=True):
                act.wait_ge(t_gate, k + 1)
                if reuse:
                    act.wait_ge(v_act2, k - 1)
                nc.scalar.activation(sil[s][:, :], PS[:, GATE], ACT.Silu).then_inc(a_sil, 1)

            def act_hi(s, k, reuse=True):
                act.wait_ge(v_act2, k + 1)
                if reuse:
                    act.wait_ge(t_down, k - 1)
                nc.scalar.activation(ahi[s][:, :], act2[s][:, :], ACT.Copy).then_inc(a_ahi, 1)

            def act_step(s, k):
                act_silu(s, k)
                act_hi(s, k)

            def take_experts(hf):
                act.wait_ge(t_down, (STEPS - AHEAD - 1, STEPS)[hf])
                nc.scalar.activation(moT[hf][:, 0], PS[:, ACC[hf]], ACT.Copy).then_inc(a_mo, 1)

            for k in range(AHEAD):
                act_silu(k % 2, k, reuse=k > 1)
                if k == 0:
                    act.wait_ge(t_ys, UNITS + YCREDIT)
                    take_y(3)
                act_hi(k % 2, k, reuse=k > 1)
                if k == 1:
                    root(3, 1, slice(4, 8))
                if k == 2:
                    transposed(2)
                    transposed(3)
                if k == 3:
                    exp_logits(1)
            with act.Fori(AHEAD, TURNS) as l:
                for m in range(2):
                    act_step(m, 2 * l + (m - AHEAD))
            take_experts(0)
            for k in range(STEPS - AHEAD, STEPS):
                act_step(k % 2, k)
            take_experts(1)

        @block.vector
        def _(dve):
            v = [0]

            def link(ins):
                v[0] += 1
                ins.then_inc(v_self, 1)
                dve.wait_ge(v_self, v[0])

            def moments(i, tiles):
                for t in tiles:
                    ins = nc.vector.bn_stats(stats[:, i, t], X[:, t])
                link(ins)
                for t in tiles:
                    ins = nc.vector.bn_aggr(mv[:, i, t], stats[:, i, t])
                ins.then_inc(v_var[i], 1)

            def normalise(i, hf, tiles, dst):
                dve.wait_ge(a_std[i], hf + 1)
                t0, t1 = tiles[0], tiles[-1] + 1
                link(nc.vector.reciprocal(rstd[:, i, t0:t1], std[:, i, t0:t1]))
                for t in tiles:
                    nc.vector.tensor_scalar(dst[:, t], X[:, t], mv[:, i, t, 0:1], rstd[:, i, t:t + 1],
                                            ALU.subtract, ALU.mult).then_inc(v_ln[i], 1)

            def take_xd(m):
                dve.wait_ge(t_xd, m + 1)
                dve.wait_ge(a_dtlow, m + 1)
                link(nc.vector.tensor_copy(xd[:, tok(m)], bank("xd", m)[0:XROWS]))
                nc.vector.tensor_tensor(xd[LO:XROWS, tok(m)], bank("xd", m)[LO:XROWS], plain(xd[LO:XROWS, tok(m)]),
                                        ALU.subtract).then_inc(v_xd, 1)

            def softplus_rest(i):
                dve.wait_ge(a_e, i + 1)
                e = dtu[:, i % 2, tok(i // 2)]
                link(nc.vector.tensor_scalar(corr[:, i % 2], e, 1.0, -1.0, ALU.add, ALU.add))
                link(nc.vector.tensor_tensor(corr[:, i % 2], e, corr[:, i % 2], ALU.subtract))

            def dt_finish(i):
                hf, c = i // 2, i % 2
                dve.wait_ge(a_ln, i + 1)
                r, e, ln = dt[:, c, tok(hf)], dtu[:, c, tok(hf)], lnbuf(i)
                link(nc.vector.tensor_tensor(r, r, ln, ALU.add))
                link(nc.vector.tensor_tensor(r, r, corr[:, i % 2], ALU.add))
                nc.vector.tensor_tensor(e, r, u[:, c, tok(hf)], ALU.mult).then_inc(v_dt, 1)

            def unit_dBu(b, j):
                dve.wait_ge(t_B, UPB * b + (j + 1))
                dve.wait_ge(t_ys, UPB * b + (j + 1))
                nc.vector.tensor_tensor(H[:, j % HRING], two_tiles(PS[:, SCAN_B]).unsqueeze(1).broadcast_to([P, 2, NG, L]),
                                        dtu[:, :, b * L:(b + 1) * L].unsqueeze(2).broadcast_to([P, 2, NG, L]),
                                        ALU.mult).then_inc(v_dBu, 1)

            def unit_scan(b, j):
                dve.wait_ge(v_dBu, UPB * b + (j + 1))
                for c in range(2):
                    dve.wait_ge(a_dA, 2 * UPB * b + (2 * j + c + 1))
                    states = H[:, j % HRING, c].rearrange("p n l -> p (n l)")
                    nc.vector.tensor_tensor_scan(states, dA[:, j % ARING, c].rearrange("p n l -> p (n l)"), states,
                                                 0.0, ALU.mult, ALU.add).then_inc(v_scan, 1)

            def add_pair(n):
                dve.wait_ge(g_Ch, 2 * (n + 1) + CREDIT)
                H0, H1 = (H[:, n % HRING, :, s] for s in range(2))
                nc.vector.tensor_tensor(H0, H0, H1, ALU.add).then_inc(v_pair, 1)

            def add_to_x(name, b, arrived, done):
                dve.wait_ge(arrived, b + 1)
                nc.vector.tensor_tensor(X[:, 2 * b:2 * b + 2], two_tiles(bank(name, b)), X[:, 2 * b:2 * b + 2],
                                        ALU.add).then_inc(done, 1)

            def ffn_out(i):
                dve.wait_ge(t_dn, i + 1)
                nc.vector.tensor_tensor(e16[:, 2 * i:2 * i + 2], two_tiles(bank("dn", i)),
                                        b1[:, :].unsqueeze(1).broadcast_to([P, 2, D]), ALU.add).then_inc(v_ffn, 1)
                dve.wait_ge(v_ffn, i + 1)
                nc.vector.tensor_tensor(X[:, 2 * i:2 * i + 2], e16[:, 2 * i:2 * i + 2], X[:, 2 * i:2 * i + 2],
                                        ALU.add).then_inc(v_x2, 1)

            def hidden(ks):
                for k in ks:
                    dve.wait_ge(a_gelu, k + 1)
                    if k >= FT:
                        dve.wait_ge(t_dn, 2)
                    nc.vector.tensor_copy(hid[:, k % FT], hid16[:, k % 4]).then_inc(v_hid, 1)

            def gate_y(b):
                dve.wait_ge(a_ys, b + 2)
                dve.wait_ge(a_silz, b // 2 + 1)
                nc.vector.tensor_tensor(ys[:, 2 * b:2 * b + 2], ys[:, 2 * b:2 * b + 2], silz[:, 2 * b:2 * b + 2],
                                        ALU.mult).then_inc(v_gated, 1)

            def row_maxima(b):
                dve.wait_ge(t_en, b + 1)
                link(nc.vector.reduce_max(negmx[:, b], two_tiles(bank("en", b)), AX_X))
                nc.vector.tensor_scalar(negmx[:, b], negmx[:, b], -1.0, None, ALU.mult).then_inc(v_mx, 1)

            nc.vector.memset(cols[:, NCOL:NCOL + 1], EPS).then_inc(v_eps, 1)
            dve.wait_ge(d_in, 32)
            nc.vector.tensor_tensor(winc[:, :, :], winc[:, :, :], inproj[:, :].unsqueeze(1).broadcast_to([P, 4, D]),
                                    ALU.mult).then_inc(v_winc, 1)
            dve.wait_ge(a_A, 1)
            nc.vector.tensor_scalar(negA[:, :, :], negA[:, :, :], -1.0, None, ALU.mult).then_inc(v_negA, 1)
            dve.wait_ge(d_x, 16)
            moments(0, range(NT))
            normalise(0, 0, range(NT), XN)

            def weights_hi(landed, rawt, hi, done):
                dve.wait_ge(landed, 16)
                nc.vector.tensor_copy(hi[:, :, :].rearrange("p k f -> p (k f)"), rawt).then_inc(done, 1)

            weights_hi(d_w0, w0raw, w0hi, v_w0)
            row_maxima(0)
            row_maxima(1)
            weights_hi(d_w1, w1raw, w1hi, v_w1)
            take_xd(0)
            row_maxima(2)
            row_maxima(3)
            for i in range(2):
                softplus_rest(i)
            for i in range(2):
                dt_finish(i)
            dve.sem_inc(v_scan, CREDIT)
            dve.wait_ge(v_dt, 2)
            unit_dBu(0, 0)
            for b in range(B):
                dve.wait_ge(a_ex, 2 * b + 2)
                link(nc.vector.reciprocal(rsum[:, b], esum[:, b]))
                for m in range(2):
                    nc.vector.tensor_scalar(att[:, b, m], att[:, b, m], rsum[:, b, m:m + 1], None, ALU.mult).then_inc(v_att, 1)
            unit_scan(0, 0)
            unit_dBu(0, 1)
            unit_scan(0, 1)
            add_pair(0)

            def x3_moments(hf):
                dve.wait_ge(v_x3, 2 * hf + 2)
                moments(3, range(4 * hf, 4 * hf + 4))

            def layernorm_parts(hf):
                for b in range(2 * hf, 2 * hf + 2):
                    dve.wait_ge(a_hT, b + 1)
                    part = slice((b % 2) * L, (b % 2 + 1) * L)
                    src = XT[:, :, b * L:(b + 1) * L]
                    nc.vector.tensor_tensor(XTlo[:, hf, :, part], src, plain(XThi[:, hf, :, part]), ALU.subtract).then_inc(v_hT, 1)

            def choose(hf):
                dve.wait_ge(t_lg, hf + 1)
                nc.vector.tensor_copy(logit[:, hf], bank("lg", hf).rearrange("p (t n) -> p t n", t=4)[:, :, 0:GW]).then_inc(v_lg, 1)
                dve.wait_ge(v_lg, hf + 1)
                for t in range(4):
                    ins = nc.vector.max(top[:, hf, t], logit[:, hf, t, 0:NE])
                link(ins)
                nc.vector.tensor_scalar(nmax[:, hf], top[:, hf, :, 0], -1.0, None, ALU.mult).then_inc(v_top, 1)
                for t in range(4):
                    ins = nc.vector.match_replace(rest[:, t], top[:, hf, t], logit[:, hf, t, 0:NE], LOWEST)
                link(ins)
                link(nc.vector.tensor_tensor(chosen[:, :, :], rest[:, :, :], logit[:, hf, :, 0:NE], ALU.not_equal))

            def weigh(hf):
                dve.wait_ge(a_pexp, 4 * hf + 4)
                link(nc.vector.tensor_tensor(chosen[:, :, :], pexp[:, hf], chosen[:, :, :], ALU.mult))
                link(nc.vector.reduce_sum(wsum[:, hf], chosen[:, :, :], AX_X))
                link(nc.vector.reciprocal(wrec[:, hf], wsum[:, hf]))
                if hf:
                    dve.wait_ge(t_WT, 1)
                nc.vector.tensor_tensor(W[:, :, 2:], chosen[:, :, :], wrec[:, hf].unsqueeze(2).broadcast_to([P, 4, NE]),
                                        ALU.mult).then_inc(v_W, 1)
                dve.wait_ge(a_sg, hf + 1)
                link(nc.vector.tensor_scalar(sg[:, hf], sg[:, hf], 1.0, None, ALU.add))
                link(nc.vector.reciprocal(sg[:, hf], sg[:, hf]))
                nc.vector.tensor_copy(W[:, :, 0:2], sg[:, hf].unsqueeze(2).broadcast_to([P, 4, 2])).then_inc(v_W, 1)

            def weights_by_expert(hf):
                dve.wait_ge(t_WT, hf + 1)
                nc.vector.tensor_copy(WT[:, hf], bank("WT", hf)[0:2 + NE]).then_inc(v_WT, 1)

            def gu_hi(i, l, rounds, freed):
                dve.wait_ge(d_raw[i], 16 * rounds)
                if freed is not 0:
                    dve.wait_ge(t_up2, freed)
                nc.vector.tensor_copy(flat(guhi[i][:, :, :, :]), raw[i][:, 0:4 * P]).then_inc(v_gu, 1)

            def dp_hi(i, l, freed):
                if freed is not 0:
                    dve.wait_ge(t_down, freed)
                nc.vector.tensor_copy(dphi[i][:, :], raw[i][:, 4 * P:]).then_inc(v_dp, 1)

            def activations(s, k, half, i, rounds, reuse=True):
                dve.wait_ge(a_sil, k + 1)
                dve.wait_ge(t_up2, k + 1)
                nc.vector.tensor_tensor(sil[s][:, :], PS[:, UP], sil[s][:, :], ALU.mult).then_inc(v_act1, 1)
                dve.wait_ge(v_act1, k + 1)
                dve.wait_ge(d_wr[i], 32 * rounds)
                if reuse:
                    dve.wait_ge(g_alo, k - 1)
                nc.vector.tensor_tensor(act2[s][:, :], sil[s][:, :], wb[i][:, half], ALU.mult).then_inc(v_act2, 1)

            def single(k):
                l = load_of(k)
                i, rounds = (l + 1) % 2, (l + 1) // 2 + 1
                freed = steps_through(l - 1) if l else 0
                if l + 1 < LOADS:
                    gu_hi(i, l + 1, rounds, freed)
                activations(k % 2, k, tok(half_of(k)), l % 2, l // 2 + 1, reuse=k > 1)
                if l + 1 < LOADS:
                    dp_hi(i, l + 1, freed)

            def double(par, l, k, rounds, next_rounds):
                gu_hi(1 - par, l + 1, next_rounds, k)
                activations(0, k, tok(0), par, rounds)
                dp_hi(1 - par, l + 1, k)
                activations(1, k + 1, tok(1), par, rounds)

            for n in range(2, UNITS):
                unit_dBu(n // UPB, n % UPB)
                unit_scan(n // UPB, n % UPB)
                if n <= PAIRED:
                    add_pair(n - 1)
                if n == 2:
                    for b in range(B):
                        add_to_x("xm", b, t_xm, v_x1)
                    dve.wait_ge(v_x1, B)
                    moments(1, range(NT))
                    take_xd(1)
                if n == 3:
                    normalise(1, 0, range(NT), XN16)
                if n in (5, 6):
                    softplus_rest(n - 3)
                    dt_finish(n - 3)
                if n == 15:
                    dve.wait_ge(v_dt, 4)
                hidden({6: range(0, 2), 7: range(2, 4), 8: range(4, 6), 9: range(6, 8), 13: range(8, 11),
                        14: range(11, 12), 15: range(12, 14), 16: range(14, 16)}.get(n, ()))
                if n == 11:
                    dve.wait_ge(d_b1, 16)
                    ffn_out(0)
                if n == 13:
                    ffn_out(1)
                    dve.wait_ge(v_x2, 2)
                    moments(2, range(0, 4))
                if n == 16:
                    normalise(2, 0, range(0, 4), XN)
                if n == 20:
                    ffn_out(2)
                if n == 21:
                    ffn_out(3)
                    dve.wait_ge(v_x2, 4)
                    moments(2, range(4, 8))
                if n == 22:
                    add_to_x("yT", 0, t_yT, v_x3)
                    add_to_x("yT", 1, t_yT, v_x3)
                    x3_moments(0)
                if n == 24:
                    normalise(3, 0, range(0, 4), XN)
                    normalise(2, 1, range(4, 8), XN)
                if n == 25:
                    gu_hi(0, 0, 1, 0)
                    dp_hi(0, 0, 0)
                if n == 27:
                    layernorm_parts(0)
                    choose(0)
                if n == 29:
                    weigh(0)
                if n == 31:
                    weights_by_expert(0)
                if n == 31:
                    add_to_x("yT", 2, t_yT, v_x3)
            for k in range(AHEAD):
                single(k)
                if k == 0:
                    gate_y(3)
                if k == 1:
                    add_to_x("yT", 3, t_yT, v_x3)
                    x3_moments(1)
                    normalise(3, 1, range(4, 8), XN)
                if k == 2:
                    layernorm_parts(1)
                if k == 3:
                    choose(1)
                    weigh(1)
                if k == 4:
                    weights_by_expert(1)
            with dve.Fori(0, (TURNS - AHEAD) // 2) as q:
                double(0, 2 * q + AHEAD, 4 * q + AHEAD, q + (AHEAD // 2 + 1), q + (AHEAD // 2 + 1))
                double(1, 2 * q + (AHEAD + 1), 4 * q + (AHEAD + 2), q + (AHEAD // 2 + 1), q + (AHEAD // 2 + 2))
            double(0, TURNS - 1, STEPS - AHEAD - 2, TURNS // 2 + 1, TURNS // 2 + 1)

            def take_experts(hf):
                dve.wait_ge(t_down, (STEPS - AHEAD - 1, STEPS)[hf])
                nc.vector.tensor_copy(moT[hf][:, 1], PS[:, ACC[2 + hf]]).then_inc(v_mo, 1)

            def x4(b):
                dve.wait_ge(t_moT, b + 1)
                nc.vector.tensor_tensor(X[:, 2 * b:2 * b + 2], two_tiles(PS[:, OUT_BANKS[b]]), X[:, 2 * b:2 * b + 2],
                                        ALU.add).then_inc(v_x4, 1)

            take_experts(0)
            for k in range(STEPS - AHEAD, STEPS):
                single(k)
                if k == STEPS - AHEAD + 2:
                    x4(0)
                    x4(1)
            take_experts(1)
            x4(2)
            x4(3)

        @block.tensor
        def _(pe):
            mm = nc.tensor.matmul

            def into(name, i):
                if (name, i) in BEFORE:
                    was, n = BEFORE[name, i]
                    signal, per = READ[was]
                    pe.wait_ge(signal, per * (n + 1))
                return bank(name, i)

            def transposes(name, i, src, signal):
                dst = into(name, i)
                for k in range(2):
                    for m in range(2):
                        ins = nc.tensor.transpose(dst[:, k * L + m * P:k * L + (m + 1) * P], src(m, k), ident[:, :])
                ins.then_inc(signal, 1)

            def xin(i):
                hf, c = i // 2, i % 2
                dst = two_tiles(into("xin", i))
                for k in range(4):
                    ins = mm(dst, winc[:, k, c * P:(c + 1) * P], ctxT[:, 2 * hf:2 * hf + 2, k:k + L], start=k == 0, stop=k == 3)
                ins.then_inc(t_xin, 1)

            def x_dbl(m):
                pe.wait_ge(a_u, 2 * m + 2)
                dst = into("xd", m)
                for k in range(2):
                    ins = mm(dst[0:XROWS], xproj2[:, k], u[:, k, tok(m)], start=k == 0, stop=k == 1)
                ins.then_inc(t_xd, 1)

            def dt_proj(i):
                hf, c = i // 2, i % 2
                pe.wait_ge(a_dtlow, hf + 1)
                mm(into("dt", i), dtproj[:, c * P:(c + 1) * P], dtlow[:, tok(hf)], start=True, stop=True).then_inc(t_dt, 1)

            def energy(b):
                dst = into("en", b)
                for m in range(2):
                    ins = mm(dst[:, m * L:(m + 1) * L], qT[:, b * L + m * P:b * L + (m + 1) * P],
                             kT[:, b * L:(b + 1) * L], start=True, stop=True)
                ins.then_inc(t_en, 1)

            def att_transposed(b):
                pe.wait_ge(v_att, 2 * b + 2)
                transposes("attT", b, lambda m, n: att[:, b, m, n * P:(n + 1) * P], t_attT)

            def att_out(b):
                pe.wait_ge(a_attT, b + 1)
                dst = into("xm", b)
                for m in range(2):
                    for n in range(2):
                        ins = mm(dst[:, m * L:(m + 1) * L], XT[:, n, b * L + m * P:b * L + (m + 1) * P],
                                 attT[:, b, n], start=n == 0, stop=n == 1)
                ins.then_inc(t_xm, 1)

            def x16(b):
                pe.wait_ge(v_ln[1], 2 * b + 2)
                dst = into("x16", b)[:, 0:L].bitcast(F16)
                for k in range(2):
                    for m in range(2):
                        lo = k * L + m * P
                        ins = nc.tensor.transpose(dst[:, lo:lo + P], XN16[:, 2 * b + m, k * P:(k + 1) * P], ident16[:, :])
                ins.then_inc(t_x16, 1)

            def ffn_up(ks):
                for k in ks:
                    hf, f = k // FT, k % FT
                    dst = into("up", k)
                    for i, w in enumerate((w0hi, w0lo)):
                        for c in range(2):
                            ins = mm(dst, w[:, c, f * P:(f + 1) * P], XTr[:, c, tok(hf)],
                                     start=i + c == 0, stop=i + c == 2)
                    ins.then_inc(t_up, 1)

            def ffn_down(i, m):
                pe.wait_ge(v_hid, FT * (i // 2 + 1))
                dst = into("dn", i) if m == 0 else bank("dn", i)
                at = (2 * (i % 2) + m) * P
                for f in range(FT):
                    for s, w in enumerate((w1hi, w1lo)):
                        ins = mm(dst[:, m * L:(m + 1) * L], hid[:, f, at:at + P], w[:, f],
                                 start=f + s == 0, stop=f + s == FT)
                if m:
                    ins.then_inc(t_dn, 1)

            def spread(b, j, first=False):
                if not first:
                    pe.wait_ge(v_dBu, UPB * b + j)
                for n in range(NG):
                    ins = mm(PS[:, SCAN_B, n * L:(n + 1) * L], sel[:, NG * j + n], xd[:, b * L:(b + 1) * L],
                             start=True, stop=True)
                ins.then_inc(t_B, 1)
                if not first:
                    pe.wait_ge(a_C, UPB * b + j)
                for n in range(NG):
                    ins = mm(PS[:, SCAN_C, n * L:(n + 1) * L], sel[:, NS + NG * j + n], xd[:, b * L:(b + 1) * L],
                             start=True, stop=True)
                ins.then_inc(t_C, 1)

            def sum_states(b, j):
                n = UPB * b + j
                if j == 0:
                    pe.wait_ge(a_ys, b + 1)
                    for c in range(2):
                        mm(PS[:, SCAN_Y, c * L:(c + 1) * L], diagD[:, c], u[:, c, b * L:(b + 1) * L], start=c == 0,
                           stop=False, skip_group_check=True)
                if n < PAIRED:
                    pe.wait_ge(v_pair, n + 1)
                else:
                    pe.wait_ge(g_Ch, 2 * (n + 1) + CREDIT)
                states = 1 if n < PAIRED else NG
                for i in range(states):
                    ins = mm(two_tiles(PS[:, SCAN_Y]), ident[:, :], H[:, j % HRING, :, i], start=False,
                             stop=j == UPB - 1 and i == states - 1, skip_group_check=True)
                ins.then_inc(t_ys, 1)

            def y_transposed(b):
                if b < B - 1:
                    pe.wait_ge(g_gated, b + 1)
                else:
                    pe.wait_ge(v_gated, 1)
                transposes("yT", b, lambda c, m: ys[:, 2 * b + c, m * P:(m + 1) * P], t_yT)

            def transposed_layernorm(hf):
                for b in range(2 * hf, 2 * hf + 2):
                    pe.wait_ge(v_ln[3], 2 * b + 2)
                    transposes("hT", b, lambda m, k: XN[:, 2 * b + m, k * P:(k + 1) * P], t_hT)

            def logits(hf):
                pe.wait_ge(d_gate, 16)
                dst = into("lg", hf)
                for t in range(4):
                    pe.wait_ge(a_hT, 2 * hf + t // 2 + 1)
                    at = (4 * hf + t) * P
                    for k in range(2):
                        ins = mm(dst[:, t * P:t * P + GW], XT[:, k, at:at + P], gate[:, k], start=k == 0, stop=k == 1)
                ins.then_inc(t_lg, 1)

            def to_expert_rows(hf):
                dst = into("WT", hf)
                pe.wait_ge(v_W, 2 * hf + 2)
                for t in range(4):
                    ins = nc.tensor.transpose(dst[0:2 + NE, t * P:(t + 1) * P], W[:, t], ident[:, :])
                ins.then_inc(t_WT, 1)

            pe.sem_inc(t_ys, YCREDIT)
            pe.wait_ge(d_ctx, 32)
            for i in range(4):
                m = i % 2
                mm(two_tiles(into("qk", i)), wqk[:, i // 2], ctxT[:, 2 * m:2 * m + 2, 3:], start=True, stop=True).then_inc(t_qk, 1)
            pe.wait_ge(g_pads, 1)
            pe.wait_ge(v_winc, 1)
            xin(0)
            xin(1)
            pe.wait_ge(a_qk, 4)
            energy(0)
            energy(1)
            pe.wait_ge(g_xp, 2)
            x_dbl(0)
            dt_proj(0)
            dt_proj(1)
            energy(2)
            energy(3)
            pe.wait_ge(a_sel, 1)
            pe.wait_ge(v_xd, 1)
            spread(0, 0, first=True)
            pe.wait_ge(g_ident, 1)
            for b in range(B):
                pe.wait_ge(v_ln[0], 2 * b + 2)
                transposes("xt", b, lambda m, k: XN[:, 2 * b + m, k * P:(k + 1) * P], t_xt)
            xin(2)
            xin(3)
            spread(0, 1)
            for b in range(B):
                att_transposed(b)
            pe.wait_ge(a_xt, B)
            pe.wait_ge(g_diag, 2)
            for n in range(1, UNITS):
                if n + 1 < UNITS:
                    spread((n + 1) // UPB, (n + 1) % UPB)
                if n > 1:
                    sum_states((n - 2) // UPB, (n - 2) % UPB)
                if n == 1:
                    for b in range(B):
                        att_out(b)
                if n == 2:
                    x_dbl(1)
                    dt_proj(2)
                    dt_proj(3)
                if n == 3:
                    pe.wait_ge(g_id16, 1)
                    for b in range(B):
                        x16(b)
                if n == 4:
                    pe.wait_ge(a_x16, B)
                    pe.wait_ge(g_w0, 1)
                if n == 9:
                    pe.wait_ge(g_w1, 1)
                ffn_up({4: range(0, 2), 5: range(2, 4), 6: range(4, 6), 7: range(6, 8), 9: [8], 10: [9], 11: [10],
                        12: [11], 13: range(12, 14), 14: range(14, 16)}.get(n, ()))
                if n in (9, 10, 11, 12):
                    ffn_down((n - 9) // 2, (n - 9) % 2)
                if n in (17, 18, 19, 20):
                    ffn_down((n - 13) // 2, (n - 13) % 2)
                if n == 20:
                    y_transposed(0)
                    y_transposed(1)
                if n == 25:
                    transposed_layernorm(0)
                if n == 26:
                    logits(0)
                if n == 30:
                    to_expert_rows(0)
                if n == 31:
                    y_transposed(2)

            def three(out_ap, whi, wlo, xhi, xlo, first, last):
                n = len(xhi)
                for i in range(n):
                    mm(out_ap, whi[i], xhi[i], start=first and i == 0, stop=False)
                    mm(out_ap, whi[i], xlo[i], start=False, stop=False)
                    ins = mm(out_ap, wlo[i], xhi[i], start=False, stop=last and i == n - 1)
                return ins

            def gate_up(i, m, k, l, first=False):
                pe.wait_ge(g_gu, l + 1)
                xhi = [XThi[:, m, c] for c in range(2)]
                xlo = [XTlo[:, m, c] for c in range(2)]
                for g, (to, read, signal) in enumerate(((GATE, a_sil, t_gate), (UP, v_act1, t_up2))):
                    if not first:
                        pe.wait_ge(read, k)
                    three(PS[:, to], [guhi[i][:, c, g] for c in range(2)], [gulo[i][:, c, g] for c in range(2)],
                          xhi, xlo, True, True).then_inc(signal, 1)

            def down(i, m, s, k, l, last=False):
                pe.wait_ge(g_alo, k + 1)
                pe.wait_ge(g_dp, l + 1)
                for o in range(2):
                    ins = three(PS[:, ACC[2 * o + m]], [dphi[i][:, o * P:(o + 1) * P]], [dplo[i][:, o * P:(o + 1) * P]],
                                [ahi[s][:, :]], [alo[s][:, :]], False, last)
                ins.then_inc(t_down, 1)

            def gate_up_of(k):
                l = load_of(k)
                gate_up(l % 2, half_of(k), k, l, first=k == 0)

            def down_of(k):
                l = load_of(k)
                down(l % 2, half_of(k), k % 2, k, l, last=k in (STEPS - AHEAD - 2, STEPS - 1))

            def clear(m):
                for o in range(2):
                    mm(PS[:, ACC[2 * o + m]], zero[:, :], XThi[:, 0, 0], start=True, stop=False)

            def to_tokens(b):
                hf = b // 2
                pe.wait_ge(a_mo, hf + 1)
                pe.wait_ge(v_mo, hf + 1)
                for m in range(2):
                    for o in range(2):
                        at = (2 * (b % 2) + m) * P
                        ins = nc.tensor.transpose(PS[:, OUT_BANKS[b], m * L + o * P:m * L + (o + 1) * P],
                                                  moT[hf][:, o, at:at + P], ident[:, :])
                ins.then_inc(t_moT, 1)

            sum_states(B - 1, UPB - 2)
            pe.wait_ge(v_hT, 2)
            pe.wait_ge(v_dBu, UNITS)
            pe.wait_ge(a_C, UNITS)
            pe.wait_ge(v_x3, 2)
            pe.wait_ge(a_hT, 2)
            pe.wait_ge(g_zero, 2)
            gate_up_of(0)
            sum_states(B - 1, UPB - 1)
            clear(0)
            for k in range(AHEAD):
                if k == AHEAD - 2:
                    to_expert_rows(1)
                gate_up_of(k + 1)
                down_of(k)
                if k == 0:
                    y_transposed(3)
                if k == 1:
                    pe.wait_ge(a_ys, B + 1)
                    transposed_layernorm(1)
                if k == 2:
                    logits(1)
            pe.wait_ge(v_hT, 4)
            pe.wait_ge(v_lg, 2)
            pe.wait_ge(v_WT, 2)
            clear(1)

            def double(par, l, k):
                gate_up(par, 1, k + 1, l)
                down(par, 0, 0, k, l)
                gate_up(1 - par, 0, k + 2, l + 1)
                down(par, 1, 1, k + 1, l)

            with pe.Fori(0, (TURNS - AHEAD) // 2) as q:
                double(0, 2 * q + AHEAD, 4 * q + AHEAD)
                double(1, 2 * q + (AHEAD + 1), 4 * q + (AHEAD + 2))
            for k in range(STEPS - AHEAD - 2, STEPS):
                if k + 1 < STEPS:
                    gate_up_of(k + 1)
                down_of(k)
                if k == STEPS - AHEAD:
                    to_tokens(0)
                    to_tokens(1)
            to_tokens(2)
            to_tokens(3)


def kernel(x, ctx_1024, L0_xattn_Wq, L0_xattn_bq, L0_xattn_Wk, L0_xattn_bk, L0_ffn_W0, L0_ffn_bias0, L0_ffn_W1,
           L0_ffn_bias1, L1_xattn_in_proj_w, L1_xattn_conv_w, L1_xattn_conv_b, L1_xattn_x_proj_w, L1_xattn_dt_proj_w,
           L1_xattn_dt_proj_b, L1_xattn_A_log, L1_xattn_D, L1_ffn_gate_w, L1_ffn_gu_w, L1_ffn_dp_w,
           L1_ffn_sh_gate_w, L1_ffn_sh_up_w, L1_ffn_sh_down_w, L1_ffn_sh_gate1_w):
    import numpy as np
    import concourse.bacc as bacc
    from concourse.bass_utils import run_bass_kernel_spmd

    def ktiles(w):
        return w.T.reshape(-1, P, w.shape[0]).transpose(1, 0, 2)

    def per_partition(v):
        return v.reshape(-1, P, *v.shape[1:]).swapaxes(0, 1).reshape(P, -1)

    a = {}
    a["x"] = x.reshape(NT, P, D).transpose(1, 0, 2)
    a["ctxT"] = ctx_1024.transpose(2, 0, 1)
    a["wqk"] = np.stack([L0_xattn_Wq.T, L0_xattn_Wk.T], 1)
    a["cols"] = np.concatenate([per_partition(v) for v in (
        L0_xattn_bq, L0_xattn_bk, L0_ffn_bias0, L1_xattn_conv_b, L1_xattn_dt_proj_b,
        L1_xattn_A_log, L1_xattn_D)], 1)
    a["inproj"] = L1_xattn_in_proj_w.T
    a["conv"] = L1_xattn_conv_w.reshape(D, 4).T
    a["xproj"] = ktiles(L1_xattn_x_proj_w)
    a["dtproj"] = L1_xattn_dt_proj_w.T
    a["w0"] = ktiles(L0_ffn_W0).reshape(P, -1)
    a["w1"] = ktiles(L0_ffn_W1).reshape(P, -1)
    a["b1"] = L0_ffn_bias1
    a["gate"] = ktiles(np.concatenate([L1_ffn_gate_w, L1_ffn_sh_gate1_w], 0))
    gu = L1_ffn_gu_w.reshape(NP, 2, 2, NI, 2, P).transpose(0, 5, 4, 2, 1, 3).reshape(NP, P, 4 * P)
    dp = L1_ffn_dp_w.transpose(0, 2, 1).reshape(NP, P, D)
    sh = np.zeros((1, P, 4 * P + D), np.float32)
    sh[0, :, :4 * P].reshape(P, 2, 2, 2, NI)[:, :, :, 0] = np.stack(
        [ktiles(L1_ffn_sh_gate_w), ktiles(L1_ffn_sh_up_w)], 2)
    sh[0, :NI, 4 * P:] = L1_ffn_sh_down_w.T
    a["experts"] = np.concatenate([sh, np.concatenate([gu, dp], 2)], 0)

    nc = bacc.Bacc("TRN2", target_bir_lowering=False, num_devices=1)
    arrays, args = {}, []
    for name, v in a.items():
        v = np.ascontiguousarray(v)
        arrays["in_" + name] = v
        args.append(nc.dram_tensor("in_" + name, v.shape, mybir.dt.from_np(v.dtype), kind="ExternalInput").ap())
    wrow = nc.dram_tensor("wrow", (NE + 2, T), F32, kind="Internal").ap()
    out = nc.dram_tensor("out_0", (T, D), F32, kind="ExternalOutput").ap()
    build(nc, *args, wrow, out.rearrange("(t p) d -> p t d", p=P))
    r = run_bass_kernel_spmd(nc, [arrays], core_ids=[0])
    return r.results[0]["out_0"].reshape(B, L, D)
```
